# Optimizing a Trainium2 kernel written in Bass

```python
import numpy as np
import jax
import jax.numpy as jnp

def _softmax(x, axis=-1):
    return jax.nn.softmax(x, axis=axis)

def _gelu(x):
    return jax.nn.gelu(x, approximate=True)

def _silu(x):
    return jax.nn.silu(x)

def _sigmoid(x):
    return jax.nn.sigmoid(x)

def _layernorm(x, axis=-1, eps=1e-05):
    m = jnp.mean(x, axis=axis, keepdims=True)
    v = jnp.var(x, axis=axis, keepdims=True)
    return (x - m) / jnp.sqrt(v + eps)

def _scatter_add(tgt, idx, src, axis=0):
    return tgt.at[idx].add(src)

def _segment_sum(src, seg, n):
    return jax.ops.segment_sum(src, seg, n)
kernel_name = 'mk_hybrid_d1_jaxref_r4_dce767'

def setup_inputs(seed: int=0):
    np.random.seed(seed)
    _w = jnp.asarray

    def _L0_attn_a_setup():
        import jax, jax.numpy as jnp
        import numpy as np
        B, L, D, H = (8, 1024, 256, 16)
        DK = D // H
        key = jax.random.key(seed)
        x = jax.random.normal(key, (B, L, D), dtype=jnp.float32)
        return {'x': x}
    _L0_attn_a_in = _L0_attn_a_setup()

    def _L0_attn_b_setup():
        import jax, jax.numpy as jnp
        import numpy as np
        import math
        B, T, C = (4, 512, 256)
        H, DQK, DV = (16, 64, 64)
        key = jax.random.key(seed)
        k1, k2, k3, k4, k5 = jax.random.split(key, 5)
        x_q = jax.random.normal(k1, (B, T, C), dtype=jnp.float32)
        w_q = jax.random.normal(k2, (H, DQK, C), dtype=jnp.float32) / math.sqrt(C)
        w_k = jax.random.normal(k3, (H, DQK, C), dtype=jnp.float32) / math.sqrt(C)
        w_v = jax.random.normal(k4, (H, DV, C), dtype=jnp.float32) / math.sqrt(C)
        w_o = jax.random.normal(k5, (DV * H, C), dtype=jnp.float32) / math.sqrt(C)
        return {'x_q': x_q, 'w_q': w_q, 'w_k': w_k, 'w_v': w_v, 'w_o': w_o}
    _L0_attn_b_in = _L0_attn_b_setup()

    def _L0_ffn_setup():
        import jax, jax.numpy as jnp
        import numpy as np
        NUM_EXPERTS = 8
        EXPERT_CAPACITY = 2.0
        DIM = 256
        HIDDEN_DIM = 1024
        key = jax.random.key(seed)
        k_x, k_g, k_w1, k_w2 = jax.random.split(key, 4)
        n, t, d, f, e = (8, 256, DIM, HIDDEN_DIM, NUM_EXPERTS)
        x = jax.random.normal(k_x, (n, t, d), dtype=jnp.float32)
        gate_w = jax.random.normal(k_g, (e, d), dtype=jnp.float32) * 0.02
        w1 = jax.random.normal(k_w1, (e, d, f), dtype=jnp.float32) * 0.02
        w2 = jax.random.normal(k_w2, (e, f, d), dtype=jnp.float32) * 0.02
        return {'x': x, 'gate_w': gate_w, 'w1': w1, 'w2': w2}
    _L0_ffn_in = _L0_ffn_setup()
    _d = {'L0_attn_a_x': _L0_attn_a_in['x'], 'L0_attn_b_w_q': _L0_attn_b_in['w_q'], 'L0_attn_b_w_k': _L0_attn_b_in['w_k'], 'L0_attn_b_w_v': _L0_attn_b_in['w_v'], 'L0_attn_b_w_o': _L0_attn_b_in['w_o'], 'L0_ffn_gate_w': _L0_ffn_in['gate_w'], 'L0_ffn_w1': _L0_ffn_in['w1'], 'L0_ffn_w2': _L0_ffn_in['w2']}
    _x0 = _d['L0_attn_a_x']
    _d['L0_attn_a_x'] = jax.random.normal(jax.random.fold_in(jax.random.key(seed), 1), (4, 1024, 256), dtype=_x0.dtype)
    del _x0
    return _d

def reference(L0_attn_a_x, L0_attn_b_w_q, L0_attn_b_w_k, L0_attn_b_w_v, L0_attn_b_w_o, L0_ffn_gate_w, L0_ffn_w1, L0_ffn_w2):

    def _L0_attn_a_ref(x):
        import jax, jax.numpy as jnp
        import numpy as np
        B, L, D, H = (8, 1024, 256, 16)
        DK = D // H
        Bx, Lx, Dx = x.shape
        xh = x.reshape(Bx, Lx, H, DK).transpose(0, 2, 1, 3)
        m = xh.mean(axis=(0, 1))
        angle = jnp.clip(m @ m.T, -jnp.pi, jnp.pi)
        logits = jnp.sin(angle * 0.5) ** 2
        attn = jax.nn.softmax(logits, axis=-1)
        out = jnp.einsum('ij,bhjd->bhid', attn, xh)
        return out.transpose(0, 2, 1, 3).reshape(Bx, Lx, Dx)

    def _L0_attn_b_ref(x_q, w_q, w_k, w_v, w_o):
        import jax, jax.numpy as jnp
        import numpy as np
        import math
        B, T, C = (4, 512, 256)
        H, DQK, DV = (16, 64, 64)
        q = jnp.einsum('ntc,hdc->nhtd', x_q, w_q)
        k = jnp.einsum('ntc,hdc->nhtd', x_q, w_k)
        v = jnp.einsum('ntc,hdc->nhtd', x_q, w_v)
        a = jnp.einsum('nhtd,nhsd->nhts', q, k) / math.sqrt(q.shape[3])
        t = a.shape[2]
        causal_forbidden = jnp.arange(t)[:, None] < jnp.arange(t)[None, :]
        a = jnp.where(causal_forbidden[None, None], -jnp.inf, a)
        a = jax.nn.softmax(a, axis=3)
        y = jnp.einsum('nhts,nhsd->nthd', a, v).reshape(a.shape[0], t, -1)
        return y @ w_o

    def _L0_ffn_ref(x, gate_w, w1, w2):
        import jax, jax.numpy as jnp
        import numpy as np
        NUM_EXPERTS = 8
        EXPERT_CAPACITY = 2.0
        DIM = 256
        HIDDEN_DIM = 1024
        n, t, d = x.shape
        e = gate_w.shape[0]
        k = int(EXPERT_CAPACITY * t / e)
        scores = jnp.einsum('ntd,ed->nte', x, gate_w)
        probs = jax.nn.softmax(scores, axis=-1)
        g, m = jax.lax.top_k(probs.transpose(0, 2, 1), k)
        batch_idx = jnp.arange(n)[:, None, None]
        xin = x[batch_idx, m]
        h = jnp.einsum('nekd,edf->nekf', xin, w1)
        h = jax.nn.gelu(h, approximate=False)
        h = jnp.einsum('nekf,efd->nekd', h, w2)
        out_tok = g[..., None] * h
        out = jnp.zeros((n, t, d), dtype=x.dtype).at[batch_idx, m].add(out_tok)
        return out
    x = L0_attn_a_x
    x = x + _L0_attn_a_ref(_layernorm(x, axis=-1))
    x = x + _L0_ffn_ref(_layernorm(x, axis=-1), L0_ffn_gate_w, L0_ffn_w1, L0_ffn_w2)
    x = x + _L0_attn_b_ref(_layernorm(x, axis=-1), L0_attn_b_w_q, L0_attn_b_w_k, L0_attn_b_w_v, L0_attn_b_w_o)
    x = x + _L0_ffn_ref(_layernorm(x, axis=-1), L0_ffn_gate_w, L0_ffn_w1, L0_ffn_w2)
    return x

_drawn_inputs = setup_inputs


def setup_inputs(seed=0):
    import zlib

    import numpy as np

    out = dict(_drawn_inputs(seed))
    spreads = {}
    factors = {}
    for name, (base, spread) in spreads.items():
        noise = np.random.default_rng([zlib.crc32(name.encode()), seed]).standard_normal(out[name].shape)
        drawn = base * np.exp(spread * noise) if base else spread * noise
        out[name] = jnp.asarray(drawn.astype(out[name].dtype))
    for name, factor in factors.items():
        out[name] = (out[name] * factor).astype(out[name].dtype)
    return out
```

```python
from contextlib import ExitStack

import numpy as np
import concourse.bass as bass
from concourse import mybir

F32 = mybir.dt.float32
F32R = mybir.dt.float32r
BF16 = mybir.dt.bfloat16
I32 = mybir.dt.int32
U32 = mybir.dt.uint32
ALU = mybir.AluOpType
ACT = mybir.ActivationFunctionType
AX = mybir.AxisListType

P = 128
BANK = 512
EPS = 1e-5
NEG = -3.0e38


class Step:

    def __init__(self, queue):
        self.queue, self.needed, self.value = queue, False, None


class Transfer:

    def __init__(self, sem, value):
        self.sem, self.value = sem, value


class DmaSem:

    def __init__(self, sem):
        self.sem, self.count = sem, 0


class Queue:

    def __init__(self, sem):
        self.sem, self.items, self.last = sem, [], None

    def wait(self, *producers):
        for p in producers:
            if p is None:
                continue
            if isinstance(p, (list, tuple)):
                self.wait(*p)
                continue
            if isinstance(p, Step):
                p.needed = True
            self.items.append(("wait", p))

    def do(self, emit, *producers):
        self.wait(*producers)
        step = Step(self)
        self.items.append(("do", emit, step))
        self.last = step
        return step

    def dma(self, emit, sem, *producers):
        self.wait(*producers)
        sem.count += 16
        self.items.append(("dma", emit, sem.sem))
        return Transfer(sem.sem, sem.count)

    def number(self):
        n = 0
        for item in self.items:
            if item[0] == "do" and item[2].needed:
                n += 1
                item[2].value = n

    def play(self, engine):
        seen = {}
        for item in self.items:
            if item[0] == "wait":
                p = item[1]
                sem = p.queue.sem if isinstance(p, Step) else p.sem
                if seen.get(id(sem), 0) < p.value:
                    engine.wait_ge(sem, p.value)
                    seen[id(sem)] = p.value
            elif item[0] == "dma":
                item[1](engine).then_inc(item[2], 16)
            else:
                instruction = item[1](engine)
                if item[2].needed:
                    instruction.then_inc(self.sem, 1)


class Buffer:

    def __init__(self, ap):
        self.ap, self.users = ap, []

    def take(self):
        users, self.users = self.users, []
        return users

    def used_by(self, *steps):
        self.users += steps


class Ring:

    def __init__(self, buffers):
        self.buffers, self.n = list(buffers), 0

    def next(self):
        b = self.buffers[self.n % len(self.buffers)]
        self.n += 1
        return b


def spread(ap, axis, n):
    ap = ap.unsqueeze(axis)
    shape = list(ap.shape)
    shape[axis] = n
    return ap.to_broadcast(shape)


def interleave(*streams):
    live = [[g, w] for g, w in streams]
    while live:
        for s in list(live):
            for _ in range(s[1]):
                try:
                    next(s[0])
                except StopIteration:
                    live.remove(s)
                    break


class Program:
    def __init__(self, nc, ctx, shapes):
        self.nc, self.ctx = nc, ctx
        self.B, self.L, self.D = shapes["x"]
        self.E, self.F = shapes["w1"][0], shapes["w1"][2]
        self.H, self.DH = shapes["w_q"][0], shapes["w_q"][1]
        self.CAP = 2 * self.L // self.E
        self.NBLK = self.L // P
        self.DT = self.D // P
        self.FT = self.F // P
        self.n_names = 0
        self.pe = Queue(self.semaphore("pe_done"))
        self.act = Queue(self.semaphore("act_done"))
        self.dve = Queue(self.semaphore("dve_done"))
        self.pool = Queue(self.semaphore("pool_done"))
        self.sp = Queue(self.semaphore("sp_done"))
        self.queues = [self.pe, self.act, self.dve, self.pool, self.sp]
        self.dma_sems = []
        psum = self.psum("psum", [P, 8 * BANK])
        self.banks = [Buffer(psum[:, i * BANK:(i + 1) * BANK]) for i in range(8)]

    def semaphore(self, name):
        return self.ctx.enter_context(self.nc.semaphore(name))

    def dma_sem(self, name):
        s = DmaSem(self.semaphore(name))
        self.dma_sems.append(s)
        return s

    def sbuf(self, stack, name, shape, dtype=F32):
        self.n_names += 1
        return stack.enter_context(self.nc.sbuf_tensor(f"{name}_{self.n_names}", shape, dtype))

    def psum(self, name, shape):
        return self.ctx.enter_context(self.nc.psum_tensor(name, shape, F32))

    def barrier(self):
        last = [q.last for q in self.queues if q.last is not None]
        moved = [Transfer(s.sem, s.count) for s in self.dma_sems if s.count]
        for q in self.queues:
            q.wait(*last, *moved)

    def constants(self):
        pool, dve = self.pool, self.dve
        c = lambda name, shape, dtype=F32: self.sbuf(self.ctx, name, shape, dtype)
        self.ident = c("ident", [P, P])
        self.ident_b = c("ident_b", [P, P], BF16)
        self.ones = c("ones", [P, P])
        self.ones_b = c("ones_b", [P, P], BF16)
        self.upto_b = c("upto_b", [P, P], BF16)
        self.same_f = c("same_f", [P, self.E])
        self.same_b = c("same_b", [P, P], BF16)
        self.minus_half = c("minus_half", [P, self.NBLK])
        NP_ = self.NPASS = 8
        self.SHIFTS = [26, 22, 18, 14, 10, 6, 2, 0]
        self.digit = c("digit", [P, NP_], I32)
        lane = c("lane", [P, 1], I32)
        self.tokid = c("tokid", [P, self.NBLK])
        tok_i = c("tok_i", [P, self.NBLK], I32)
        self.iota16 = c("iota16", [P, 16])
        iota_i = c("iota_i", [P, 16], I32)
        self.zero_i = c("zero_i", [P, 1], I32)
        m = [pool.do(lambda e, t=t, v=v: e.memset(t[:], v))
             for t, v in ((self.ident, 0.0), (self.ident_b, 0.0), (self.ones, 1.0), (self.ones_b, 1.0),
                          (self.minus_half, -0.5))]
        pool.wait(m[-1])
        eye = dict(compare_op=ALU.not_equal, fill=1.0, base=0, pattern=[[-1, P]], channel_multiplier=1)
        pool.do(lambda e: e.affine_select(out=self.ident[:], in_=self.ident[:], **eye))
        pool.do(lambda e: e.affine_select(out=self.ident_b[:], in_=self.ident_b[:], **eye))
        pool.do(lambda e: e.affine_select(out=self.upto_b[:], in_=self.ones_b[:], compare_op=ALU.is_ge, fill=0.0,
                                          base=0, pattern=[[1, P]], channel_multiplier=-1))

        def same(out, in_, q, n):
            a = pool.do(lambda e: e.affine_select(out=out, in_=in_, compare_op=ALU.is_ge, fill=0.0, base=0,
                                                  pattern=[[-16, q]] + n, channel_multiplier=1))
            pool.do(lambda e: e.affine_select(out=out, in_=out, compare_op=ALU.is_ge, fill=0.0, base=15,
                                              pattern=[[16, q]] + [[-s, k] for s, k in n],
                                              channel_multiplier=-1), a)
        same(self.same_f[:], self.ones[:, 0:self.E], self.E, [])
        v = lambda t: t[:].rearrange("p (e j) -> p e j", j=16)
        same(v(self.same_b), v(self.ones_b), self.E, [[0, 16]])
        pool.do(lambda e: e.iota(lane[:], pattern=[[0, 1]], base=0, channel_multiplier=1))
        pool.do(lambda e: e.iota(tok_i[:], pattern=[[P, self.NBLK]], base=0, channel_multiplier=1))
        made = pool.do(lambda e: e.iota(iota_i[:], pattern=[[1, 16]], base=0, channel_multiplier=0))
        dve.do(lambda e: e.tensor_copy(self.tokid[:], tok_i[:]), made)
        dve.do(lambda e: e.tensor_copy(self.iota16[:], iota_i[:]))
        dve.do(lambda e: e.memset(self.zero_i[:], 0))
        for n, s in enumerate(self.SHIFTS):
            keep = 3 if s == 0 else 15
            dve.do(lambda e, n=n, s=s, k=keep: e.tensor_scalar(
                self.digit[:, n:n + 1], lane[:], k, s, ALU.bitwise_and, ALU.logical_shift_left))

    def layer_norm(self, x, y, stats, mv, rstd, nb, *ready):
        dve, pool = self.dve, self.pool
        dve.wait(*ready)
        for i in range(nb):
            s = dve.do(lambda e, i=i: e.bn_stats(stats[:, i, :], x[:, i, :]))
        for i in range(nb):
            s2 = dve.do(lambda e, i=i: e.bn_aggr(mv[:, i, :], stats[:, i, :]), s)
        s = dve.do(lambda e: e.tensor_scalar(rstd[:, 0:nb], mv[:, 0:nb, 1], EPS, None, ALU.add), s2)
        s = pool.do(lambda e: e.tensor_tensor(rstd[:, 0:nb], rstd[:, 0:nb], self.minus_half[:, 0:nb], ALU.pow), s)
        out = []
        for i in range(nb):
            out.append(dve.do(lambda e, i=i: e.tensor_scalar(y[:, i, :], x[:, i, :], mv[:, i, 0:1], rstd[:, i:i + 1],
                                                             ALU.subtract, ALU.mult), s))
        return out

    def stage_a(self, x_dram, out_dram, x_sem, out_sem):
        pe, act, dve, pool, sp = self.queues
        B, NBLK, D, DK = self.B, self.NBLK, self.D, 16
        H = D // DK
        half = BANK // D
        with ExitStack() as st:
            x = self.sbuf(st, "a_x", [P, B, NBLK, D])
            y = self.sbuf(st, "a_y", [P, NBLK, B, D])
            mix = self.sbuf(st, "a_mix", [P, NBLK, self.L])
            ang = [Buffer(self.sbuf(st, "a_ang", [P, self.L])) for _ in range(2)]
            stats = self.sbuf(st, "a_stats", [P, B, NBLK, 6])
            mv = self.sbuf(st, "a_mv", [P, B, NBLK, 2])
            rstd = self.sbuf(st, "a_rstd", [P, B, NBLK])
            msum = self.sbuf(st, "a_msum", [P, NBLK, DK])
            mT = self.sbuf(st, "a_mT", [DK, self.L])
            den = self.sbuf(st, "a_den", [P, NBLK])
            rden = self.sbuf(st, "a_rden", [P, NBLK])
            loads = []
            for b in range(B):
                loads.append(sp.dma(lambda e, b=b: e.dma_start(
                    x[:, b], x_dram[b * self.L:(b + 1) * self.L, :].rearrange("(n p) d -> p n d", p=P)), x_sem[b % 4]))
            norm = []
            for b in range(B):
                norm += self.layer_norm(x[:, b], y[:, :, b, :], stats[:, b], mv[:, b], rstd[:, b], NBLK, loads[b])
            sums = []
            for n in range(NBLK):
                s = dve.do(lambda e, n=n: e.tensor_reduce(
                    msum[:, n, :], y[:, n].rearrange("p b (h k) -> p k b h", k=DK), AX.XY, ALU.add), norm)
                sums.append(dve.do(lambda e, n=n: e.tensor_scalar(msum[:, n, :], msum[:, n, :], 1.0 / (B * H), None,
                                                                  ALU.mult), s))
            for c in range(2):
                bank = self.banks[c]
                pe.wait(bank.take())
                for n in range(4 * c, 4 * c + 4):
                    t = pe.do(lambda e, n=n, bank=bank: e.transpose(
                        bank.ap[0:DK, (n % 4) * P:(n % 4 + 1) * P], msum[:, n, :], self.ident[:]),
                        sums[n], pool.last if n == 0 else None)
                s = act.do(lambda e, c=c, bank=bank: e.copy(mT[:, c * BANK:(c + 1) * BANK], bank.ap[0:DK, :]), t)
                bank.used_by(s)
            mt_ready = s
            exps = []
            ring = Ring(self.banks[2:6])
            for n in range(NBLK):
                a = ang[n % 2]
                for c in range(2):
                    bank = ring.next()
                    t = pe.do(lambda e, n=n, c=c, bank=bank: e.matmul(
                        bank.ap, mT[:, n * P:(n + 1) * P], mT[:, c * BANK:(c + 1) * BANK], start=True, stop=True),
                        mt_ready, bank.take())
                    s = dve.do(lambda e, a=a, c=c, bank=bank: e.tensor_scalar(
                        a.ap[:, c * BANK:(c + 1) * BANK], bank.ap, float(np.pi), float(-np.pi), ALU.min, ALU.max),
                        t, a.take() if c == 0 else None)
                    bank.used_by(s)
                s = act.do(lambda e, a=a: e.activation(a.ap[:], a.ap[:], ACT.Sin, scale=0.5), s)
                s = pool.do(lambda e, a=a, n=n: e.tensor_tensor(mix[:, n, :], a.ap[:], a.ap[:], ALU.mult), s)
                a.used_by(s)
                exps.append(s)
            done = []
            for n in range(NBLK):
                s = act.do(lambda e, n=n: e.activation(mix[:, n, :], mix[:, n, :], ACT.Exp,
                                                       accum_out=den[:, n:n + 1]), exps[n])
                done.append(s)
            s = dve.do(lambda e: e.reciprocal(rden[:], den[:]), done[-1])
            pe.wait(done[-1], norm[-1])
            ring = Ring(self.banks)
            for i in range(NBLK):
                for c in range(B // half):
                    bank = ring.next()
                    pe.wait(bank.take())
                    for j in range(NBLK):
                        t = pe.do(lambda e, i=i, j=j, c=c, bank=bank: e.matmul(
                            bank.ap, mix[:, j, i * P:(i + 1) * P],
                            y[:, j, c * half:(c + 1) * half, :].rearrange("p b d -> p (b d)"),
                            start=(j == 0), stop=(j == NBLK - 1)))
                    v = bank.ap.rearrange("p (b d) -> p b d", b=half)
                    xs = x[:, c * half:(c + 1) * half, i, :]
                    t = dve.do(lambda e, v=v, xs=xs, i=i: e.scalar_tensor_tensor(
                        out=xs, in0=v, scalar=rden[:, i:i + 1], in1=xs, op0=ALU.mult, op1=ALU.add), t, s)
                    bank.used_by(t)
                    for b in range(c * half, (c + 1) * half):
                        r0 = b * self.L + i * P
                        sp.dma(lambda e, b=b, i=i, r0=r0: e.dma_start(out_dram[r0:r0 + P, :], x[:, b, i, :]),
                               out_sem, t)
            self.barrier()

    def stage_f_tiles(self, st):
        t = {}
        sb = lambda n, s, d=F32: self.sbuf(st, n, s, d)
        B, NBLK, D, E = self.B, self.NBLK, self.D, self.E
        t["x"] = Ring([Buffer(sb("f_x", [P, NBLK, D]))])
        t["y"] = Ring([Buffer(sb("f_y", [P, NBLK, D]))])
        t["yT"] = Ring([Buffer(sb("f_yT", [P, self.DT, self.L]))])
        t["stats"] = sb("f_stats", [P, NBLK, 6])
        t["mv"] = sb("f_mv", [P, NBLK, 2])
        t["rstd"] = sb("f_rstd", [P, NBLK])
        for n in ("scd", "ex", "pr"):
            t[n] = sb("f_" + n, [P, NBLK, E])
        for n in ("mx", "sm"):
            t[n] = sb("f_" + n, [P, NBLK])
        t["wide"] = sb("f_wide", [P, NBLK, E, 16])
        t["pT"] = sb("f_pT", [P, self.L])
        t["junk"] = sb("f_junk", [P, self.L], BF16)
        t["cnt"] = sb("f_cnt", [P, 1])
        t["ind"] = sb("f_ind", [P, 1], BF16)
        t["bits"] = sb("f_bits", [P, 1], I32)
        t["prefix"] = sb("f_prefix", [P, 1], I32)
        t["thr"] = sb("f_thr", [P, 1], I32)
        t["Tfull"] = sb("f_Tfull", [P, P])
        t["Tb"] = sb("f_Tb", [P, E])
        t["ge"] = sb("f_ge", [P, 2, NBLK, E], BF16)
        t["need"] = sb("f_need", [P, E])
        for n in ("m1", "sel", "pos"):
            t[n] = sb("f_" + n, [P, NBLK, E])
        for n in ("key", "hi4", "lo4"):
            t[n] = sb("f_" + n, [P, NBLK, E], I32)
        t["A"] = sb("f_A", [P, NBLK, E, 16])
        t["C"] = sb("f_C", [P, NBLK, E, 16, 2])
        t["Rw"] = sb("f_Rw", [P, E, 32])
        t["R"] = sb("f_R", [P, 32])
        t["tab"] = [sb("f_tab", [P, E, 2, 2]) for _ in range(B)]
        t["idx"] = [sb("f_idx", [P, E, 2], U32) for _ in range(B)]
        t["row"] = [sb("f_row", [P, E, 2], U32) for _ in range(B)]
        t["wst"] = Buffer(sb("f_wst", [P, 2, self.DT * self.F]))
        t["whi"] = [Buffer(sb("f_whi", [P, 2, self.DT * self.F], F32R)) for _ in range(2)]
        t["wlo"] = [Buffer(sb("f_wlo", [P, 2, self.DT * self.F], F32R)) for _ in range(2)]
        t["xg"] = Ring([Buffer(sb("f_xg", [P, D])) for _ in range(8)])
        t["xin"] = Ring([Buffer((sb("f_xhi", [P, self.DT, BANK], F32R), sb("f_xlo", [P, self.DT, BANK], F32R)))
                         for _ in range(1)])
        t["h"] = Ring([Buffer(sb("f_h", [P, BANK])) for _ in range(2)])
        t["hs"] = [Buffer((sb("f_hhi", [P, BANK], F32R), sb("f_hlo", [P, BANK], F32R))) for _ in range(self.FT)]
        t["yo"] = Ring([Buffer(sb("f_yo", [P, D])) for _ in range(4)])
        return t

    def route(self, b, t, res_dram, ysc, tabs, gateT, sems):
        pe, act, dve, pool, sp = self.queues
        NBLK, D, E, DT, L = self.NBLK, self.D, self.E, self.DT, self.L
        ring = self.route_banks
        xb, yb, yTb = t["x"].next(), t["y"].next(), t["yT"].next()
        rows = slice(b * L, (b + 1) * L)
        s = sp.dma(lambda e: e.dma_start(xb.ap[:], res_dram[rows, :].rearrange("(n p) d -> p n d", p=P)),
                   sems["x"], xb.take())
        dve.wait(yb.take())
        norm = self.layer_norm(xb.ap, yb.ap, t["stats"], t["mv"], t["rstd"], NBLK, s, self.rstd_user)
        self.rstd_user = norm[-1]
        xb.used_by(norm[-1])
        s = sp.dma(lambda e: e.dma_start(ysc[b].rearrange("(n p) d -> p n d", p=P), yb.ap[:]),
                   sems["y"][b], norm[-1])
        yb.used_by(s)
        self.y_written[b] = s
        yield
        act.wait(yTb.take())
        for dt in range(DT):
            for c in range(2):
                bank = ring.next()
                pe.wait(bank.take())
                for n in range(4 * c, 4 * c + 4):
                    s = pe.do(lambda e, n=n, bank=bank, dt=dt: e.transpose(
                        bank.ap[:, (n % 4) * P:(n % 4 + 1) * P], yb.ap[:, n, dt * P:(dt + 1) * P], self.ident[:]),
                        norm[-1])
                ev = act.do(lambda e, c=c, bank=bank, dt=dt: e.copy(
                    yTb.ap[:, dt, c * BANK:(c + 1) * BANK], bank.ap), s)
                bank.used_by(ev)
                yield
        yb.used_by(s)
        bank = ring.next()
        pe.wait(bank.take(), ev)
        for n in range(NBLK):
            for dt in range(DT):
                s = pe.do(lambda e, n=n, dt=dt, bank=bank: e.matmul(
                    bank.ap[:, n * E:(n + 1) * E], yTb.ap[:, dt, n * P:(n + 1) * P], gateT[:, dt, :],
                    start=(dt == 0), stop=(dt == DT - 1)))
        yTb.used_by(s)
        sc = bank.ap[:, 0:NBLK * E].rearrange("p (n e) -> p n e", e=E)
        s = dve.do(lambda e: e.tensor_reduce(t["mx"][:], sc, AX.X, ALU.max), s)
        s = dve.do(lambda e: e.tensor_tensor(t["scd"][:], sc, spread(t["mx"][:], 2, E), ALU.subtract), s)
        bank.used_by(s)
        yield
        s = act.do(lambda e: e.activation(t["ex"][:], t["scd"][:], ACT.Exp), s)
        s = dve.do(lambda e: e.tensor_reduce(t["sm"][:], t["ex"][:], AX.X, ALU.add), s)
        s = dve.do(lambda e: e.reciprocal(t["sm"][:], t["sm"][:]), s)
        s = dve.do(lambda e: e.tensor_tensor(t["pr"][:], t["ex"][:], spread(t["sm"][:], 2, E), ALU.mult), s)
        s = dve.do(lambda e: e.tensor_copy(t["wide"][:], spread(t["pr"][:], 3, 16)), s)
        yield
        for c in range(2):
            bank = ring.next()
            pe.wait(bank.take(), s)
            for n in range(4 * c, 4 * c + 4):
                m = pe.do(lambda e, n=n, bank=bank: e.transpose(
                    bank.ap[:, (n % 4) * P:(n % 4 + 1) * P],
                    t["wide"][:, n].rearrange("p e j -> p (e j)"), self.ident[:]))
            ev = act.do(lambda e, c=c, bank=bank: e.copy(t["pT"][:, c * BANK:(c + 1) * BANK], bank.ap), m)
            bank.used_by(ev)
        yield
        prefix, thr = self.zero_i, self.digit[:, 0:1]
        for n, shift in enumerate(self.SHIFTS):
            s = dve.do(lambda e, thr=thr: e.tensor_scalar(
                t["junk"][:], t["pT"][:], thr.bitcast(F32), 0.0, ALU.is_ge, ALU.add, accum_out=t["cnt"][:]), ev, s)
            s = dve.do(lambda e: e.tensor_scalar(t["ind"][:], t["cnt"][:], self.CAP - 0.5, None, ALU.is_ge), s)
            bank = ring.next()
            s = pe.do(lambda e, bank=bank: e.matmul(bank.ap[:, 0:1], self.same_b[:], t["ind"][:],
                                                    start=True, stop=True), s, bank.take())
            copies = 4 if shift == 0 else 1
            s = dve.do(lambda e, bank=bank, a=float(1 << shift) / copies, c=-float(1 << shift): e.tensor_scalar(
                t["bits"][:], bank.ap[:, 0:1], a, c, ALU.mult, ALU.add), s)
            bank.used_by(s)
            s = dve.do(lambda e, p=prefix: e.tensor_tensor(t["prefix"][:], p[:], t["bits"][:], ALU.bitwise_or), s)
            prefix = t["prefix"]
            if n + 1 < len(self.SHIFTS):
                s = dve.do(lambda e, n=n: e.tensor_tensor(t["thr"][:], prefix[:], self.digit[:, n + 1:n + 2],
                                                          ALU.bitwise_or), s)
                thr = t["thr"][:, 0:1]
            yield
        s = dve.do(lambda e: e.tensor_copy(t["Tfull"][:], prefix[:].bitcast(F32).to_broadcast([P, P])), s)
        bank = ring.next()
        s = pe.do(lambda e, bank=bank: e.transpose(bank.ap[:, 0:P], t["Tfull"][:], self.ident[:]), s, bank.take())
        s = dve.do(lambda e, bank=bank: e.tensor_copy(
            t["Tb"][:], bank.ap[:, 0:P].rearrange("p (e j) -> p e j", j=16)[:, :, 0]), s)
        bank.used_by(s)
        Tb = spread(t["Tb"][:], 1, NBLK)
        g1 = dve.do(lambda e: e.tensor_tensor(t["ge"][:, 0], t["pr"][:], Tb, ALU.is_gt), s)
        s = dve.do(lambda e: e.tensor_tensor(t["ge"][:, 1], t["pr"][:], Tb, ALU.is_equal), s)
        yield
        cb, tb_ = ring.next(), ring.next()
        cu = cb.ap[:, 0:2 * NBLK * E].rearrange("p (g n e) -> p g n e", g=2, e=E)
        tot = tb_.ap[:, 0:E]
        pe.wait(cb.take(), tb_.take(), s)
        pe.do(lambda e: e.matmul(cb.ap[:, 0:2 * NBLK * E], self.upto_b[:],
                                 t["ge"][:].rearrange("p g n e -> p (g n e)"),
                                 start=True, stop=False, skip_group_check=True))
        for n in range(NBLK - 1):
            for g in range(2):
                pe.do(lambda e, n=n, g=g: e.matmul(
                    cu[:, g, n + 1:, :], self.ones_b[:], spread(t["ge"][:, g, n, :], 1, NBLK - 1 - n),
                    start=False, stop=(n == NBLK - 2 and g == 1), skip_group_check=True))
        for n in range(NBLK):
            s = pe.do(lambda e, n=n: e.matmul(tot, self.ones_b[:], t["ge"][:, 0, n, :],
                                              start=(n == 0), stop=(n == NBLK - 1)))
        yield
        s = dve.do(lambda e: e.tensor_scalar(t["need"][:], tot, -1.0, float(self.CAP), ALU.mult, ALU.add), s)
        tb_.used_by(s)
        need = spread(t["need"][:], 1, NBLK)
        s = dve.do(lambda e: e.tensor_tensor(t["m1"][:], cu[:, 1], need, ALU.is_le), s)
        s2 = dve.do(lambda e: e.tensor_tensor(t["pos"][:], cu[:, 1], need, ALU.min), s)
        s = dve.do(lambda e: e.tensor_tensor(t["sel"][:], t["m1"][:], t["ge"][:, 1], ALU.mult), s)
        s2 = dve.do(lambda e: e.tensor_tensor(t["pos"][:], cu[:, 0], t["pos"][:], ALU.add), s2)
        cb.used_by(s2)
        s = dve.do(lambda e: e.tensor_tensor(t["sel"][:], t["sel"][:], t["ge"][:, 0], ALU.add), s)
        s = dve.do(lambda e: e.tensor_tensor(t["pos"][:], t["pos"][:], t["sel"][:], ALU.mult), s, s2)
        s = dve.do(lambda e: e.tensor_scalar(t["key"][:], t["pos"][:], -1.0, None, ALU.add), s)
        dve.do(lambda e: e.tensor_scalar(t["hi4"][:], t["key"][:], 4, None, ALU.arith_shift_right), s)
        s = dve.do(lambda e: e.tensor_scalar(t["lo4"][:], t["key"][:], 15, None, ALU.bitwise_and), s)
        yield
        i16 = spread(spread(self.iota16[:], 1, E), 1, NBLK)
        s1 = dve.do(lambda e: e.tensor_tensor(t["A"][:], spread(t["hi4"][:], 3, 16), i16, ALU.is_equal), s)
        s = dve.do(lambda e: e.tensor_tensor(t["C"][:, :, :, :, 0], spread(t["lo4"][:], 3, 16), i16, ALU.is_equal), s)
        s2 = pool.do(lambda e: e.tensor_tensor(t["C"][:, :, :, :, 1], t["C"][:, :, :, :, 0],
                                               spread(t["pr"][:], 3, 16), ALU.mult), s)
        s = dve.do(lambda e: e.tensor_tensor(t["C"][:, :, :, :, 0], t["C"][:, :, :, :, 0],
                                             spread(spread(self.tokid[:], 2, E), 3, 16), ALU.mult), s2)
        yield
        bank = ring.next()
        pe.wait(bank.take(), s, s1, s2)
        for n in range(NBLK):
            m = pe.do(lambda e, n=n, bank=bank: e.matmul(
                bank.ap[:, 0:E * 32], t["A"][:, n].rearrange("p e a -> p (e a)"),
                t["C"][:, n].rearrange("p e c t -> p (e c t)"), start=(n == 0), stop=(n == NBLK - 1)))
        s = dve.do(lambda e, bank=bank: e.tensor_tensor(
            t["Rw"][:], bank.ap[:, 0:E * 32].rearrange("p (e k) -> p e k", e=E),
            spread(self.same_f[:], 2, 32), ALU.mult), m)
        bank.used_by(s)
        s = dve.do(lambda e: e.tensor_reduce(t["R"][:], t["Rw"][:].rearrange("p e k -> p k e"), AX.X, ALU.add),
                   s, self.r_user)
        s = sp.dma(lambda e: e.dma_start(tabs[b].rearrange("e (a k) -> (e a) k", a=16), t["R"][:]), sems["tab"], s)
        self.r_user = s
        tab, idx = t["tab"][b], t["idx"][b]
        s = sp.dma(lambda e: e.dma_start(
            tab[:].rearrange("p e h t -> p e (h t)"), tabs[b].rearrange("e (q k) -> q e k", k=4)),
            sems["tab"], s)
        yield
        dve.do(lambda e: e.tensor_copy(idx[:], tab[:, :, :, 0]), s)
        s = dve.do(lambda e: e.tensor_scalar(t["row"][b][:], tab[:, :, :, 0], float(b * L), None, ALU.add))
        self.idx_ready[b] = s
        yield

    def load_expert(self, e_, t, w1, w2, sems):
        pe, act, dve, pool, sp = self.queues
        D, Fh, DT, FT = self.D, self.F, self.DT, self.FT
        n = self.loaded
        self.loaded += 1
        stg, hi, lo = t["wst"], t["whi"][n % 2], t["wlo"][n % 2]
        users = stg.take()
        a = sp.dma(lambda e: e.dma_start(stg.ap[:, 0].rearrange("p (k f) -> p k f", k=DT),
                                         w1[e_].rearrange("(k p) f -> p k f", p=P)), sems["w1"], users)
        c = sp.dma(lambda e: e.dma_start(stg.ap[:, 1].rearrange("p (k d) -> p k d", k=FT),
                                         w2[e_].rearrange("(k p) d -> p k d", p=P)), sems["w2"], users)
        act.wait(hi.take())
        pool.wait(lo.take())
        steps = []
        for i, ready in ((0, a), (1, c)):
            for h in range(2):
                k = slice(h * DT * Fh // 2, (h + 1) * DT * Fh // 2)
                s = act.do(lambda e, i=i, k=k: e.copy(hi.ap[:, i, k], stg.ap[:, i, k]), ready)
                s = pool.do(lambda e, i=i, k=k: e.tensor_tensor(lo.ap[:, i, k], stg.ap[:, i, k],
                                                                hi.ap[:, i, k].bitcast(F32), ALU.subtract), s)
                stg.used_by(s)
                steps.append(s)
                yield
        self.weights[n] = (hi, lo, steps)

    def experts(self, pair, t, w1, w2, ysc, res_dram, sems):
        pe, act, dve, pool, sp = self.queues
        D, DT, FT, E = self.D, self.DT, self.FT, self.E
        x0, x1 = self.banks[0], self.banks[1]
        up = Ring(self.banks[2:4])
        down = self.banks[4:6]

        def gather(e_):
            tiles = []
            for b in pair:
                for h in range(2):
                    g = t["xg"].next()
                    s = pool.dma(lambda e, g=g, b=b, h=h: e.indirect_dma_start(
                        out=g.ap[:], out_offset=None, in_=ysc[b],
                        in_offset=bass.IndirectOffsetOnAxis(ap=t["idx"][b][:, e_, h:h + 1], axis=0)),
                        sems["xg"][(t["xg"].n - 1) % 8], g.take(), self.idx_ready[b], self.y_written[b])
                    tiles.append((g, s))
            return tiles

        def xin(tiles):
            buf = t["xin"].next()
            hi, lo = buf.ap
            pe.wait(x0.take(), x1.take())
            for k, (g, s) in enumerate(tiles):
                pe.wait(s)
                for dt, bank in enumerate((x0, x1)):
                    m = pe.do(lambda e, k=k, g=g, dt=dt, bank=bank: e.transpose(
                        bank.ap[:, k * P:(k + 1) * P], g.ap[:, dt * P:(dt + 1) * P], self.ident[:]))
                g.used_by(m)
            out = []
            act.wait(buf.take())
            for dt, bank in enumerate((x0, x1)):
                a = act.do(lambda e, dt=dt, bank=bank: e.copy(hi[:, dt, :], bank.ap), m)
                c = dve.do(lambda e, dt=dt, bank=bank: e.tensor_tensor(lo[:, dt, :], bank.ap,
                                                                       hi[:, dt, :].bitcast(F32), ALU.subtract), a)
                bank.used_by(c)
                out.append(c)
            return buf, hi, lo, out

        buf, xhi, xlo, xready = xin(gather(0))
        yield
        for e_ in range(E):
            tiles = gather(e_ + 1) if e_ + 1 < E else None
            while self.used not in self.weights:
                next(self.weights_ahead)
            whi, wlo, wready = self.weights[self.used]
            self.used += 1
            pe.wait(xready, wready)
            w1h = whi.ap[:, 0].rearrange("p (k f) -> p k f", k=DT)
            w1l = wlo.ap[:, 0].rearrange("p (k f) -> p k f", k=DT)
            w2h = whi.ap[:, 1].rearrange("p (k d) -> p k d", k=FT)
            w2l = wlo.ap[:, 1].rearrange("p (k d) -> p k d", k=FT)
            hready = []
            for f in range(FT):
                bank = up.next()
                pe.wait(bank.take())
                fs = slice(f * P, (f + 1) * P)
                terms = [(w, x, dt) for dt in range(DT) for w, x in ((w1h, xhi), (w1h, xlo), (w1l, xhi))]
                for k, (w, x, dt) in enumerate(terms):
                    m = pe.do(lambda e, w=w, x=x, dt=dt, fs=fs, bank=bank, k=k: e.matmul(
                        bank.ap, w[:, dt, fs], x[:, dt, :], start=(k == 0), stop=(k == len(terms) - 1)))
                hb, parts = t["h"].next(), t["hs"][f]
                hhi, hlo = parts.ap
                a = act.do(lambda e, hb=hb, bank=bank: e.activation(hb.ap[:], bank.ap, ACT.Gelu), m, hb.take())
                bank.used_by(a)
                c = dve.do(lambda e, hb=hb, hhi=hhi: e.tensor_copy(hhi[:], hb.ap[:]), a, parts.take())
                c = dve.do(lambda e, hb=hb, hhi=hhi, hlo=hlo: e.tensor_tensor(
                    hlo[:], hb.ap[:], hhi[:].bitcast(F32), ALU.subtract), c)
                hb.used_by(c)
                hready.append(c)
                yield
            buf.used_by(m)
            if tiles:
                buf, xhi, xlo, xready = xin(tiles)
            for bank in down:
                pe.wait(bank.take())
            for f in range(FT):
                pe.wait(hready[f])
                hhi, hlo = t["hs"][f].ap
                for k in range(4):
                    bank = down[k // 2]
                    ks = slice(k * P, (k + 1) * P)
                    out = bank.ap[:, (k % 2) * D:(k % 2 + 1) * D]
                    for j, (h, w) in enumerate(((hhi, w2h), (hhi, w2l), (hlo, w2h))):
                        m = pe.do(lambda e, h=h, w=w, ks=ks, out=out, f=f, j=j, k=k: e.matmul(
                            out, h[:, ks], w[:, f, :], start=(f == 0 and j == 0 and k % 2 == 0),
                            stop=(f == FT - 1 and j == 2), skip_group_check=True))
                t["hs"][f].used_by(m)
                if f % 2:
                    yield
            whi.used_by(m)
            wlo.used_by(m)
            self.through += 1
            for k in range(4):
                b, h = pair[k // 2], k % 2
                bank = down[k // 2]
                yo = t["yo"].next()
                s = act.do(lambda e, yo=yo, bank=bank, h=h, b=b, e_=e_: e.mul(
                    yo.ap[:], bank.ap[:, h * D:(h + 1) * D], t["tab"][b][:, e_, h, 1:2]), m, yo.take())
                bank.used_by(s)
                s = pool.dma(lambda e, yo=yo, b=b, h=h, e_=e_: e.indirect_dma_start(
                    out=res_dram[:, :], out_offset=bass.IndirectOffsetOnAxis(ap=t["row"][b][:, e_, h:h + 1], axis=0),
                    in_=yo.ap[:], in_offset=None, compute_op=ALU.add),
                    sems["add"][b][h], s, self.added[b])
                yo.used_by(s)
                self.adding[b].append(s)
                if h == 1:
                    self.added[b], self.adding[b] = self.adding[b], []
            yield

    def stage_f(self, res_dram, gate_w, w1, w2, ysc, tabs, sems):
        pe, act, dve, pool, sp = self.queues
        with ExitStack() as st:
            t = self.stage_f_tiles(st)
            self.route_banks = Ring(self.banks[6:8])
            self.y_written, self.idx_ready = {}, {}
            self.added = {b: [] for b in range(self.B)}
            self.adding = {b: [] for b in range(self.B)}
            self.rstd_user = self.r_user = None
            self.loaded = self.used = self.through = 0
            self.weights = {}
            gate = self.sbuf(st, "f_gate", [self.E, self.D])
            gateT = self.sbuf(st, "f_gateT", [P, self.DT, self.E])
            s = sp.dma(lambda e: e.dma_start(gate[:], gate_w), sems["gate"])
            bank = self.route_banks.next()
            pe.wait(bank.take(), s, pool.last)
            for dt in range(self.DT):
                m = pe.do(lambda e, dt=dt: e.transpose(bank.ap[:, dt * self.E:(dt + 1) * self.E],
                                                       gate[:, dt * P:(dt + 1) * P], self.ident[0:self.E, 0:self.E]))
            s = dve.do(lambda e: e.tensor_copy(gateT[:], bank.ap[:, 0:self.DT * self.E].rearrange(
                "p (k e) -> p k e", e=self.E)), m)
            bank.used_by(s)
            pe.wait(s)
            route = lambda b: self.route(b, t, res_dram, ysc, tabs, gateT, sems)
            n_pairs = self.B // 2
            order = [e_ for _ in range(n_pairs) for e_ in range(self.E)]

            def prefetch():
                for k, e_ in enumerate(order[2:]):
                    while self.through <= k:
                        yield
                    yield from self.load_expert(e_, t, w1, w2, sems)

            def chain(*gens):
                for g in gens:
                    yield from g
            ahead = chain(*(self.load_expert(e_, t, w1, w2, sems) for e_ in order[:2]))
            interleave((chain(route(0), route(1)), 1), (ahead, 1))
            later = chain(*(route(b) for b in range(2, self.B)))
            self.weights_ahead = prefetch()
            pairs = [(2 * k, 2 * k + 1) for k in range(n_pairs)]

            def work():
                for k, pair in enumerate(pairs):
                    for _ in self.experts(pair, t, w1, w2, ysc, res_dram, sems):
                        self.pump(self.weights_ahead)
                        if k == 0:
                            self.pump(later)
                        yield
                    if k == 0:
                        for _ in later:
                            pass
            for _ in work():
                pass
            self.barrier()

    @staticmethod
    def pump(gen):
        try:
            next(gen)
        except StopIteration:
            pass

    def transpose_weights(self, st, weights, scratch, sems):
        pe, act, dve, pool, sp = self.queues
        NT = self.H * self.DH // P
        natural = Ring([Buffer(self.sbuf(st, "w_nat", [P, NT, self.D])) for _ in range(2)])
        parts = Ring([Buffer(self.sbuf(st, "w_parts", [P, NT, 2, self.DT, P], F32R)) for _ in range(2)])
        ring = Ring(self.banks[6:8])
        for i, (w, out) in enumerate(zip(weights, scratch)):
            nat, prt = natural.next(), parts.next()
            s = sp.dma(lambda e, w=w, nat=nat: e.dma_start(nat.ap[:], w.rearrange("h d c -> (h d) c").rearrange(
                "(n p) c -> p n c", p=P)), sems["nat"][i], nat.take())
            act.wait(prt.take())
            for ct in range(self.DT):
                for c in range(NT // 4):
                    bank = ring.next()
                    pe.wait(bank.take(), s)
                    for n in range(4 * c, 4 * c + 4):
                        m = pe.do(lambda e, n=n, ct=ct, bank=bank, nat=nat: e.transpose(
                            bank.ap[:, (n % 4) * P:(n % 4 + 1) * P], nat.ap[:, n, ct * P:(ct + 1) * P], self.ident[:]))
                    v = bank.ap.rearrange("p (n j) -> p n j", j=P)
                    ns = slice(4 * c, 4 * c + 4)
                    a = act.do(lambda e, v=v, ns=ns, ct=ct, prt=prt: e.copy(prt.ap[:, ns, 0, ct, :], v), m)
                    d = dve.do(lambda e, v=v, ns=ns, ct=ct, prt=prt: e.tensor_tensor(
                        prt.ap[:, ns, 1, ct, :], v, prt.ap[:, ns, 0, ct, :].bitcast(F32), ALU.subtract), a)
                    bank.used_by(d)
            nat.used_by(m)
            s = sp.dma(lambda e, prt=prt, out=out: e.dma_start(
                out.rearrange("n p k -> p n k"), prt.ap[:].rearrange("p n t c j -> p n (t c j)").bitcast(F32)),
                sems["wT"][i], d)
            prt.used_by(s)

    def stage_t(self, x_dram, out_dram, w_o, scratch, sems):
        pe, act, dve, pool, sp = self.queues
        B, L, D, NBLK, DT, DH = self.B, self.L, self.D, self.NBLK, self.DT, self.DH
        NHP = self.H // 2
        NC = L // BANK
        KPC = BANK // P
        QROWS = DH + NBLK
        scale = 1.0 / float(np.sqrt(DH))
        with ExitStack() as st:
            sb = lambda n, s, d=F32: self.sbuf(st, n, s, d)
            xy = Buffer(sb("t_xy", [P, NBLK, D]))
            xres = Buffer(sb("t_xres", [P, NBLK, D]))
            xT = Buffer((sb("t_xThi", [P, DT, L], F32R), sb("t_xTlo", [P, DT, L], F32R)))
            stats, mv, rstd = sb("t_stats", [P, NBLK, 6]), sb("t_mv", [P, NBLK, 2]), sb("t_rstd", [P, NBLK])
            wo = sb("t_wo", [P, NHP, D])
            wq_r = Ring([Buffer(sb("t_wq", [P, 2, DT, P], F32R)) for _ in range(2)])
            wk_r = Ring([Buffer(sb("t_wk", [P, 2, DT, P], F32R)) for _ in range(2)])
            wv_r = Ring([Buffer(sb("t_wv", [P, 2, 2, DT, P], F32R)) for _ in range(1)])
            v_r = Ring([Buffer(sb("t_v", [P, NBLK, 4 * DH])) for _ in range(2)])
            heads = [[Buffer({k: sb("t_" + k, [P, L], F32R) for k in ("qa", "qb", "ka", "kb")}) for _ in range(2)]
                     for _ in range(2)]
            p_r = Ring([Buffer(sb("t_p", [P, BANK])) for _ in range(6)])
            acc_r = Ring([Buffer(sb("t_acc", [P, BANK])) for _ in range(4)])
            yT = Buffer(sb("t_yT", [P, NHP, L]))
            rden_r = Ring([Buffer(sb("t_rden", [P, BANK])) for _ in range(1)])
            mask = sb("t_mask", [P, BANK])
            pick = sb("t_pick", [NBLK, NBLK, P])
            junk_r = Ring([Buffer(sb("t_junk", [P, BANK], BF16)) for _ in range(3)])
            mcol_r = Ring([Buffer(sb("t_mcol", [P, 2, NBLK])) for _ in range(2)])
            score_banks, st_banks = Ring(self.banks[0:2]), Ring(self.banks[2:5])
            pv_bank, den_bank, misc = self.banks[5], self.banks[6], self.banks[7]

            s = pool.do(lambda e: e.memset(mask[:], 0.0))
            s2 = pool.do(lambda e: e.memset(pick[:], 0.0))
            pool.do(lambda e: e.affine_select(out=mask[:], in_=mask[:], compare_op=ALU.is_ge, fill=NEG,
                                              base=BANK - P, pattern=[[-1, BANK]], channel_multiplier=1), s, s2)
            consts = pool.do(lambda e: e.affine_select(out=pick[:], in_=pick[:], compare_op=ALU.not_equal, fill=-1.0,
                                                       base=0, pattern=[[-1, NBLK], [0, P]], channel_multiplier=1))
            for pair in heads:
                for hd in pair:
                    consts = dve.do(lambda e, hd=hd: e.tensor_copy(
                        hd.ap["kb"][DH:QROWS, :].rearrange("p (a b) -> p a b", b=P),
                        spread(self.ones[DH:QROWS, :], 1, NBLK)), consts)
            wo_ready = sp.dma(lambda e: e.dma_start(wo[:], w_o.rearrange("(n p) d -> p n d", p=P)), sems["w1"])
            dve.wait(consts)
            pe.wait(consts)
            self.t_rstd_user = None
            vbuf = {}
            ready = {}

            def prepare(b):
                rows = slice(b * L, (b + 1) * L)
                s = sp.dma(lambda e: e.dma_start(xy.ap[:], x_dram[rows, :].rearrange("(n p) d -> p n d", p=P)),
                           sems["x"], xy.take())
                norm = self.layer_norm(xy.ap, xy.ap, stats, mv, rstd, NBLK, s, self.t_rstd_user)
                self.t_rstd_user = norm[-1]
                yield
                hi, lo = xT.ap
                act.wait(xT.take())
                for dt in range(DT):
                    for c in range(NC):
                        bank = misc
                        pe.wait(bank.take(), norm[-1])
                        for n in range(4 * c, 4 * c + 4):
                            m = pe.do(lambda e, n=n, dt=dt, bank=bank: e.transpose(
                                bank.ap[:, (n % 4) * P:(n % 4 + 1) * P], xy.ap[:, n, dt * P:(dt + 1) * P],
                                self.ident[:]))
                        cs = slice(c * BANK, (c + 1) * BANK)
                        a = act.do(lambda e, dt=dt, cs=cs, bank=bank: e.copy(hi[:, dt, cs], bank.ap), m)
                        d = dve.do(lambda e, dt=dt, cs=cs, bank=bank: e.tensor_tensor(
                            lo[:, dt, cs], bank.ap, hi[:, dt, cs].bitcast(F32), ALU.subtract), a)
                        bank.used_by(d)
                        yield
                xy.used_by(m)
                pe.wait(d)

            def project(b, hp):
                if hp == 0:
                    yield from prepare(b)
                xhi, xlo = xT.ap
                wq, wk = wq_r.next(), wk_r.next()
                pair = heads[hp % 2]
                views = []
                for w, ring, d in ((wq, wq_r, scratch[0]), (wk, wk_r, scratch[1])):
                    s = sp.dma(lambda e, w=w, d=d: e.dma_start(w.ap[:].rearrange("p t c j -> p (t c j)").bitcast(F32), d[hp]),
                               sems["wqk"][hp % 2], w.take())
                    views.append(w)
                pe.wait(s)
                for hd in pair:
                    users = hd.take()
                    act.wait(users), dve.wait(users), pool.wait(users)
                out = []
                for is_k, w in enumerate(views):
                    for c in range(NC):
                        cs = slice(c * BANK, (c + 1) * BANK)
                        bank = misc
                        pe.wait(bank.take())
                        terms = [(pw, px, ct) for ct in range(DT) for pw, px in ((0, xhi), (1, xhi), (0, xlo))]
                        for k, (pw, px, ct) in enumerate(terms):
                            m = pe.do(lambda e, w=w, pw=pw, px=px, ct=ct, k=k, cs=cs, bank=bank: e.matmul(
                                bank.ap, w.ap[:, pw, ct, :], px[:, ct, cs],
                                start=(k == 0), stop=(k == len(terms) - 1)))
                        yield
                        for i, hd in enumerate(pair):
                            src = bank.ap[i * DH:(i + 1) * DH, :]
                            t = hd.ap
                            hi = t["ka" if is_k else "qa"]
                            a = act.do(lambda e, hi=hi, cs=cs, src=src: e.copy(hi[0:DH, cs], src), m)
                            lo = t["kb"][0:DH, cs] if is_k else t["qa"][DH:2 * DH, cs]
                            d = dve.do(lambda e, lo=lo, hi=hi, cs=cs, src=src: e.tensor_tensor(
                                lo, src, hi[0:DH, cs].bitcast(F32), ALU.subtract), a)
                            dup = t["ka"][DH:2 * DH, cs] if is_k else t["qb"][0:DH, cs]
                            g = pool.do(lambda e, dup=dup, hi=hi, cs=cs: e.tensor_copy(
                                dup, hi[0:DH, cs].bitcast(F32)), a, pool.last)
                            out += [d, g]
                        bank.used_by(d)
                    w.used_by(m)
                if hp % 2 == 0:
                    wv, v = wv_r.next(), v_r.next()
                    vbuf[hp // 2] = v
                    s = sp.dma(lambda e: e.dma_start(wv.ap[:].rearrange("p n t c j -> p n (t c j)").bitcast(F32),
                                                     scratch[2][hp:hp + 2].rearrange("n p k -> p n k")),
                               sems["wv"], wv.take())
                    pe.wait(s)
                    act.wait(v.take())
                    for n in range(0, NBLK, 2):
                        bank = misc
                        pe.wait(bank.take())
                        for i in range(2):
                            ns = slice((n + i) * P, (n + i + 1) * P)
                            for k, (pw, px, ct) in enumerate(terms):
                                m = pe.do(lambda e, pw=pw, px=px, ct=ct, k=k, ns=ns, i=i, bank=bank: e.matmul(
                                    bank.ap[:, i * 4 * DH:(i + 1) * 4 * DH], px[:, ct, ns], wv.ap[:, :, pw, ct, :],
                                    start=(k == 0), stop=(k == len(terms) - 1)))
                        a = act.do(lambda e, n=n, bank=bank: e.copy(
                            v.ap[:, n:n + 2, :], bank.ap.rearrange("p (i d) -> p i d", i=2)), m)
                        bank.used_by(a)
                        yield
                    wv.used_by(m)
                    out.append(a)
                if hp == NHP - 1:
                    xT.used_by(m)
                ready["qk"] = out

            def maxima(b, hp):
                pe.wait(ready["qk"])
                out = []
                for i, hd in enumerate(heads[hp % 2]):
                    t = hd.ap
                    mc = mcol_r.next()
                    dve.wait(mc.take())
                    for n in range(NBLK):
                        for c in range(n // KPC + 1):
                            w = min(BANK, (n + 1) * P - c * BANK)
                            bank = score_banks.next()
                            m = pe.do(lambda e, t=t, n=n, c=c, w=w, bank=bank: e.matmul(
                                bank.ap[:, 0:w], t["qa"][:, n * P:(n + 1) * P], t["ka"][:, c * BANK:c * BANK + w],
                                start=True, stop=True), bank.take())
                            if c == n // KPC:
                                junk = junk_r.next()
                                dve.wait(junk.take())
                                d = dve.do(lambda e, n=n, c=c, w=w, bank=bank, mc=mc, junk=junk: e.tensor_tensor_reduce(
                                    junk.ap[:, 0:w], bank.ap[:, 0:w], mask[:, BANK - w:BANK], 1.0, NEG, ALU.add, ALU.max,
                                    mc.ap[:, c, n:n + 1]), m)
                                junk.used_by(d)
                            else:
                                d = dve.do(lambda e, n=n, c=c, bank=bank, mc=mc: e.tensor_reduce(
                                    mc.ap[:, c, n:n + 1], bank.ap, AX.X, ALU.max), m)
                            bank.used_by(d)
                            yield
                    d = dve.do(lambda e, mc=mc: e.tensor_tensor(
                        mc.ap[:, 0, KPC:], mc.ap[:, 0, KPC:], mc.ap[:, 1, KPC:], ALU.max), d)
                    m = pe.do(lambda e, mc=mc: e.transpose(misc.ap[0:NBLK, 0:P], mc.ap[:, 0, :], self.ident[:]),
                              misc.take(), d)
                    mc.used_by(m)
                    d = dve.do(lambda e, t=t: e.tensor_tensor(
                        t["qb"][DH:QROWS, :].rearrange("p (a b) -> p a b", b=P),
                        spread(misc.ap[0:NBLK, 0:P], 1, NBLK), pick[:], ALU.mult), m)
                    misc.used_by(d)
                    out.append(d)
                    yield
                ready["max"] = out

            def attend(b, hp, max_ready):
                pair = heads[hp % 2]
                v = vbuf[hp // 2]
                vcol = (hp % 2) * 2 * DH
                pe.wait(max_ready)
                if hp == 0:
                    dve.wait(yT.take())
                for c in range(NC):
                    last = KPC * (c + 1) - 1
                    accs = [acc_r.next(), acc_r.next()]
                    tiles = [(kt, i) for kt in range(last + 1) for i in range(2)]
                    pending = []
                    sums = [None, None]

                    def weigh():
                        kt, i, p, q0, s = pending.pop(0)
                        m = pe.do(lambda e: e.matmul(
                            pv_bank.ap[i * DH:(i + 1) * DH, q0:BANK],
                            v.ap[:, kt, vcol + i * DH:vcol + (i + 1) * DH], p.ap[:, q0:BANK],
                            start=(kt == 0), stop=(kt == last), skip_group_check=True),
                            s, pv_bank.take() if (kt, i) == (0, 0) else None)
                        p.used_by(m)
                        return m
                    for kt, i in tiles:
                        t = pair[i].ap
                        q0 = max(0, kt * P - c * BANK)
                        bank = st_banks.next()
                        qs = slice(c * BANK + q0, (c + 1) * BANK)
                        ks = slice(kt * P, (kt + 1) * P)
                        pe.wait(bank.take())
                        pe.do(lambda e, t=t, ks=ks, qs=qs, q0=q0, bank=bank: e.matmul(
                            bank.ap[:, q0:BANK], t["ka"][:, ks], t["qa"][:, qs], start=True, stop=False))
                        m = pe.do(lambda e, t=t, ks=ks, qs=qs, q0=q0, bank=bank: e.matmul(
                            bank.ap[:, q0:BANK], t["kb"][0:QROWS, ks], t["qb"][0:QROWS, qs], start=False, stop=True))
                        p = p_r.next()
                        s = act.do(lambda e, p=p, q0=q0, bank=bank: e.activation(
                            p.ap[:, q0:BANK], bank.ap[:, q0:BANK], ACT.Exp, scale=scale), m, p.take())
                        bank.used_by(s)
                        if kt >= KPC * c:
                            s = pool.do(lambda e, p=p, q0=q0: e.affine_select(
                                out=p.ap[:, q0:q0 + P], in_=p.ap[:, q0:q0 + P], compare_op=ALU.is_ge, fill=0.0,
                                base=0, pattern=[[1, P]], channel_multiplier=-1), s, pool.last)
                        acc = accs[i]
                        if kt == 0:
                            d = dve.do(lambda e, acc=acc, p=p: e.tensor_copy(acc.ap[:], p.ap[:]), s, acc.take())
                        else:
                            d = dve.do(lambda e, acc=acc, p=p, q0=q0: e.tensor_tensor(
                                acc.ap[:, q0:BANK], acc.ap[:, q0:BANK], p.ap[:, q0:BANK], ALU.add), s, sums[i])
                        sums[i] = d
                        p.used_by(d)
                        pending.append((kt, i, p, q0, s))
                        if len(pending) > 3:
                            weigh()
                        yield
                    while pending:
                        m = weigh()
                    for i in range(2):
                        m = pe.do(lambda e, i=i, acc=accs[i]: e.matmul(
                            den_bank.ap[i * DH:(i + 1) * DH, :], self.ones[:, 0:DH], acc.ap[:], start=True, stop=True),
                            sums[i], den_bank.take() if i == 0 else None)
                        accs[i].used_by(m)
                    rd = rden_r.next()
                    d = dve.do(lambda e, rd=rd: e.reciprocal(rd.ap[:], den_bank.ap), m, rd.take())
                    den_bank.used_by(d)
                    d = dve.do(lambda e, rd=rd, c=c: e.tensor_tensor(
                        yT.ap[:, hp, c * BANK:(c + 1) * BANK], pv_bank.ap, rd.ap[:], ALU.mult), d)
                    rd.used_by(d)
                    pv_bank.used_by(d)
                    yield
                for hd in pair:
                    hd.used_by(m)
                v.used_by(m)
                if hp == NHP - 1:
                    yield from output(b, d)

            def output(b, y_ready):
                rows = slice(b * L, (b + 1) * L)
                s = sp.dma(lambda e: e.dma_start(xres.ap[:], x_dram[rows, :].rearrange("(n p) d -> p n d", p=P)),
                           sems["xr"], xres.take())
                pe.wait(y_ready, wo_ready)
                for n in range(NBLK):
                    bank = den_bank
                    pe.wait(bank.take())
                    for k in range(NHP):
                        m = pe.do(lambda e, n=n, k=k, bank=bank: e.matmul(
                            bank.ap[:, 0:D], yT.ap[:, k, n * P:(n + 1) * P], wo[:, k, :],
                            start=(k == 0), stop=(k == NHP - 1)))
                    d = dve.do(lambda e, n=n, bank=bank: e.tensor_tensor(
                        xres.ap[:, n, :], bank.ap[:, 0:D], xres.ap[:, n, :], ALU.add), m, s)
                    bank.used_by(d)
                    yield
                yT.used_by(m)
                s = sp.dma(lambda e: e.dma_start(out_dram[rows, :].rearrange("(n p) d -> p n d", p=P), xres.ap[:]),
                           sems["xr"], d)
                xres.used_by(s)

            units = [(b, hp) for b in range(B) for hp in range(NHP)]

            def ahead(b, hp):
                yield from project(b, hp)
                yield from maxima(b, hp)
            for _ in ahead(*units[0]):
                pass
            for n, (b, hp) in enumerate(units):
                now = attend(b, hp, ready["max"])
                if n + 1 < len(units):
                    interleave((now, 2), (ahead(*units[n + 1]), 3))
                else:
                    for _ in now:
                        pass
            self.barrier()


PHASES = "AFTF"


def hybrid_kernel(nc, x, w_q, w_k, w_v, w_o, gate_w, w1, w2, out):
    B, L, D = x.shape
    E, _, Fh = w1.shape
    H = w_q.shape[0]
    rows = B * L
    scratch = lambda name, shape, dtype=F32: nc.dram_tensor(name, shape, dtype, kind="Internal").ap()
    n_f = PHASES.count("F")
    with ExitStack() as ctx:
        pr = Program(nc, ctx, dict(x=x.shape, w1=w1.shape, w_q=w_q.shape))
        sems = {n: pr.dma_sem("loaded_" + n) for n in ("x", "xr", "tab", "w1", "w2", "wv", "gate")}
        sems["wqk"] = [pr.dma_sem(f"loaded_wqk{i}") for i in range(2)]
        sems["y"] = [pr.dma_sem(f"stored_y{b}") for b in range(B)]
        sems["xg"] = [pr.dma_sem(f"gathered{i}") for i in range(8)]
        sems["add"] = [[pr.dma_sem(f"added{b}_{h}") for h in range(2)] for b in range(B)]
        a_x = [pr.dma_sem(f"a_x{b}") for b in range(B)]
        a_out = pr.dma_sem("a_out")
        sems["nat"] = [pr.dma_sem(f"loaded_nat{i}") for i in range(3)]
        sems["wT"] = [pr.dma_sem(f"stored_wT{i}") for i in range(3)]
        pr.constants()
        pr.barrier()
        wT = [scratch(n, (H * pr.DH // P, P, 2 * pr.DT * P)) for n in ("wqT", "wkT", "wvT")]
        flat_x, flat_out = x.rearrange("b l d -> (b l) d"), out.rearrange("b l d -> (b l) d")
        res = scratch("res", (rows, D))
        f_round = 0
        if "T" in PHASES:
            with ExitStack() as st:
                pr.transpose_weights(st, (w_q, w_k, w_v), wT, sems)
                pr.barrier()
        for n, phase in enumerate(PHASES):
            if phase == "A":
                pr.stage_a(flat_x, res if "T" in PHASES else flat_out, a_x, a_out)
            elif phase == "F":
                ysc = [scratch(f"ysc{f_round}_{b}", (L, D)) for b in range(B)]
                tabs = [scratch(f"tab{f_round}_{b}", (E, 512)) for b in range(B)]
                f_round += 1
                pr.stage_f(flat_out if ("T" not in PHASES or "T" in PHASES[:n]) else res, gate_w, w1, w2,
                           ysc, tabs, sems)
            else:
                pr.stage_t(res, flat_out, w_o, wT, sems)
        for q in pr.queues:
            q.number()
        block = ctx.enter_context(nc.Block())
        block.tensor(lambda e: pr.pe.play(e))
        block.scalar(lambda e: pr.act.play(e))
        block.vector(lambda e: pr.dve.play(e))
        block.gpsimd(lambda e: pr.pool.play(e))
        block.sync(lambda e: pr.sp.play(e))


NAMES = ["L0_attn_a_x", "L0_attn_b_w_q", "L0_attn_b_w_k", "L0_attn_b_w_v", "L0_attn_b_w_o",
         "L0_ffn_gate_w", "L0_ffn_w1", "L0_ffn_w2"]


def kernel(**inputs):
    import concourse.bacc as bacc
    from concourse.bass_utils import run_bass_kernel_spmd as run

    nc = bacc.Bacc("TRN2", target_bir_lowering=False, num_devices=1)
    arrays = {n: np.ascontiguousarray(inputs[n]) for n in NAMES}
    args = [nc.dram_tensor("in_" + n, a.shape, mybir.dt.from_np(a.dtype), kind="ExternalInput").ap()
            for n, a in arrays.items()]
    out = nc.dram_tensor("out", arrays[NAMES[0]].shape, F32, kind="ExternalOutput").ap()
    hybrid_kernel(nc, *args, out)
    r = run(nc, [{"in_" + n: a for n, a in arrays.items()}], core_ids=[0])
    return r.results[0]["out"]
```

```python
from contextlib import ExitStack

import numpy as np
import concourse.bass as bass
from concourse import mybir

F32 = mybir.dt.float32
F32R = mybir.dt.float32r
BF16 = mybir.dt.bfloat16
I32 = mybir.dt.int32
U32 = mybir.dt.uint32
ALU = mybir.AluOpType
ACT = mybir.ActivationFunctionType
AX = mybir.AxisListType

P = 128
BANK = 512
EPS = 1e-5
NEG = -3.0e38


class Step:

    def __init__(self, queue):
        self.queue, self.needed, self.value = queue, False, None


class Transfer:

    def __init__(self, sem, value):
        self.sem, self.value = sem, value


class DmaSem:

    def __init__(self, sem):
        self.sem, self.count = sem, 0


class Queue:

    def __init__(self, sem):
        self.sem, self.items, self.last = sem, [], None

    def wait(self, *producers):
        for p in producers:
            if p is None:
                continue
            if isinstance(p, (list, tuple)):
                self.wait(*p)
                continue
            if isinstance(p, Step):
                p.needed = True
            self.items.append(("wait", p))

    def do(self, emit, *producers):
        self.wait(*producers)
        step = Step(self)
        self.items.append(("do", emit, step))
        self.last = step
        return step

    def dma(self, emit, sem, *producers):
        self.wait(*producers)
        sem.count += 16
        self.items.append(("dma", emit, sem.sem))
        return Transfer(sem.sem, sem.count)

    def number(self):
        n = 0
        for item in self.items:
            if item[0] == "do" and item[2].needed:
                n += 1
                item[2].value = n

    def play(self, engine):
        seen = {}
        for item in self.items:
            if item[0] == "wait":
                p = item[1]
                sem = p.queue.sem if isinstance(p, Step) else p.sem
                if seen.get(id(sem), 0) < p.value:
                    engine.wait_ge(sem, p.value)
                    seen[id(sem)] = p.value
            elif item[0] == "dma":
                item[1](engine).then_inc(item[2], 16)
            else:
                instruction = item[1](engine)
                if item[2].needed:
                    instruction.then_inc(self.sem, 1)


class Buffer:

    def __init__(self, ap):
        self.ap, self.users = ap, []

    def take(self):
        users, self.users = self.users, []
        return users

    def used_by(self, *steps):
        self.users += steps


class Ring:

    def __init__(self, buffers):
        self.buffers, self.n = list(buffers), 0

    def next(self):
        b = self.buffers[self.n % len(self.buffers)]
        self.n += 1
        return b


def spread(ap, axis, n):
    ap = ap.unsqueeze(axis)
    shape = list(ap.shape)
    shape[axis] = n
    return ap.to_broadcast(shape)


def interleave(*streams):
    live = [[g, w] for g, w in streams]
    while live:
        for s in list(live):
            for _ in range(s[1]):
                try:
                    next(s[0])
                except StopIteration:
                    live.remove(s)
                    break


class Program:
    def __init__(self, nc, ctx, shapes):
        self.nc, self.ctx = nc, ctx
        self.B, self.L, self.D = shapes["x"]
        self.E, self.F = shapes["w1"][0], shapes["w1"][2]
        self.H, self.DH = shapes["w_q"][0], shapes["w_q"][1]
        self.CAP = 2 * self.L // self.E
        self.NBLK = self.L // P
        self.DT = self.D // P
        self.FT = self.F // P
        self.n_names = 0
        self.pe = Queue(self.semaphore("pe_done"))
        self.act = Queue(self.semaphore("act_done"))
        self.dve = Queue(self.semaphore("dve_done"))
        self.pool = Queue(self.semaphore("pool_done"))
        self.sp = Queue(self.semaphore("sp_done"))
        self.queues = [self.pe, self.act, self.dve, self.pool, self.sp]
        self.dma_sems = []
        self.psum_all = psum = self.psum("psum", [P, 8 * BANK])
        self.banks = [Buffer(psum[:, i * BANK:(i + 1) * BANK]) for i in range(8)]

    def semaphore(self, name):
        return self.ctx.enter_context(self.nc.semaphore(name))

    def dma_sem(self, name):
        s = DmaSem(self.semaphore(name))
        self.dma_sems.append(s)
        return s

    def sbuf(self, stack, name, shape, dtype=F32):
        self.n_names += 1
        return stack.enter_context(self.nc.sbuf_tensor(f"{name}_{self.n_names}", shape, dtype))

    def psum(self, name, shape):
        return self.ctx.enter_context(self.nc.psum_tensor(name, shape, F32))

    def barrier(self):
        last = [q.last for q in self.queues if q.last is not None]
        moved = [Transfer(s.sem, s.count) for s in self.dma_sems if s.count]
        for q in self.queues:
            q.wait(*last, *moved)

    def constants(self):
        pool, dve = self.pool, self.dve
        c = lambda name, shape, dtype=F32: self.sbuf(self.ctx, name, shape, dtype)
        self.ident = c("ident", [P, P])
        self.ident_b = c("ident_b", [P, P], BF16)
        self.ones = c("ones", [P, P])
        self.ones_b = c("ones_b", [P, P], BF16)
        self.upto_b = c("upto_b", [P, P], BF16)
        self.same_f = c("same_f", [P, self.E])
        self.same_b = c("same_b", [P, P], BF16)
        self.minus_half = c("minus_half", [P, self.NBLK])
        NP_ = self.NPASS = 8
        self.SHIFTS = [26, 22, 18, 14, 10, 6, 2, 0]
        self.digit = c("digit", [P, NP_], I32)
        lane = c("lane", [P, 1], I32)
        self.tokid = c("tokid", [P, self.NBLK])
        tok_i = c("tok_i", [P, self.NBLK], I32)
        self.iota16 = c("iota16", [P, 16])
        iota_i = c("iota_i", [P, 16], I32)
        self.zero_i = c("zero_i", [P, 1], I32)
        m = [pool.do(lambda e, t=t, v=v: e.memset(t[:], v))
             for t, v in ((self.ident, 0.0), (self.ident_b, 0.0), (self.ones, 1.0), (self.ones_b, 1.0),
                          (self.minus_half, -0.5))]
        pool.wait(m[-1])
        eye = dict(compare_op=ALU.not_equal, fill=1.0, base=0, pattern=[[-1, P]], channel_multiplier=1)
        pool.do(lambda e: e.affine_select(out=self.ident[:], in_=self.ident[:], **eye))
        pool.do(lambda e: e.affine_select(out=self.ident_b[:], in_=self.ident_b[:], **eye))
        pool.do(lambda e: e.affine_select(out=self.upto_b[:], in_=self.ones_b[:], compare_op=ALU.is_ge, fill=0.0,
                                          base=0, pattern=[[1, P]], channel_multiplier=-1))

        def same(out, in_, q, n):
            a = pool.do(lambda e: e.affine_select(out=out, in_=in_, compare_op=ALU.is_ge, fill=0.0, base=0,
                                                  pattern=[[-16, q]] + n, channel_multiplier=1))
            pool.do(lambda e: e.affine_select(out=out, in_=out, compare_op=ALU.is_ge, fill=0.0, base=15,
                                              pattern=[[16, q]] + [[-s, k] for s, k in n],
                                              channel_multiplier=-1), a)
        same(self.same_f[:], self.ones[:, 0:self.E], self.E, [])
        v = lambda t: t[:].rearrange("p (e j) -> p e j", j=16)
        same(v(self.same_b), v(self.ones_b), self.E, [[0, 16]])
        pool.do(lambda e: e.iota(lane[:], pattern=[[0, 1]], base=0, channel_multiplier=1))
        pool.do(lambda e: e.iota(tok_i[:], pattern=[[P, self.NBLK]], base=0, channel_multiplier=1))
        made = pool.do(lambda e: e.iota(iota_i[:], pattern=[[1, 16]], base=0, channel_multiplier=0))
        dve.do(lambda e: e.tensor_copy(self.tokid[:], tok_i[:]), made)
        dve.do(lambda e: e.tensor_copy(self.iota16[:], iota_i[:]))
        dve.do(lambda e: e.memset(self.zero_i[:], 0))
        for n, s in enumerate(self.SHIFTS):
            keep = 3 if s == 0 else 15
            dve.do(lambda e, n=n, s=s, k=keep: e.tensor_scalar(
                self.digit[:, n:n + 1], lane[:], k, s, ALU.bitwise_and, ALU.logical_shift_left))

    def layer_norm(self, x, y, stats, mv, rstd, nb, *ready):
        dve, pool = self.dve, self.pool
        dve.wait(*ready)
        for i in range(nb):
            s = dve.do(lambda e, i=i: e.bn_stats(stats[:, i, :], x[:, i, :]))
        for i in range(nb):
            s2 = dve.do(lambda e, i=i: e.bn_aggr(mv[:, i, :], stats[:, i, :]), s)
        s = dve.do(lambda e: e.tensor_scalar(rstd[:, 0:nb], mv[:, 0:nb, 1], EPS, None, ALU.add), s2)
        s = pool.do(lambda e: e.tensor_tensor(rstd[:, 0:nb], rstd[:, 0:nb], self.minus_half[:, 0:nb], ALU.pow), s)
        out = []
        for i in range(nb):
            out.append(dve.do(lambda e, i=i: e.tensor_scalar(y[:, i, :], x[:, i, :], mv[:, i, 0:1], rstd[:, i:i + 1],
                                                             ALU.subtract, ALU.mult), s))
        return out

    def stage_a(self, x_dram, out_dram, x_sem, out_sem):
        pe, act, dve, pool, sp = self.queues
        B, NBLK, D, DK = self.B, self.NBLK, self.D, 16
        H = D // DK
        half = BANK // D
        with ExitStack() as st:
            x = self.sbuf(st, "a_x", [P, B, NBLK, D])
            y = self.sbuf(st, "a_y", [P, NBLK, B, D])
            mix = self.sbuf(st, "a_mix", [P, NBLK, self.L])
            ang = [Buffer(self.sbuf(st, "a_ang", [P, self.L])) for _ in range(2)]
            stats = self.sbuf(st, "a_stats", [P, B, NBLK, 6])
            mv = self.sbuf(st, "a_mv", [P, B, NBLK, 2])
            rstd = self.sbuf(st, "a_rstd", [P, B, NBLK])
            msum = self.sbuf(st, "a_msum", [P, NBLK, DK])
            mT = self.sbuf(st, "a_mT", [DK, self.L])
            den = self.sbuf(st, "a_den", [P, NBLK])
            rden = self.sbuf(st, "a_rden", [P, NBLK])
            loads = []
            for b in range(B):
                loads.append(sp.dma(lambda e, b=b: e.dma_start(
                    x[:, b], x_dram[b * self.L:(b + 1) * self.L, :].rearrange("(n p) d -> p n d", p=P)), x_sem[b % 4]))
            norm = []
            for b in range(B):
                norm += self.layer_norm(x[:, b], y[:, :, b, :], stats[:, b], mv[:, b], rstd[:, b], NBLK, loads[b])
            sums = []
            for n in range(NBLK):
                s = dve.do(lambda e, n=n: e.tensor_reduce(
                    msum[:, n, :], y[:, n].rearrange("p b (h k) -> p k b h", k=DK), AX.XY, ALU.add), norm)
                sums.append(dve.do(lambda e, n=n: e.tensor_scalar(msum[:, n, :], msum[:, n, :], 1.0 / (B * H), None,
                                                                  ALU.mult), s))
            for c in range(2):
                bank = self.banks[c]
                pe.wait(bank.take())
                for n in range(4 * c, 4 * c + 4):
                    t = pe.do(lambda e, n=n, bank=bank: e.transpose(
                        bank.ap[0:DK, (n % 4) * P:(n % 4 + 1) * P], msum[:, n, :], self.ident[:]),
                        sums[n], pool.last if n == 0 else None)
                s = act.do(lambda e, c=c, bank=bank: e.copy(mT[:, c * BANK:(c + 1) * BANK], bank.ap[0:DK, :]), t)
                bank.used_by(s)
            mt_ready = s
            exps = []
            ring = Ring(self.banks[2:6])
            for n in range(NBLK):
                a = ang[n % 2]
                for c in range(2):
                    bank = ring.next()
                    t = pe.do(lambda e, n=n, c=c, bank=bank: e.matmul(
                        bank.ap, mT[:, n * P:(n + 1) * P], mT[:, c * BANK:(c + 1) * BANK], start=True, stop=True),
                        mt_ready, bank.take())
                    s = dve.do(lambda e, a=a, c=c, bank=bank: e.tensor_scalar(
                        a.ap[:, c * BANK:(c + 1) * BANK], bank.ap, float(np.pi), float(-np.pi), ALU.min, ALU.max),
                        t, a.take() if c == 0 else None)
                    bank.used_by(s)
                s = act.do(lambda e, a=a: e.activation(a.ap[:], a.ap[:], ACT.Sin, scale=0.5), s)
                s = pool.do(lambda e, a=a, n=n: e.tensor_tensor(mix[:, n, :], a.ap[:], a.ap[:], ALU.mult), s)
                a.used_by(s)
                exps.append(s)
            done = []
            for n in range(NBLK):
                s = act.do(lambda e, n=n: e.activation(mix[:, n, :], mix[:, n, :], ACT.Exp,
                                                       accum_out=den[:, n:n + 1]), exps[n])
                done.append(s)
            s = dve.do(lambda e: e.reciprocal(rden[:], den[:]), done[-1])
            pe.wait(done[-1], norm[-1])
            ring = Ring(self.banks)
            for i in range(NBLK):
                for c in range(B // half):
                    bank = ring.next()
                    pe.wait(bank.take())
                    for j in range(NBLK):
                        t = pe.do(lambda e, i=i, j=j, c=c, bank=bank: e.matmul(
                            bank.ap, mix[:, j, i * P:(i + 1) * P],
                            y[:, j, c * half:(c + 1) * half, :].rearrange("p b d -> p (b d)"),
                            start=(j == 0), stop=(j == NBLK - 1)))
                    v = bank.ap.rearrange("p (b d) -> p b d", b=half)
                    xs = x[:, c * half:(c + 1) * half, i, :]
                    t = dve.do(lambda e, v=v, xs=xs, i=i: e.scalar_tensor_tensor(
                        out=xs, in0=v, scalar=rden[:, i:i + 1], in1=xs, op0=ALU.mult, op1=ALU.add), t, s)
                    bank.used_by(t)
                    for b in range(c * half, (c + 1) * half):
                        r0 = b * self.L + i * P
                        sp.dma(lambda e, b=b, i=i, r0=r0: e.dma_start(out_dram[r0:r0 + P, :], x[:, b, i, :]),
                               out_sem, t)
            self.barrier()

    def stage_f_tiles(self, st):
        t = {}
        sb = lambda n, s, d=F32: self.sbuf(st, n, s, d)
        B, NBLK, D, E = self.B, self.NBLK, self.D, self.E
        t["x"] = Ring([Buffer(sb("f_x", [P, NBLK, D]))])
        t["y"] = Ring([Buffer(sb("f_y", [P, NBLK, D]))])
        t["yT"] = Ring([Buffer(sb("f_yT", [P, self.DT, self.L]))])
        t["stats"] = sb("f_stats", [P, NBLK, 6])
        t["mv"] = sb("f_mv", [P, NBLK, 2])
        t["rstd"] = sb("f_rstd", [P, NBLK])
        for n in ("scd", "ex", "pr"):
            t[n] = sb("f_" + n, [P, NBLK, E])
        for n in ("mx", "sm"):
            t[n] = sb("f_" + n, [P, NBLK])
        t["wide"] = sb("f_wide", [P, NBLK, E, 16])
        t["pT"] = sb("f_pT", [P, self.L])
        t["junk"] = sb("f_junk", [P, self.L], BF16)
        t["cnt"] = sb("f_cnt", [P, 1])
        t["ind"] = sb("f_ind", [P, 1], BF16)
        t["bits"] = sb("f_bits", [P, 1], I32)
        t["prefix"] = sb("f_prefix", [P, 1], I32)
        t["thr"] = sb("f_thr", [P, 1], I32)
        t["Tfull"] = sb("f_Tfull", [P, P])
        t["Tb"] = sb("f_Tb", [P, E])
        t["ge"] = sb("f_ge", [P, 2, NBLK, E], BF16)
        t["need"] = sb("f_need", [P, E])
        for n in ("m1", "sel", "pos"):
            t[n] = sb("f_" + n, [P, NBLK, E])
        for n in ("key", "hi4", "lo4"):
            t[n] = sb("f_" + n, [P, NBLK, E], I32)
        t["A"] = sb("f_A", [P, NBLK, E, 16])
        t["C"] = sb("f_C", [P, NBLK, E, 16, 2])
        t["Rw"] = sb("f_Rw", [P, E, 32])
        t["R"] = sb("f_R", [P, 32])
        t["tab"] = [sb("f_tab", [P, E, 2, 2]) for _ in range(B)]
        t["idx"] = [sb("f_idx", [P, E, 2], U32) for _ in range(B)]
        t["row"] = [sb("f_row", [P, E, 2], U32) for _ in range(B)]
        t["wst"] = Buffer(sb("f_wst", [P, 2, self.DT * self.F]))
        t["whi"] = [Buffer(sb("f_whi", [P, 2, self.DT * self.F], F32R)) for _ in range(2)]
        t["wlo"] = [Buffer(sb("f_wlo", [P, 2, self.DT * self.F], F32R)) for _ in range(2)]
        t["xg"] = Ring([Buffer(sb("f_xg", [P, D])) for _ in range(8)])
        t["xin"] = Ring([Buffer((sb("f_xhi", [P, self.DT, BANK], F32R), sb("f_xlo", [P, self.DT, BANK], F32R)))
                         for _ in range(1)])
        t["h"] = Ring([Buffer(sb("f_h", [P, BANK])) for _ in range(2)])
        t["hs"] = [Buffer((sb("f_hhi", [P, BANK], F32R), sb("f_hlo", [P, BANK], F32R))) for _ in range(self.FT)]
        t["yo"] = Ring([Buffer(sb("f_yo", [P, D])) for _ in range(4)])
        return t

    def route(self, b, t, res_dram, ysc, tabs, gateT, sems):
        pe, act, dve, pool, sp = self.queues
        NBLK, D, E, DT, L = self.NBLK, self.D, self.E, self.DT, self.L
        ring = self.route_banks
        xb, yb, yTb = t["x"].next(), t["y"].next(), t["yT"].next()
        rows = slice(b * L, (b + 1) * L)
        s = sp.dma(lambda e: e.dma_start(xb.ap[:], res_dram[rows, :].rearrange("(n p) d -> p n d", p=P)),
                   sems["x"], xb.take())
        dve.wait(yb.take())
        norm = self.layer_norm(xb.ap, yb.ap, t["stats"], t["mv"], t["rstd"], NBLK, s, self.rstd_user)
        self.rstd_user = norm[-1]
        xb.used_by(norm[-1])
        s = sp.dma(lambda e: e.dma_start(ysc[b].rearrange("(n p) d -> p n d", p=P), yb.ap[:]),
                   sems["y"][b], norm[-1])
        yb.used_by(s)
        self.y_written[b] = s
        yield
        act.wait(yTb.take())
        for dt in range(DT):
            for c in range(2):
                bank = ring.next()
                pe.wait(bank.take())
                for n in range(4 * c, 4 * c + 4):
                    s = pe.do(lambda e, n=n, bank=bank, dt=dt: e.transpose(
                        bank.ap[:, (n % 4) * P:(n % 4 + 1) * P], yb.ap[:, n, dt * P:(dt + 1) * P], self.ident[:]),
                        norm[-1])
                ev = act.do(lambda e, c=c, bank=bank, dt=dt: e.copy(
                    yTb.ap[:, dt, c * BANK:(c + 1) * BANK], bank.ap), s)
                bank.used_by(ev)
                yield
        yb.used_by(s)
        bank = ring.next()
        pe.wait(bank.take(), ev)
        for n in range(NBLK):
            for dt in range(DT):
                s = pe.do(lambda e, n=n, dt=dt, bank=bank: e.matmul(
                    bank.ap[:, n * E:(n + 1) * E], yTb.ap[:, dt, n * P:(n + 1) * P], gateT[:, dt, :],
                    start=(dt == 0), stop=(dt == DT - 1)))
        yTb.used_by(s)
        sc = bank.ap[:, 0:NBLK * E].rearrange("p (n e) -> p n e", e=E)
        s = dve.do(lambda e: e.tensor_reduce(t["mx"][:], sc, AX.X, ALU.max), s)
        s = dve.do(lambda e: e.tensor_tensor(t["scd"][:], sc, spread(t["mx"][:], 2, E), ALU.subtract), s)
        bank.used_by(s)
        yield
        s = act.do(lambda e: e.activation(t["ex"][:], t["scd"][:], ACT.Exp), s)
        s = dve.do(lambda e: e.tensor_reduce(t["sm"][:], t["ex"][:], AX.X, ALU.add), s)
        s = dve.do(lambda e: e.reciprocal(t["sm"][:], t["sm"][:]), s)
        s = dve.do(lambda e: e.tensor_tensor(t["pr"][:], t["ex"][:], spread(t["sm"][:], 2, E), ALU.mult), s)
        s = dve.do(lambda e: e.tensor_copy(t["wide"][:], spread(t["pr"][:], 3, 16)), s)
        yield
        for c in range(2):
            bank = ring.next()
            pe.wait(bank.take(), s)
            for n in range(4 * c, 4 * c + 4):
                m = pe.do(lambda e, n=n, bank=bank: e.transpose(
                    bank.ap[:, (n % 4) * P:(n % 4 + 1) * P],
                    t["wide"][:, n].rearrange("p e j -> p (e j)"), self.ident[:]))
            ev = act.do(lambda e, c=c, bank=bank: e.copy(t["pT"][:, c * BANK:(c + 1) * BANK], bank.ap), m)
            bank.used_by(ev)
        yield
        prefix, thr = self.zero_i, self.digit[:, 0:1]
        for n, shift in enumerate(self.SHIFTS):
            s = dve.do(lambda e, thr=thr: e.tensor_scalar(
                t["junk"][:], t["pT"][:], thr.bitcast(F32), 0.0, ALU.is_ge, ALU.add, accum_out=t["cnt"][:]), ev, s)
            s = dve.do(lambda e: e.tensor_scalar(t["ind"][:], t["cnt"][:], self.CAP - 0.5, None, ALU.is_ge), s)
            bank = ring.next()
            s = pe.do(lambda e, bank=bank: e.matmul(bank.ap[:, 0:1], self.same_b[:], t["ind"][:],
                                                    start=True, stop=True), s, bank.take())
            copies = 4 if shift == 0 else 1
            s = dve.do(lambda e, bank=bank, a=float(1 << shift) / copies, c=-float(1 << shift): e.tensor_scalar(
                t["bits"][:], bank.ap[:, 0:1], a, c, ALU.mult, ALU.add), s)
            bank.used_by(s)
            s = dve.do(lambda e, p=prefix: e.tensor_tensor(t["prefix"][:], p[:], t["bits"][:], ALU.bitwise_or), s)
            prefix = t["prefix"]
            if n + 1 < len(self.SHIFTS):
                s = dve.do(lambda e, n=n: e.tensor_tensor(t["thr"][:], prefix[:], self.digit[:, n + 1:n + 2],
                                                          ALU.bitwise_or), s)
                thr = t["thr"][:, 0:1]
            yield
        s = dve.do(lambda e: e.tensor_copy(t["Tfull"][:], prefix[:].bitcast(F32).to_broadcast([P, P])), s)
        bank = ring.next()
        s = pe.do(lambda e, bank=bank: e.transpose(bank.ap[:, 0:P], t["Tfull"][:], self.ident[:]), s, bank.take())
        s = dve.do(lambda e, bank=bank: e.tensor_copy(
            t["Tb"][:], bank.ap[:, 0:P].rearrange("p (e j) -> p e j", j=16)[:, :, 0]), s)
        bank.used_by(s)
        Tb = spread(t["Tb"][:], 1, NBLK)
        g1 = dve.do(lambda e: e.tensor_tensor(t["ge"][:, 0], t["pr"][:], Tb, ALU.is_gt), s)
        s = dve.do(lambda e: e.tensor_tensor(t["ge"][:, 1], t["pr"][:], Tb, ALU.is_equal), s)
        yield
        cb, tb_ = ring.next(), ring.next()
        cu = cb.ap[:, 0:2 * NBLK * E].rearrange("p (g n e) -> p g n e", g=2, e=E)
        tot = tb_.ap[:, 0:E]
        pe.wait(cb.take(), tb_.take(), s)
        pe.do(lambda e: e.matmul(cb.ap[:, 0:2 * NBLK * E], self.upto_b[:],
                                 t["ge"][:].rearrange("p g n e -> p (g n e)"),
                                 start=True, stop=False, skip_group_check=True))
        for n in range(NBLK - 1):
            for g in range(2):
                pe.do(lambda e, n=n, g=g: e.matmul(
                    cu[:, g, n + 1:, :], self.ones_b[:], spread(t["ge"][:, g, n, :], 1, NBLK - 1 - n),
                    start=False, stop=(n == NBLK - 2 and g == 1), skip_group_check=True))
        for n in range(NBLK):
            s = pe.do(lambda e, n=n: e.matmul(tot, self.ones_b[:], t["ge"][:, 0, n, :],
                                              start=(n == 0), stop=(n == NBLK - 1)))
        yield
        s = dve.do(lambda e: e.tensor_scalar(t["need"][:], tot, -1.0, float(self.CAP), ALU.mult, ALU.add), s)
        tb_.used_by(s)
        need = spread(t["need"][:], 1, NBLK)
        s = dve.do(lambda e: e.tensor_tensor(t["m1"][:], cu[:, 1], need, ALU.is_le), s)
        s2 = dve.do(lambda e: e.tensor_tensor(t["pos"][:], cu[:, 1], need, ALU.min), s)
        s = dve.do(lambda e: e.tensor_tensor(t["sel"][:], t["m1"][:], t["ge"][:, 1], ALU.mult), s)
        s2 = dve.do(lambda e: e.tensor_tensor(t["pos"][:], cu[:, 0], t["pos"][:], ALU.add), s2)
        cb.used_by(s2)
        s = dve.do(lambda e: e.tensor_tensor(t["sel"][:], t["sel"][:], t["ge"][:, 0], ALU.add), s)
        s = dve.do(lambda e: e.tensor_tensor(t["pos"][:], t["pos"][:], t["sel"][:], ALU.mult), s, s2)
        s = dve.do(lambda e: e.tensor_scalar(t["key"][:], t["pos"][:], -1.0, None, ALU.add), s)
        dve.do(lambda e: e.tensor_scalar(t["hi4"][:], t["key"][:], 4, None, ALU.arith_shift_right), s)
        s = dve.do(lambda e: e.tensor_scalar(t["lo4"][:], t["key"][:], 15, None, ALU.bitwise_and), s)
        yield
        i16 = spread(spread(self.iota16[:], 1, E), 1, NBLK)
        s1 = dve.do(lambda e: e.tensor_tensor(t["A"][:], spread(t["hi4"][:], 3, 16), i16, ALU.is_equal), s)
        s = dve.do(lambda e: e.tensor_tensor(t["C"][:, :, :, :, 0], spread(t["lo4"][:], 3, 16), i16, ALU.is_equal), s)
        s2 = pool.do(lambda e: e.tensor_tensor(t["C"][:, :, :, :, 1], t["C"][:, :, :, :, 0],
                                               spread(t["pr"][:], 3, 16), ALU.mult), s)
        s = dve.do(lambda e: e.tensor_tensor(t["C"][:, :, :, :, 0], t["C"][:, :, :, :, 0],
                                             spread(spread(self.tokid[:], 2, E), 3, 16), ALU.mult), s2)
        yield
        bank = ring.next()
        pe.wait(bank.take(), s, s1, s2)
        for n in range(NBLK):
            m = pe.do(lambda e, n=n, bank=bank: e.matmul(
                bank.ap[:, 0:E * 32], t["A"][:, n].rearrange("p e a -> p (e a)"),
                t["C"][:, n].rearrange("p e c t -> p (e c t)"), start=(n == 0), stop=(n == NBLK - 1)))
        s = dve.do(lambda e, bank=bank: e.tensor_tensor(
            t["Rw"][:], bank.ap[:, 0:E * 32].rearrange("p (e k) -> p e k", e=E),
            spread(self.same_f[:], 2, 32), ALU.mult), m)
        bank.used_by(s)
        s = dve.do(lambda e: e.tensor_reduce(t["R"][:], t["Rw"][:].rearrange("p e k -> p k e"), AX.X, ALU.add),
                   s, self.r_user)
        s = sp.dma(lambda e: e.dma_start(tabs[b].rearrange("e (a k) -> (e a) k", a=16), t["R"][:]), sems["tab"], s)
        self.r_user = s
        tab, idx = t["tab"][b], t["idx"][b]
        s = sp.dma(lambda e: e.dma_start(
            tab[:].rearrange("p e h t -> p e (h t)"), tabs[b].rearrange("e (q k) -> q e k", k=4)),
            sems["tab"], s)
        yield
        dve.do(lambda e: e.tensor_copy(idx[:], tab[:, :, :, 0]), s)
        s = dve.do(lambda e: e.tensor_scalar(t["row"][b][:], tab[:, :, :, 0], float(b * L), None, ALU.add))
        self.idx_ready[b] = s
        yield

    def load_expert(self, e_, t, w1, w2, sems):
        pe, act, dve, pool, sp = self.queues
        D, Fh, DT, FT = self.D, self.F, self.DT, self.FT
        n = self.loaded
        self.loaded += 1
        stg, hi, lo = t["wst"], t["whi"][n % 2], t["wlo"][n % 2]
        users = stg.take()
        a = sp.dma(lambda e: e.dma_start(stg.ap[:, 0].rearrange("p (k f) -> p k f", k=DT),
                                         w1[e_].rearrange("(k p) f -> p k f", p=P)), sems["w1"], users)
        c = sp.dma(lambda e: e.dma_start(stg.ap[:, 1].rearrange("p (k d) -> p k d", k=FT),
                                         w2[e_].rearrange("(k p) d -> p k d", p=P)), sems["w2"], users)
        act.wait(hi.take())
        pool.wait(lo.take())
        steps = []
        for i, ready in ((0, a), (1, c)):
            for h in range(2):
                k = slice(h * DT * Fh // 2, (h + 1) * DT * Fh // 2)
                s = act.do(lambda e, i=i, k=k: e.copy(hi.ap[:, i, k], stg.ap[:, i, k]), ready)
                s = pool.do(lambda e, i=i, k=k: e.tensor_tensor(lo.ap[:, i, k], stg.ap[:, i, k],
                                                                hi.ap[:, i, k].bitcast(F32), ALU.subtract), s)
                stg.used_by(s)
                steps.append(s)
                yield
        self.weights[n] = (hi, lo, steps)

    def experts(self, pair, t, w1, w2, ysc, res_dram, sems):
        pe, act, dve, pool, sp = self.queues
        D, DT, FT, E = self.D, self.DT, self.FT, self.E
        x0, x1 = self.banks[0], self.banks[1]
        up = Ring(self.banks[2:4])
        down = self.banks[4:6]

        def gather(e_):
            tiles = []
            for b in pair:
                for h in range(2):
                    g = t["xg"].next()
                    s = pool.dma(lambda e, g=g, b=b, h=h: e.indirect_dma_start(
                        out=g.ap[:], out_offset=None, in_=ysc[b],
                        in_offset=bass.IndirectOffsetOnAxis(ap=t["idx"][b][:, e_, h:h + 1], axis=0)),
                        sems["xg"][(t["xg"].n - 1) % 8], g.take(), self.idx_ready[b], self.y_written[b])
                    tiles.append((g, s))
            return tiles

        def xin(tiles):
            buf = t["xin"].next()
            hi, lo = buf.ap
            pe.wait(x0.take(), x1.take())
            for k, (g, s) in enumerate(tiles):
                pe.wait(s)
                for dt, bank in enumerate((x0, x1)):
                    m = pe.do(lambda e, k=k, g=g, dt=dt, bank=bank: e.transpose(
                        bank.ap[:, k * P:(k + 1) * P], g.ap[:, dt * P:(dt + 1) * P], self.ident[:]))
                g.used_by(m)
            out = []
            act.wait(buf.take())
            for dt, bank in enumerate((x0, x1)):
                a = act.do(lambda e, dt=dt, bank=bank: e.copy(hi[:, dt, :], bank.ap), m)
                c = dve.do(lambda e, dt=dt, bank=bank: e.tensor_tensor(lo[:, dt, :], bank.ap,
                                                                       hi[:, dt, :].bitcast(F32), ALU.subtract), a)
                bank.used_by(c)
                out.append(c)
            return buf, hi, lo, out

        buf, xhi, xlo, xready = xin(gather(0))
        yield
        for e_ in range(E):
            tiles = gather(e_ + 1) if e_ + 1 < E else None
            while self.used not in self.weights:
                next(self.weights_ahead)
            whi, wlo, wready = self.weights[self.used]
            self.used += 1
            pe.wait(xready, wready)
            w1h = whi.ap[:, 0].rearrange("p (k f) -> p k f", k=DT)
            w1l = wlo.ap[:, 0].rearrange("p (k f) -> p k f", k=DT)
            w2h = whi.ap[:, 1].rearrange("p (k d) -> p k d", k=FT)
            w2l = wlo.ap[:, 1].rearrange("p (k d) -> p k d", k=FT)
            hready = []
            for f in range(FT):
                bank = up.next()
                pe.wait(bank.take())
                fs = slice(f * P, (f + 1) * P)
                terms = [(w, x, dt) for dt in range(DT) for w, x in ((w1h, xhi), (w1h, xlo), (w1l, xhi))]
                for k, (w, x, dt) in enumerate(terms):
                    m = pe.do(lambda e, w=w, x=x, dt=dt, fs=fs, bank=bank, k=k: e.matmul(
                        bank.ap, w[:, dt, fs], x[:, dt, :], start=(k == 0), stop=(k == len(terms) - 1)))
                hb, parts = t["h"].next(), t["hs"][f]
                hhi, hlo = parts.ap
                a = act.do(lambda e, hb=hb, bank=bank: e.activation(hb.ap[:], bank.ap, ACT.Gelu), m, hb.take())
                bank.used_by(a)
                c = dve.do(lambda e, hb=hb, hhi=hhi: e.tensor_copy(hhi[:], hb.ap[:]), a, parts.take())
                c = dve.do(lambda e, hb=hb, hhi=hhi, hlo=hlo: e.tensor_tensor(
                    hlo[:], hb.ap[:], hhi[:].bitcast(F32), ALU.subtract), c)
                hb.used_by(c)
                hready.append(c)
                yield
            buf.used_by(m)
            if tiles:
                buf, xhi, xlo, xready = xin(tiles)
            for bank in down:
                pe.wait(bank.take())
            for f in range(FT):
                pe.wait(hready[f])
                hhi, hlo = t["hs"][f].ap
                for k in range(4):
                    bank = down[k // 2]
                    ks = slice(k * P, (k + 1) * P)
                    out = bank.ap[:, (k % 2) * D:(k % 2 + 1) * D]
                    for j, (h, w) in enumerate(((hhi, w2h), (hhi, w2l), (hlo, w2h))):
                        m = pe.do(lambda e, h=h, w=w, ks=ks, out=out, f=f, j=j, k=k: e.matmul(
                            out, h[:, ks], w[:, f, :], start=(f == 0 and j == 0 and k % 2 == 0),
                            stop=(f == FT - 1 and j == 2), skip_group_check=True))
                t["hs"][f].used_by(m)
                if f % 2:
                    yield
            whi.used_by(m)
            wlo.used_by(m)
            self.through += 1
            for k in range(4):
                b, h = pair[k // 2], k % 2
                bank = down[k // 2]
                yo = t["yo"].next()
                s = act.do(lambda e, yo=yo, bank=bank, h=h, b=b, e_=e_: e.mul(
                    yo.ap[:], bank.ap[:, h * D:(h + 1) * D], t["tab"][b][:, e_, h, 1:2]), m, yo.take())
                bank.used_by(s)
                s = pool.dma(lambda e, yo=yo, b=b, h=h, e_=e_: e.indirect_dma_start(
                    out=res_dram[:, :], out_offset=bass.IndirectOffsetOnAxis(ap=t["row"][b][:, e_, h:h + 1], axis=0),
                    in_=yo.ap[:], in_offset=None, compute_op=ALU.add),
                    sems["add"][b][h], s, self.added[b])
                yo.used_by(s)
                self.adding[b].append(s)
                if h == 1:
                    self.added[b], self.adding[b] = self.adding[b], []
            yield

    def stage_f(self, res_dram, gate_w, w1, w2, ysc, tabs, sems):
        pe, act, dve, pool, sp = self.queues
        with ExitStack() as st:
            t = self.stage_f_tiles(st)
            self.route_banks = Ring(self.banks[6:8])
            self.y_written, self.idx_ready = {}, {}
            self.added = {b: [] for b in range(self.B)}
            self.adding = {b: [] for b in range(self.B)}
            self.rstd_user = self.r_user = None
            self.loaded = self.used = self.through = 0
            self.weights = {}
            gate = self.sbuf(st, "f_gate", [self.E, self.D])
            gateT = self.sbuf(st, "f_gateT", [P, self.DT, self.E])
            s = sp.dma(lambda e: e.dma_start(gate[:], gate_w), sems["gate"])
            bank = self.route_banks.next()
            pe.wait(bank.take(), s, pool.last)
            for dt in range(self.DT):
                m = pe.do(lambda e, dt=dt: e.transpose(bank.ap[:, dt * self.E:(dt + 1) * self.E],
                                                       gate[:, dt * P:(dt + 1) * P], self.ident[0:self.E, 0:self.E]))
            s = dve.do(lambda e: e.tensor_copy(gateT[:], bank.ap[:, 0:self.DT * self.E].rearrange(
                "p (k e) -> p k e", e=self.E)), m)
            bank.used_by(s)
            pe.wait(s)
            route = lambda b: self.route(b, t, res_dram, ysc, tabs, gateT, sems)
            n_pairs = self.B // 2
            order = [e_ for _ in range(n_pairs) for e_ in range(self.E)]

            def prefetch():
                for k, e_ in enumerate(order[2:]):
                    while self.through <= k:
                        yield
                    yield from self.load_expert(e_, t, w1, w2, sems)

            def chain(*gens):
                for g in gens:
                    yield from g
            ahead = chain(*(self.load_expert(e_, t, w1, w2, sems) for e_ in order[:2]))
            interleave((chain(route(0), route(1)), 1), (ahead, 1))
            later = chain(*(route(b) for b in range(2, self.B)))
            self.weights_ahead = prefetch()
            pairs = [(2 * k, 2 * k + 1) for k in range(n_pairs)]

            def work():
                for k, pair in enumerate(pairs):
                    for _ in self.experts(pair, t, w1, w2, ysc, res_dram, sems):
                        self.pump(self.weights_ahead)
                        if k == 0:
                            self.pump(later)
                        yield
                    if k == 0:
                        for _ in later:
                            pass
            for _ in work():
                pass
            self.barrier()

    @staticmethod
    def pump(gen):
        try:
            next(gen)
        except StopIteration:
            pass

    def transpose_weights(self, st, weights, scratch, sems):
        pe, act, dve, pool, sp = self.queues
        NT = self.H * self.DH // P
        natural = Ring([Buffer(self.sbuf(st, "w_nat", [P, NT, self.D])) for _ in range(2)])
        parts = Ring([Buffer(self.sbuf(st, "w_parts", [P, NT, 2, self.DT, P], F32R)) for _ in range(2)])
        ring = Ring(self.banks[6:8])
        for i, (w, out) in enumerate(zip(weights, scratch)):
            nat, prt = natural.next(), parts.next()
            s = sp.dma(lambda e, w=w, nat=nat: e.dma_start(nat.ap[:], w.rearrange("h d c -> (h d) c").rearrange(
                "(n p) c -> p n c", p=P)), sems["nat"][i], nat.take())
            act.wait(prt.take())
            for ct in range(self.DT):
                for c in range(NT // 4):
                    bank = ring.next()
                    pe.wait(bank.take(), s)
                    for n in range(4 * c, 4 * c + 4):
                        m = pe.do(lambda e, n=n, ct=ct, bank=bank, nat=nat: e.transpose(
                            bank.ap[:, (n % 4) * P:(n % 4 + 1) * P], nat.ap[:, n, ct * P:(ct + 1) * P], self.ident[:]))
                    v = bank.ap.rearrange("p (n j) -> p n j", j=P)
                    ns = slice(4 * c, 4 * c + 4)
                    a = act.do(lambda e, v=v, ns=ns, ct=ct, prt=prt: e.copy(prt.ap[:, ns, 0, ct, :], v), m)
                    d = dve.do(lambda e, v=v, ns=ns, ct=ct, prt=prt: e.tensor_tensor(
                        prt.ap[:, ns, 1, ct, :], v, prt.ap[:, ns, 0, ct, :].bitcast(F32), ALU.subtract), a)
                    bank.used_by(d)
            nat.used_by(m)
            s = sp.dma(lambda e, prt=prt, out=out: e.dma_start(
                out.rearrange("n p k -> p n k"), prt.ap[:].rearrange("p n t c j -> p n (t c j)").bitcast(F32)),
                sems["wT"][i], d)
            prt.used_by(s)

    def stage_t(self, x_dram, out_dram, w_o, scratch, sems):
        pe, act, dve, pool, sp = self.queues
        B, L, D, NBLK, DT, DH = self.B, self.L, self.D, self.NBLK, self.DT, self.DH
        NHP = self.H // 2
        NC = L // BANK
        KPC = BANK // P
        QROWS = DH + NBLK
        scale = 1.0 / float(np.sqrt(DH))
        with ExitStack() as st:
            sb = lambda n, s, d=F32: self.sbuf(st, n, s, d)
            xy = Buffer(sb("t_xy", [P, NBLK, D]))
            xres_r = Ring([Buffer(sb("t_xres", [P, KPC, D])) for _ in range(2)])
            xT = Buffer((sb("t_xThi", [P, DT, L], F32R), sb("t_xTlo", [P, DT, L], F32R)))
            stats, mv, rstd = sb("t_stats", [P, NBLK, 6]), sb("t_mv", [P, NBLK, 2]), sb("t_rstd", [P, NBLK])
            wo = sb("t_wo", [P, NHP, D])
            wq_r = Ring([Buffer(sb("t_wq", [P, 2, DT, P], F32R)) for _ in range(2)])
            wk_r = Ring([Buffer(sb("t_wk", [P, 2, DT, P], F32R)) for _ in range(2)])
            wv_b = Buffer(sb("t_wv", [P, 2, 2, DT, P], F32R))
            v_r = Ring([Buffer(sb("t_v", [P, NBLK, 4 * DH])) for _ in range(2)])
            heads = [[Buffer({k: sb("t_" + k, [P, L], F32R) for k in ("qa", "qb", "ka", "kb")}) for _ in range(2)]
                     for _ in range(2)]
            p_r = Ring([Buffer(sb("t_p", [P, 2, BANK])) for _ in range(3)])
            acc_r = Ring([Buffer(sb("t_acc", [P, 2, BANK])) for _ in range(2)])
            yT = [Buffer(sb("t_yT", [P, NHP, BANK])) for _ in range(NC)]
            pvs_r = Ring([Buffer(sb("t_pvs", [P, BANK])) for _ in range(2)])
            rden_r = Ring([Buffer(sb("t_rden", [P, 2 * KPC])) for _ in range(2)])
            mask = sb("t_mask", [P, BANK])
            pick = sb("t_pick", [NBLK, NBLK, P])
            junk_r = Ring([Buffer(sb("t_junk", [P, BANK], BF16)) for _ in range(2)])
            mcol_r = Ring([Buffer(sb("t_mcol", [P, 2, NBLK])) for _ in range(2)])
            work = Ring([self.banks[0], self.banks[1], self.banks[7]])
            psum2 = lambda k: Buffer(self.psum_all[:, k * BANK:(k + 2) * BANK].rearrange("p (i q) -> p i q", i=2))
            st_banks = Ring([psum2(2), psum2(4)])
            pv_bank = self.banks[6]

            s = pool.do(lambda e: e.memset(mask[:], 0.0))
            s2 = pool.do(lambda e: e.memset(pick[:], 0.0))
            pool.do(lambda e: e.affine_select(out=mask[:], in_=mask[:], compare_op=ALU.is_ge, fill=NEG,
                                              base=BANK - P, pattern=[[-1, BANK]], channel_multiplier=1), s, s2)
            consts = pool.do(lambda e: e.affine_select(out=pick[:], in_=pick[:], compare_op=ALU.not_equal, fill=-1.0,
                                                       base=0, pattern=[[-1, NBLK], [0, P]], channel_multiplier=1))
            for pair in heads:
                for hd in pair:
                    consts = dve.do(lambda e, hd=hd: e.tensor_copy(
                        hd.ap["kb"][DH:QROWS, :].rearrange("p (a b) -> p a b", b=P),
                        spread(self.ones[DH:QROWS, :], 1, NBLK)), consts)
            wo_ready = sp.dma(lambda e: e.dma_start(wo[:], w_o.rearrange("(n p) d -> p n d", p=P)), sems["w1"])
            pe.wait(consts)

            state = dict(tick=0, rstd_user=None)
            due = []
            v_of, qk_ready, late_ready, max_ready = {}, {}, {}, {}
            extra = []

            def at(delay, function):
                due.append((state["tick"] + delay, function))

            def tick():
                now = [f for t, f in due if t <= state["tick"]]
                due[:] = [(t, f) for t, f in due if t > state["tick"]]
                for f in now:
                    f()
                state["tick"] += 1

            def prepare(b):
                rows = slice(b * L, (b + 1) * L)
                s = sp.dma(lambda e: e.dma_start(xy.ap[:], x_dram[rows, :].rearrange("(n p) d -> p n d", p=P)),
                           sems["x"], xy.take())
                norm = self.layer_norm(xy.ap, xy.ap, stats, mv, rstd, NBLK, s, state["rstd_user"])
                state["rstd_user"] = norm[-1]
                yield
                hi, lo = xT.ap
                users = xT.take()
                act.wait(users)
                dve.wait(users)
                for dt in range(DT):
                    for c in range(NC):
                        bank = work.next()
                        pe.wait(bank.take(), norm[-1])
                        for n in range(4 * c, 4 * c + 4):
                            m = pe.do(lambda e, n=n, dt=dt, bank=bank: e.transpose(
                                bank.ap[:, (n % 4) * P:(n % 4 + 1) * P], xy.ap[:, n, dt * P:(dt + 1) * P],
                                self.ident[:]))
                        cs = slice(c * BANK, (c + 1) * BANK)
                        a = act.do(lambda e, dt=dt, cs=cs, bank=bank: e.copy(hi[:, dt, cs], bank.ap), m)
                        d = dve.do(lambda e, dt=dt, cs=cs, bank=bank: e.tensor_tensor(
                            lo[:, dt, cs], bank.ap, hi[:, dt, cs].bitcast(F32), ALU.subtract), a)
                        bank.used_by(d)
                        yield
                xy.used_by(m)
                pe.wait(d)

            def project(b, hp):
                if hp == 0:
                    yield from prepare(b)
                xhi, xlo = xT.ap
                half = hp % 2
                pair = heads[half]
                wk, wq = wk_r.next(), wq_r.next()
                loads = [sp.dma(lambda e, w=w, d=d: e.dma_start(
                    w.ap[:].rearrange("p t c j -> p (t c j)").bitcast(F32), d[hp]), sems["wqk"][half][i], w.take())
                    for i, (w, d) in enumerate(((wk, scratch[1]), (wq, scratch[0])))]
                if half == 0:
                    wv_loaded = sp.dma(lambda e: e.dma_start(
                        wv_b.ap[:].rearrange("p n t c j -> p n (t c j)").bitcast(F32),
                        scratch[2][hp:hp + 2].rearrange("n p k -> p n k")), sems["wv"], wv_b.take())
                for hd in pair:
                    users = hd.take()
                    act.wait(users)
                    dve.wait(users)
                    sp.wait(users)
                terms = [(0, xhi, 0), (1, xhi, 0), (0, xlo, 0), (0, xhi, 1), (1, xhi, 1), (0, xlo, 1)]
                out, late = [], []
                finish = None
                for is_q, w in enumerate((wk, wq)):
                    pe.wait(loads[is_q])
                    copies = []
                    for c in range(NC):
                        cs = slice(c * BANK, (c + 1) * BANK)
                        bank = work.next()
                        pe.wait(bank.take())
                        for k, (pw, px, ct) in enumerate(terms):
                            m = pe.do(lambda e, w=w, pw=pw, px=px, ct=ct, k=k, cs=cs, bank=bank: e.matmul(
                                bank.ap, w.ap[:, pw, ct, :], px[:, ct, cs],
                                start=(k == 0), stop=(k == len(terms) - 1)))
                        hs = []
                        for i, hd in enumerate(pair):
                            src = bank.ap[i * DH:(i + 1) * DH, :]
                            hi = hd.ap["qa" if is_q else "ka"]
                            hs.append(act.do(lambda e, hi=hi, cs=cs, src=src: e.copy(hi[0:DH, cs], src), m))
                        copies.append(hs)
                        if finish:
                            finish()

                        def finish(is_q=is_q, cs=cs, bank=bank, hs=hs):
                            for i, hd in enumerate(pair):
                                src = bank.ap[i * DH:(i + 1) * DH, :]
                                hi = hd.ap["qa" if is_q else "ka"]
                                lo = hd.ap["qa"][DH:2 * DH, cs] if is_q else hd.ap["kb"][0:DH, cs]
                                d = dve.do(lambda e, lo=lo, hi=hi, cs=cs, src=src: e.tensor_tensor(
                                    lo, src, hi[0:DH, cs].bitcast(F32), ALU.subtract), hs[i])
                                out.append(d)
                            bank.used_by(d)
                        yield
                    w.used_by(m)
                    for i, hd in enumerate(pair):
                        src = hd.ap["qa" if is_q else "ka"][0:DH, :]
                        dup = hd.ap["qb"][0:DH, :] if is_q else hd.ap["ka"][DH:2 * DH, :]
                        (late if is_q else out).append(sp.dma(lambda e, dup=dup, src=src: e.dma_start(dup.bitcast(F32), src.bitcast(F32)),
                                          sems["dup"][half][i][is_q], [h[i] for h in copies]))
                if half == 0:
                    v = v_r.next()
                    v_of[b, hp // 2] = v
                    pe.wait(wv_loaded)
                    act.wait(v.take())
                    for n in range(0, NBLK, 2):
                        bank = work.next()
                        pe.wait(bank.take())
                        for i in range(2):
                            ns = slice((n + i) * P, (n + i + 1) * P)
                            for k, (pw, px, ct) in enumerate(terms):
                                m = pe.do(lambda e, pw=pw, px=px, ct=ct, k=k, ns=ns, i=i, bank=bank: e.matmul(
                                    bank.ap[:, i * 4 * DH:(i + 1) * 4 * DH], px[:, ct, ns], wv_b.ap[:, :, pw, ct, :],
                                    start=(k == 0), stop=(k == len(terms) - 1)))
                        a = act.do(lambda e, n=n, bank=bank, v=v: e.copy(
                            v.ap[:, n:n + 2, :], bank.ap.rearrange("p (i d) -> p i d", i=2)), m)
                        bank.used_by(a)
                        if finish:
                            finish()
                            finish = None
                        yield
                    wv_b.used_by(m)
                    late.append(a)
                if finish:
                    finish()
                if hp == NHP - 1:
                    xT.used_by(m)
                qk_ready[b, hp], late_ready[b, hp] = out, late

            def maxima(b, hp):
                pe.wait(qk_ready[b, hp])
                out = []
                spread_rows = None
                for i, hd in enumerate(heads[hp % 2]):
                    t = hd.ap
                    mc = mcol_r.next()
                    dve.wait(mc.take())
                    for n in range(NBLK):
                        for c in range(n // KPC + 1):
                            w = min(BANK, (n + 1) * P - c * BANK)
                            bank = work.next()
                            m = pe.do(lambda e, t=t, n=n, c=c, w=w, bank=bank: e.matmul(
                                bank.ap[:, 0:w], t["qa"][:, n * P:(n + 1) * P], t["ka"][:, c * BANK:c * BANK + w],
                                start=True, stop=True), bank.take())
                            if c == n // KPC:
                                junk = junk_r.next()
                                d = dve.do(lambda e, n=n, c=c, w=w, bank=bank, mc=mc, junk=junk:
                                           e.tensor_tensor_reduce(
                                               junk.ap[:, 0:w], bank.ap[:, 0:w], mask[:, BANK - w:BANK], 1.0, NEG,
                                               ALU.add, ALU.max, mc.ap[:, c, n:n + 1]), m, junk.take())
                                junk.used_by(d)
                            else:
                                d = dve.do(lambda e, n=n, c=c, bank=bank, mc=mc: e.tensor_reduce(
                                    mc.ap[:, c, n:n + 1], bank.ap, AX.X, ALU.max), m)
                            bank.used_by(d)
                        if spread_rows:
                            spread_rows()
                            spread_rows = None
                        if n != 0 and n != 2:
                            yield
                    d = dve.do(lambda e, mc=mc: e.tensor_tensor(
                        mc.ap[:, 0, KPC:], mc.ap[:, 0, KPC:], mc.ap[:, 1, KPC:], ALU.max), d)

                    def spread_rows(t=t, mc=mc, d=d):
                        bank = work.next()
                        m = pe.do(lambda e: e.transpose(bank.ap[0:NBLK, 0:P], mc.ap[:, 0, :], self.ident[:]),
                                  bank.take(), d)
                        mc.used_by(m)
                        d2 = dve.do(lambda e: e.tensor_tensor(
                            t["qb"][DH:QROWS, :].rearrange("p (a b) -> p a b", b=P),
                            spread(bank.ap[0:NBLK, 0:P], 1, NBLK), pick[:], ALU.mult), m)
                        bank.used_by(d2)
                        out.append(d2)
                spread_rows()
                max_ready[b, hp] = out + late_ready[b, hp]

            def attend(b, hp):
                pair = heads[hp % 2]
                v = v_of[b, hp // 2]
                vcol = (hp % 2) * 2 * DH
                pe.wait(max_ready[b, hp])
                for c in range(NC):
                    last = KPC * (c + 1) - 1
                    acc = acc_r.next()
                    chunk = dict(sum=None)

                    def weigh(kt, q0, p, s, c=c, last=last, acc=acc, chunk=chunk):
                        if kt == 0:
                            d = dve.do(lambda e: e.tensor_copy(acc.ap[:], p.ap[:]), s, acc.take())
                            pe.wait(pv_bank.take())
                        else:
                            adder = pool if kt % 3 == 2 else dve
                            d = adder.do(lambda e: e.tensor_tensor(acc.ap[:, :, q0:], acc.ap[:, :, q0:],
                                                                   p.ap[:, :, q0:], ALU.add), s, chunk["sum"])
                        chunk["sum"] = d
                        pe.wait(s)
                        for i in range(2):
                            m = pe.do(lambda e, i=i: e.matmul(
                                pv_bank.ap[i * DH:(i + 1) * DH, q0:BANK],
                                v.ap[:, kt, vcol + i * DH:vcol + (i + 1) * DH], p.ap[:, i, q0:BANK],
                                start=(kt == 0), stop=(kt == last), skip_group_check=True))
                        p.used_by(d, m)
                        if kt == last:
                            pvs = pvs_r.next()
                            a = act.do(lambda e: e.copy(pvs.ap[:], pv_bank.ap), m, pvs.take())
                            pv_bank.used_by(a)
                            v.used_by(m)
                            at(1, lambda: divide(c, acc, d, pvs, a))

                    def divide(c, acc, d, pvs, a):
                        bank = work.next()
                        pe.wait(bank.take(), d)
                        for i in range(2):
                            for k in range(KPC):
                                m = pe.do(lambda e, i=i, k=k: e.matmul(
                                    bank.ap[:, i * KPC + k:i * KPC + k + 1], acc.ap[:, i, k * P:(k + 1) * P],
                                    self.ones[:, 0:1], start=True, stop=True))
                        acc.used_by(m)
                        rden = rden_r.next()
                        d = dve.do(lambda e: e.reciprocal(rden.ap[:], bank.ap[:, 0:2 * KPC]), m, rden.take())
                        bank.used_by(d)

                        def scale_rows():
                            bank = work.next()
                            pe.wait(bank.take(), d)
                            for k in range(KPC):
                                for i in range(2):
                                    m = pe.do(lambda e, i=i, k=k: e.matmul(
                                        bank.ap[i * DH:(i + 1) * DH, k * P:(k + 1) * P],
                                        rden.ap[:, i * KPC + k:i * KPC + k + 1].to_broadcast([P, DH]), self.ident[:],
                                        start=True, stop=True, skip_group_check=True))
                            rden.used_by(m)
                            if hp == 0:
                                dve.wait(yT[c].take())
                            d2 = dve.do(lambda e: e.tensor_tensor(yT[c].ap[:, hp, :], pvs.ap[:], bank.ap, ALU.mult),
                                        m, a)
                            bank.used_by(d2)
                            pvs.used_by(d2)
                            if hp == NHP - 1:
                                extra.append(output(b, c, d2))
                        at(1, scale_rows)

                    for kt in range(last + 1):
                        tick()
                        q0 = max(0, kt * P - c * BANK)
                        bank = st_banks.next()
                        qs = slice(c * BANK + q0, (c + 1) * BANK)
                        ks = slice(kt * P, (kt + 1) * P)
                        pe.wait(bank.take())
                        for i in range(2):
                            t = pair[i].ap
                            pe.do(lambda e, t=t, ks=ks, qs=qs, q0=q0, i=i, bank=bank: e.matmul(
                                bank.ap[:, i, q0:], t["ka"][:, ks], t["qa"][:, qs], start=True, stop=False))
                            m = pe.do(lambda e, t=t, ks=ks, qs=qs, q0=q0, i=i, bank=bank: e.matmul(
                                bank.ap[:, i, q0:], t["kb"][0:QROWS, ks], t["qb"][0:QROWS, qs],
                                start=False, stop=True))
                        p = p_r.next()
                        s = act.do(lambda e, p=p, q0=q0, bank=bank: e.activation(
                            p.ap[:, :, q0:], bank.ap[:, :, q0:], ACT.Exp, scale=scale), m, p.take())
                        bank.used_by(s)
                        if kt >= KPC * c:
                            s = pool.do(lambda e, p=p, q0=q0: e.affine_select(
                                out=p.ap[:, :, q0:q0 + P], in_=p.ap[:, :, q0:q0 + P], compare_op=ALU.is_ge, fill=0.0,
                                base=0, pattern=[[0, 2], [1, P]], channel_multiplier=-1), s)
                        at(1, lambda kt=kt, q0=q0, p=p, s=s, weigh=weigh: weigh(kt, q0, p, s))
                        yield
                for hd in pair:
                    hd.used_by(m)

            def output(b, c, y_ready):
                rows = slice(b * L + c * BANK, b * L + (c + 1) * BANK)
                k_ = xres_r.n % 2
                xres = xres_r.next()
                s = sp.dma(lambda e: e.dma_start(xres.ap[:], x_dram[rows, :].rearrange("(n p) d -> p n d", p=P)),
                           sems["xr"][k_], xres.take())
                pe.wait(y_ready, wo_ready)
                for n in range(KPC):
                    bank = work.next()
                    pe.wait(bank.take())
                    for k in range(NHP):
                        m = pe.do(lambda e, n=n, k=k, bank=bank: e.matmul(
                            bank.ap[:, 0:D], yT[c].ap[:, k, n * P:(n + 1) * P], wo[:, k, :],
                            start=(k == 0), stop=(k == NHP - 1)))
                    d = dve.do(lambda e, n=n, bank=bank, xres=xres: e.tensor_tensor(
                        xres.ap[:, n, :], bank.ap[:, 0:D], xres.ap[:, n, :], ALU.add), m, s)
                    bank.used_by(d)
                    if n == KPC - 1:
                        yT[c].used_by(m)
                        s = sp.dma(lambda e: e.dma_start(
                            out_dram[rows, :].rearrange("(n p) d -> p n d", p=P), xres.ap[:]), sems["xo"][k_], d)
                        xres.used_by(s)
                    yield

            units = [(b, hp) for b in range(B) for hp in range(NHP)]

            def ahead(b, hp):
                yield from project(b, hp)
                yield from maxima(b, hp)
            for _ in ahead(*units[0]):
                pass
            for n, unit in enumerate(units):
                coming = ahead(*units[n + 1]) if n + 1 < len(units) else iter(())
                hp = (unit[1] + 1) % NHP
                pieces = 2 * NC + NBLK // 2 * (hp % 2 == 0) + 12 + 5 * (hp == 0)
                owed = 0.0
                for _ in attend(*unit):
                    owed += pieces / 10.5
                    while owed >= 1:
                        self.pump(coming)
                        owed -= 1
                    if extra and extra[0] is not None:
                        try:
                            next(extra[0])
                        except StopIteration:
                            extra.pop(0)
                for _ in coming:
                    pass
            while due:
                tick()
            for stream in extra:
                for _ in stream:
                    pass
            self.barrier()


PHASES = "AFTF"


def hybrid_kernel(nc, x, w_q, w_k, w_v, w_o, gate_w, w1, w2, out):
    B, L, D = x.shape
    E, _, Fh = w1.shape
    H = w_q.shape[0]
    rows = B * L
    scratch = lambda name, shape, dtype=F32: nc.dram_tensor(name, shape, dtype, kind="Internal").ap()
    n_f = PHASES.count("F")
    with ExitStack() as ctx:
        pr = Program(nc, ctx, dict(x=x.shape, w1=w1.shape, w_q=w_q.shape))
        sems = {n: pr.dma_sem("loaded_" + n) for n in ("x", "tab", "w1", "w2", "wv", "gate")}
        sems["xr"] = [pr.dma_sem(f"loaded_xres{i}") for i in range(2)]
        sems["xo"] = [pr.dma_sem(f"stored_x{i}") for i in range(2)]
        sems["wqk"] = [[pr.dma_sem(f"loaded_w{n}{i}") for n in "kq"] for i in range(2)]
        sems["dup"] = [[[pr.dma_sem(f"doubled_{n}{i}_{h}") for n in "kq"] for h in range(2)] for i in range(2)]
        sems["y"] = [pr.dma_sem(f"stored_y{b}") for b in range(B)]
        sems["xg"] = [pr.dma_sem(f"gathered{i}") for i in range(8)]
        sems["add"] = [[pr.dma_sem(f"added{b}_{h}") for h in range(2)] for b in range(B)]
        a_x = [pr.dma_sem(f"a_x{b}") for b in range(B)]
        a_out = pr.dma_sem("a_out")
        sems["nat"] = [pr.dma_sem(f"loaded_nat{i}") for i in range(3)]
        sems["wT"] = [pr.dma_sem(f"stored_wT{i}") for i in range(3)]
        pr.constants()
        pr.barrier()
        wT = [scratch(n, (H * pr.DH // P, P, 2 * pr.DT * P)) for n in ("wqT", "wkT", "wvT")]
        flat_x, flat_out = x.rearrange("b l d -> (b l) d"), out.rearrange("b l d -> (b l) d")
        res = scratch("res", (rows, D))
        f_round = 0
        if "T" in PHASES:
            with ExitStack() as st:
                pr.transpose_weights(st, (w_q, w_k, w_v), wT, sems)
                pr.barrier()
        for n, phase in enumerate(PHASES):
            if phase == "A":
                pr.stage_a(flat_x, res if "T" in PHASES else flat_out, a_x, a_out)
            elif phase == "F":
                ysc = [scratch(f"ysc{f_round}_{b}", (L, D)) for b in range(B)]
                tabs = [scratch(f"tab{f_round}_{b}", (E, 512)) for b in range(B)]
                f_round += 1
                pr.stage_f(flat_out if ("T" not in PHASES or "T" in PHASES[:n]) else res, gate_w, w1, w2,
                           ysc, tabs, sems)
            else:
                pr.stage_t(res, flat_out, w_o, wT, sems)
        for q in pr.queues:
            q.number()
        block = ctx.enter_context(nc.Block())
        block.tensor(lambda e: pr.pe.play(e))
        block.scalar(lambda e: pr.act.play(e))
        block.vector(lambda e: pr.dve.play(e))
        block.gpsimd(lambda e: pr.pool.play(e))
        block.sync(lambda e: pr.sp.play(e))


NAMES = ["L0_attn_a_x", "L0_attn_b_w_q", "L0_attn_b_w_k", "L0_attn_b_w_v", "L0_attn_b_w_o",
         "L0_ffn_gate_w", "L0_ffn_w1", "L0_ffn_w2"]


def kernel(**inputs):
    import concourse.bacc as bacc
    from concourse.bass_utils import run_bass_kernel_spmd as run

    nc = bacc.Bacc("TRN2", target_bir_lowering=False, num_devices=1)
    arrays = {n: np.ascontiguousarray(inputs[n]) for n in NAMES}
    args = [nc.dram_tensor("in_" + n, a.shape, mybir.dt.from_np(a.dtype), kind="ExternalInput").ap()
            for n, a in arrays.items()]
    out = nc.dram_tensor("out", arrays[NAMES[0]].shape, F32, kind="ExternalOutput").ap()
    hybrid_kernel(nc, *args, out)
    r = run(nc, [{"in_" + n: a for n, a in arrays.items()}], core_ids=[0])
    return r.results[0]["out"]
```

```python
from contextlib import ExitStack

import numpy as np
import concourse.bass as bass
from concourse import mybir

F32 = mybir.dt.float32
F32R = mybir.dt.float32r
BF16 = mybir.dt.bfloat16
I32 = mybir.dt.int32
U32 = mybir.dt.uint32
ALU = mybir.AluOpType
ACT = mybir.ActivationFunctionType
AX = mybir.AxisListType

P = 128
BANK = 512
EPS = 1e-5
NEG = -3.0e38


class Step:

    def __init__(self, queue):
        self.queue, self.needed, self.value = queue, False, None


class Transfer:

    def __init__(self, sem, value):
        self.sem, self.value = sem, value


class DmaSem:

    def __init__(self, sem):
        self.sem, self.count = sem, 0


class Queue:

    def __init__(self, sem):
        self.sem, self.items, self.last = sem, [], None

    def wait(self, *producers):
        for p in producers:
            if p is None:
                continue
            if isinstance(p, (list, tuple)):
                self.wait(*p)
                continue
            if isinstance(p, Step):
                p.needed = True
            self.items.append(("wait", p))

    def do(self, emit, *producers):
        self.wait(*producers)
        step = Step(self)
        self.items.append(("do", emit, step))
        self.last = step
        return step

    def dma(self, emit, sem, *producers):
        self.wait(*producers)
        sem.count += 16
        self.items.append(("dma", emit, sem.sem))
        return Transfer(sem.sem, sem.count)

    def number(self):
        n = 0
        for item in self.items:
            if item[0] == "do" and item[2].needed:
                n += 1
                item[2].value = n

    def play(self, engine):
        seen = {}
        for item in self.items:
            if item[0] == "wait":
                p = item[1]
                sem = p.queue.sem if isinstance(p, Step) else p.sem
                if seen.get(id(sem), 0) < p.value:
                    engine.wait_ge(sem, p.value)
                    seen[id(sem)] = p.value
            elif item[0] == "dma":
                item[1](engine).then_inc(item[2], 16)
            else:
                instruction = item[1](engine)
                if item[2].needed:
                    instruction.then_inc(self.sem, 1)


class Buffer:

    def __init__(self, ap):
        self.ap, self.users = ap, []

    def take(self):
        users, self.users = self.users, []
        return users

    def used_by(self, *steps):
        self.users += steps


class Ring:

    def __init__(self, buffers):
        self.buffers, self.n = list(buffers), 0

    def next(self):
        b = self.buffers[self.n % len(self.buffers)]
        self.n += 1
        return b


def spread(ap, axis, n):
    ap = ap.unsqueeze(axis)
    shape = list(ap.shape)
    shape[axis] = n
    return ap.to_broadcast(shape)


def interleave(*streams):
    live = [[g, w] for g, w in streams]
    while live:
        for s in list(live):
            for _ in range(s[1]):
                try:
                    next(s[0])
                except StopIteration:
                    live.remove(s)
                    break


class Program:
    def __init__(self, nc, ctx, shapes):
        self.nc, self.ctx = nc, ctx
        self.B, self.L, self.D = shapes["x"]
        self.E, self.F = shapes["w1"][0], shapes["w1"][2]
        self.H, self.DH = shapes["w_q"][0], shapes["w_q"][1]
        self.CAP = 2 * self.L // self.E
        self.NBLK = self.L // P
        self.DT = self.D // P
        self.FT = self.F // P
        self.n_names = 0
        self.stored = {}
        self.rows_free = None
        self.pe = Queue(self.semaphore("pe_done"))
        self.act = Queue(self.semaphore("act_done"))
        self.dve = Queue(self.semaphore("dve_done"))
        self.pool = Queue(self.semaphore("pool_done"))
        self.sp = Queue(self.semaphore("sp_done"))
        self.queues = [self.pe, self.act, self.dve, self.pool, self.sp]
        self.dma_sems = []
        self.psum_all = psum = self.psum("psum", [P, 8 * BANK])
        self.banks = [Buffer(psum[:, i * BANK:(i + 1) * BANK]) for i in range(8)]

    def semaphore(self, name):
        return self.ctx.enter_context(self.nc.semaphore(name))

    def dma_sem(self, name):
        s = DmaSem(self.semaphore(name))
        self.dma_sems.append(s)
        return s

    def sbuf(self, stack, name, shape, dtype=F32):
        self.n_names += 1
        return stack.enter_context(self.nc.sbuf_tensor(f"{name}_{self.n_names}", shape, dtype))

    def psum(self, name, shape):
        return self.ctx.enter_context(self.nc.psum_tensor(name, shape, F32))

    def barrier(self):
        last = [q.last for q in self.queues if q.last is not None]
        moved = [Transfer(s.sem, s.count) for s in self.dma_sems if s.count]
        for q in self.queues:
            q.wait(*last, *moved)

    def constants(self):
        pool, dve = self.pool, self.dve
        c = lambda name, shape, dtype=F32: self.sbuf(self.ctx, name, shape, dtype)
        self.ident = c("ident", [P, P])
        self.ident_b = c("ident_b", [P, P], BF16)
        self.ones = c("ones", [P, P])
        self.ones_b = c("ones_b", [P, P], BF16)
        self.upto_b = c("upto_b", [P, P], BF16)
        self.same_f = c("same_f", [P, self.E])
        self.same_b = c("same_b", [P, P], BF16)
        self.minus_half = c("minus_half", [P, self.NBLK])
        self.NCAND = 8
        self.SHIFTS = list(range(27, -1, -3))
        self.digit = c("digit", [P, len(self.SHIFTS)], I32)
        lane = c("lane", [P, 1], I32)
        self.tokid = c("tokid", [P, self.NBLK])
        tok_i = c("tok_i", [P, self.NBLK], I32)
        self.iota16 = c("iota16", [P, 16])
        iota_i = c("iota_i", [P, 16], I32)
        self.zero_i = c("zero_i", [P, 1], I32)
        m = [pool.do(lambda e, t=t, v=v: e.memset(t[:], v))
             for t, v in ((self.ident, 0.0), (self.ident_b, 0.0), (self.ones, 1.0), (self.ones_b, 1.0),
                          (self.minus_half, -0.5))]
        pool.wait(m[-1])
        eye = dict(compare_op=ALU.not_equal, fill=1.0, base=0, pattern=[[-1, P]], channel_multiplier=1)
        pool.do(lambda e: e.affine_select(out=self.ident[:], in_=self.ident[:], **eye))
        pool.do(lambda e: e.affine_select(out=self.ident_b[:], in_=self.ident_b[:], **eye))
        pool.do(lambda e: e.affine_select(out=self.upto_b[:], in_=self.ones_b[:], compare_op=ALU.is_ge, fill=0.0,
                                          base=0, pattern=[[1, P]], channel_multiplier=-1))

        def same(out, in_, w, q, n):
            a = pool.do(lambda e: e.affine_select(out=out, in_=in_, compare_op=ALU.is_ge, fill=0.0, base=0,
                                                  pattern=[[-w, q]] + n, channel_multiplier=1))
            pool.do(lambda e: e.affine_select(out=out, in_=out, compare_op=ALU.is_ge, fill=0.0, base=w - 1,
                                              pattern=[[w, q]] + n, channel_multiplier=-1), a)
        same(self.same_f[:], self.ones[:, 0:self.E], P // self.E, self.E, [])
        v = lambda t: t[:].rearrange("p (e j) -> p e j", j=self.NCAND)
        same(v(self.same_b), v(self.ones_b), self.NCAND, P // self.NCAND, [[0, self.NCAND]])
        pool.do(lambda e: e.iota(lane[:], pattern=[[0, 1]], base=0, channel_multiplier=1))
        pool.do(lambda e: e.iota(tok_i[:], pattern=[[P, self.NBLK]], base=0, channel_multiplier=1))
        made = pool.do(lambda e: e.iota(iota_i[:], pattern=[[1, 16]], base=0, channel_multiplier=0))
        dve.do(lambda e: e.tensor_copy(self.tokid[:], tok_i[:]), made)
        dve.do(lambda e: e.tensor_copy(self.iota16[:], iota_i[:]))
        dve.do(lambda e: e.memset(self.zero_i[:], 0))
        for n, s in enumerate(self.SHIFTS):
            dve.do(lambda e, n=n, s=s: e.tensor_scalar(
                self.digit[:, n:n + 1], lane[:], self.NCAND - 1, s, ALU.bitwise_and, ALU.logical_shift_left))

    def layer_norm_pieces(self, x, y, stats, mv, rstd, nb, out, *ready):
        act, dve, pool = self.act, self.dve, self.pool
        dve.wait(*ready)
        for i in range(nb):
            s = dve.do(lambda e, i=i: e.bn_stats(stats[:, i, :], x[:, i, :]))
            if i % 4 == 3:
                yield
        for i in range(nb):
            s2 = dve.do(lambda e, i=i: e.bn_aggr(mv[:, i, :], stats[:, i, :]), s)
        s = dve.do(lambda e: e.tensor_scalar(rstd[:, 0:nb], mv[:, 0:nb, 1], EPS, None, ALU.add), s2)
        s = pool.do(lambda e: e.tensor_tensor(rstd[:, 0:nb], rstd[:, 0:nb], self.minus_half[:, 0:nb], ALU.pow), s)
        yield
        s2 = dve.do(lambda e: e.scalar_tensor_tensor(
            out=rstd[:, nb:2 * nb], in0=mv[:, 0:nb, 0], scalar=-1.0, in1=rstd[:, 0:nb], op0=ALU.mult, op1=ALU.mult), s)
        for i in range(nb):
            if i % 2:
                out.append(dve.do(lambda e, i=i: e.tensor_scalar(
                    y[:, i, :], x[:, i, :], mv[:, i, 0:1], rstd[:, i:i + 1], ALU.subtract, ALU.mult), s))
            else:
                out.append(act.do(lambda e, i=i: e.activation(
                    y[:, i, :], x[:, i, :], ACT.Identity, bias=rstd[:, nb + i:nb + i + 1],
                    scale=rstd[:, i:i + 1]), s2))
            if i % 2:
                yield

    def layer_norm(self, x, y, stats, mv, rstd, nb, *ready):
        out = []
        for _ in self.layer_norm_pieces(x, y, stats, mv, rstd, nb, out, *ready):
            pass
        return out

    def stage_a(self, x_dram, out_dram, x_sem, out_sem, weights_stream):
        pe, act, dve, pool, sp = self.queues
        B, NBLK, D, DK = self.B, self.NBLK, self.D, 16
        H = D // DK
        half = BANK // D
        with ExitStack() as st:
            x = self.sbuf(st, "a_x", [P, B, NBLK, D])
            y = self.sbuf(st, "a_y", [P, NBLK, B, D])
            mix = self.sbuf(st, "a_mix", [P, NBLK, self.L])
            ang = [Buffer(self.sbuf(st, "a_ang", [P, self.L])) for _ in range(2)]
            stats = self.sbuf(st, "a_stats", [P, B, NBLK, 6])
            mv = self.sbuf(st, "a_mv", [P, B, NBLK, 2])
            rstd = self.sbuf(st, "a_rstd", [P, B, 2 * NBLK])
            msum = self.sbuf(st, "a_msum", [P, NBLK, DK])
            mT = self.sbuf(st, "a_mT", [DK, self.L])
            den = self.sbuf(st, "a_den", [P, NBLK])
            rden = self.sbuf(st, "a_rden", [P, NBLK])
            loads = []
            for b in range(B):
                loads.append(sp.dma(lambda e, b=b: e.dma_start(
                    x[:, b], x_dram[b * self.L:(b + 1) * self.L, :].rearrange("(n p) d -> p n d", p=P)), x_sem[b % 4]))
            norm = []
            halves = mix[:].rearrange("p n (h k) -> p (n h) k", k=BANK)
            weights = weights_stream(st, (halves[:, 0:NBLK], halves[:, NBLK:]))
            self.pump(weights)
            for b in range(B):
                norm += self.layer_norm(x[:, b], y[:, :, b, :], stats[:, b], mv[:, b], rstd[:, b], NBLK, loads[b])
                self.pump(weights)
            sums = []
            for n in range(NBLK):
                s = dve.do(lambda e, n=n: e.tensor_reduce(
                    msum[:, n, :], y[:, n].rearrange("p b (h k) -> p k b h", k=DK), AX.XY, ALU.add), norm[-2:])
                sums.append(dve.do(lambda e, n=n: e.tensor_scalar(msum[:, n, :], msum[:, n, :], 1.0 / (B * H), None,
                                                                  ALU.mult), s))
                self.pump(weights)
            for _ in weights:
                pass
            for c in range(2):
                bank = self.banks[c]
                pe.wait(bank.take())
                for n in range(4 * c, 4 * c + 4):
                    t = pe.do(lambda e, n=n, bank=bank: e.transpose(
                        bank.ap[0:DK, (n % 4) * P:(n % 4 + 1) * P], msum[:, n, :], self.ident[:]),
                        sums[n], pool.last if n == 0 else None)
                s = act.do(lambda e, c=c, bank=bank: e.copy(mT[:, c * BANK:(c + 1) * BANK], bank.ap[0:DK, :]), t)
                bank.used_by(s)
            mt_ready = s
            exps = []
            ring = Ring(self.banks[2:6])
            for n in range(NBLK):
                a = ang[n % 2]
                for c in range(2):
                    bank = ring.next()
                    t = pe.do(lambda e, n=n, c=c, bank=bank: e.matmul(
                        bank.ap, mT[:, n * P:(n + 1) * P], mT[:, c * BANK:(c + 1) * BANK], start=True, stop=True),
                        mt_ready, bank.take())
                    s = dve.do(lambda e, a=a, c=c, bank=bank: e.tensor_scalar(
                        a.ap[:, c * BANK:(c + 1) * BANK], bank.ap, float(np.pi), float(-np.pi), ALU.min, ALU.max),
                        t, a.take() if c == 0 else None)
                    bank.used_by(s)
                s = act.do(lambda e, a=a: e.activation(a.ap[:], a.ap[:], ACT.Sin, scale=0.5), s)
                squarer = pool if n % 3 == 2 else dve
                s = squarer.do(lambda e, a=a, n=n: e.tensor_tensor(mix[:, n, :], a.ap[:], a.ap[:], ALU.mult), s,
                               self.weights_moved)
                a.used_by(s)
                exps.append(s)
            done = []
            for n in range(NBLK):
                s = act.do(lambda e, n=n: e.activation(mix[:, n, :], mix[:, n, :], ACT.Exp,
                                                       accum_out=den[:, n:n + 1]), exps[n])
                done.append(s)
            s = dve.do(lambda e: e.reciprocal(rden[:], den[:]), done[-1])
            pe.wait(norm[-2:])
            ring = Ring(self.banks[0:6])
            for c in range(B // half):
                moved = []
                for i in range(NBLK):
                    bank = ring.next()
                    pe.wait(bank.take())
                    for j in range(NBLK):
                        pe.wait(done[j])
                        t = pe.do(lambda e, i=i, j=j, c=c, bank=bank: e.matmul(
                            bank.ap, mix[:, j, i * P:(i + 1) * P],
                            y[:, j, c * half:(c + 1) * half, :].rearrange("p b d -> p (b d)"),
                            start=(j == 0), stop=(j == NBLK - 1)))
                        if c:
                            yield
                    v = bank.ap.rearrange("p (b d) -> p b d", b=half)
                    xs = x[:, c * half:(c + 1) * half, i, :]
                    t = dve.do(lambda e, v=v, xs=xs, i=i: e.scalar_tensor_tensor(
                        out=xs, in0=v, scalar=rden[:, i:i + 1], in1=xs, op0=ALU.mult, op1=ALU.add), t, s)
                    bank.used_by(t)
                    for b in range(c * half, (c + 1) * half):
                        r0 = b * self.L + i * P
                        moved.append(sp.dma(lambda e, b=b, i=i, r0=r0: e.dma_start(
                            out_dram[r0:r0 + P, :], x[:, b, i, :]), out_sem[c], t))
                for b in range(c * half, (c + 1) * half):
                    self.stored[b] = moved[-1]
            self.barrier()

    def route_tiles(self, st):
        t = {}
        sb = lambda n, s, d=F32: self.sbuf(st, n, s, d)
        B, NBLK, D, E = self.B, self.NBLK, self.D, self.E
        t["xy"] = Ring([Buffer(sb("f_xy", [P, NBLK, D])) for _ in range(2)])
        t["yT"] = Buffer(sb("f_yT", [P, self.DT, self.L]))
        t["stats"] = [sb("f_stats", [P, NBLK, 6]) for _ in range(2)]
        t["mv"] = [sb("f_mv", [P, NBLK, 2]) for _ in range(2)]
        t["rstd"] = [sb("f_rstd", [P, 2 * NBLK]) for _ in range(2)]
        for n in ("scd", "ex", "pr", "m1", "sel", "pos"):
            t[n] = sb("f_" + n, [P, 2, NBLK, E])
        for n in ("key", "hi4", "lo4"):
            t[n] = sb("f_" + n, [P, 2, NBLK, E], I32)
        for n in ("mx", "sm"):
            t[n] = sb("f_" + n, [P, 2, NBLK])
        t["wide"] = sb("f_wide", [P, NBLK, 2, E, self.NCAND])
        t["pT"] = sb("f_pT", [P, self.L])
        t["junk"] = sb("f_junk", [P, self.L], BF16)
        t["cnt"] = sb("f_cnt", [P, 1])
        t["ind"] = sb("f_ind", [P, 1], BF16)
        t["bits"] = sb("f_bits", [P, 1], I32)
        t["prefix"] = sb("f_prefix", [P, 1], I32)
        t["thr"] = sb("f_thr", [P, 1], I32)
        t["Tfull"] = sb("f_Tfull", [P, P])
        t["Tb"] = sb("f_Tb", [P, 2, E])
        t["ge"] = sb("f_ge", [P, 2, 2, NBLK, E], BF16)
        t["need"] = sb("f_need", [P, 2, E])
        t["A"] = Buffer(sb("f_A", [P, NBLK, E, 16]))
        t["C"] = Buffer(sb("f_C", [P, NBLK, E, 16, 2]))
        t["Rw"] = sb("f_Rw", [P, E, 32])
        t["R"] = [Buffer(sb("f_R", [P, 32])) for _ in range(2)]
        t["tab"] = [sb("f_tab", [P, E, 2, 2]) for _ in range(B)]
        t["idx"] = [sb("f_idx", [P, E, 2], U32) for _ in range(B)]
        t["row"] = [sb("f_row", [P, E, 2], U32) for _ in range(B)]
        t["wst"] = Buffer(sb("f_wst", [P, 2, self.DT * self.F]))
        t["xg"] = Ring([Buffer(sb("f_xg", [P, self.D])) for _ in range(8)])
        t["gate"] = sb("f_gate", [self.E, self.D])
        t["gateT"] = sb("f_gateT", [P, self.DT, self.E])
        return t

    def expert_tiles(self, st, t):
        sb = lambda n, s, d=F32: self.sbuf(st, n, s, d)
        t["whi"] = [Buffer(sb("f_whi", [P, 2, self.DT * self.F], F32R)) for _ in range(2)]
        t["wlo"] = [Buffer(sb("f_wlo", [P, 2, self.DT * self.F], F32R)) for _ in range(2)]
        t["xin"] = Buffer((sb("f_xhi", [P, self.DT, BANK], F32R), sb("f_xlo", [P, self.DT, BANK], F32R)))
        t["h"] = Ring([Buffer(sb("f_h", [P, BANK])) for _ in range(2)])
        t["hs"] = [Buffer((sb("f_hhi", [P, BANK], F32R), sb("f_hlo", [P, BANK], F32R))) for _ in range(self.FT)]
        t["yo"] = Ring([Buffer(sb("f_yo", [P, self.D])) for _ in range(4)])

    def route(self, pair, t, res_dram, ysc, tabs, sems):
        pe, act, dve, pool, sp = self.queues
        NBLK, D, E, DT, L = self.NBLK, self.D, self.E, self.DT, self.L
        ring = self.route_banks
        pr, yT, gateT = t["pr"], t["yT"], t["gateT"]
        bufs, norms = [], []
        for i, b in enumerate(pair):
            xy = t["xy"].next()
            rows = slice(b * L, (b + 1) * L)
            s = sp.dma(lambda e, xy=xy, rows=rows: e.dma_start(
                xy.ap[:], res_dram[rows, :].rearrange("(n p) d -> p n d", p=P)), sems["fx"][i],
                xy.take(), self.stored.get(b))
            bufs.append((xy, s))
        for i, (b, (xy, s)) in enumerate(zip(pair, bufs)):
            if i == 0:
                for _ in range(6):
                    yield
            norm = []
            yield from self.layer_norm_pieces(xy.ap, xy.ap, t["stats"][i], t["mv"][i], t["rstd"][i], NBLK, norm, s,
                                              self.rstd_user.get(i))
            self.rstd_user[i] = norm[-2:]
            norms.append(norm)
            s = sp.dma(lambda e, xy=xy, b=b: e.dma_start(ysc[b].rearrange("(n p) d -> p n d", p=P), xy.ap[:]),
                       sems["y"][b], norm[-2:])
            xy.used_by(s)
            self.y_written[b] = s
            yield
        score = ring.next()
        gates = []
        pe.wait(score.take())
        sc = score.ap[:, 0:2 * NBLK * E].rearrange("p (b n e) -> p b n e", b=2, e=E)
        tring = Ring([x for x in ring.buffers if x is not score])
        for i, (xy, _) in enumerate(bufs):
            act.wait(yT.take())
            evs = []
            for c in range(2):
                for dt in range(DT):
                    bank = tring.next()
                    pe.wait(bank.take())
                    for n in range(4 * c, 4 * c + 4):
                        m = pe.do(lambda e, n=n, bank=bank, dt=dt, xy=xy: e.transpose(
                            bank.ap[:, (n % 4) * P:(n % 4 + 1) * P], xy.ap[:, n, dt * P:(dt + 1) * P],
                            self.ident[:]), norms[i][n])
                    ev = act.do(lambda e, c=c, bank=bank, dt=dt: e.copy(
                        yT.ap[:, dt, c * BANK:(c + 1) * BANK], bank.ap), m)
                    bank.used_by(ev)
                    evs.append(ev)
                    yield
            xy.used_by(m)
            pe.wait(evs)
            for n in range(NBLK):
                for dt in range(DT):
                    m = pe.do(lambda e, n=n, dt=dt, i=i: e.matmul(
                        sc[:, i, n, :], yT.ap[:, dt, n * P:(n + 1) * P], gateT[:, dt, :],
                        start=(dt == 0), stop=(dt == DT - 1)))
            yT.used_by(m)
            gates.append(m)
            yield
        v16 = lambda a: a.rearrange("p b n e -> p (b n) e")
        s = dve.do(lambda e: e.tensor_reduce(t["mx"][:].rearrange("p b n -> p (b n)"), v16(sc), AX.X, ALU.max), gates)
        s = dve.do(lambda e: e.tensor_tensor(v16(t["scd"][:]), v16(sc),
                                             spread(t["mx"][:].rearrange("p b n -> p (b n)"), 2, E), ALU.subtract), s)
        score.used_by(s)
        s = act.do(lambda e: e.activation(t["ex"][:], t["scd"][:], ACT.Exp), s)
        yield
        sm = t["sm"][:].rearrange("p b n -> p (b n)")
        s = dve.do(lambda e: e.tensor_reduce(sm, v16(t["ex"][:]), AX.X, ALU.add), s)
        s = dve.do(lambda e: e.reciprocal(sm, sm), s)
        s = dve.do(lambda e: e.tensor_tensor(v16(pr[:]), v16(t["ex"][:]), spread(sm, 2, E), ALU.mult), s)
        w = [dve.do(lambda e, i=i: e.tensor_copy(t["wide"][:, :, i], spread(pr[:, i], 3, self.NCAND)), s,
                    self.onehot_user)
             for i in range(2)]
        yield
        yield
        evs = []
        for c in range(2):
            bank = ring.next()
            pe.wait(bank.take(), w)
            for n in range(4 * c, 4 * c + 4):
                m = pe.do(lambda e, n=n, bank=bank: e.transpose(
                    bank.ap[:, (n % 4) * P:(n % 4 + 1) * P],
                    t["wide"][:, n].rearrange("p b e j -> p (b e j)"), self.ident[:]))
            ev = act.do(lambda e, c=c, bank=bank: e.copy(t["pT"][:, c * BANK:(c + 1) * BANK], bank.ap), m)
            bank.used_by(ev)
            evs.append(ev)
            yield
        prefix, thr, s = self.zero_i, self.digit[:, 0:1], evs
        for n, shift in enumerate(self.SHIFTS):
            s = dve.do(lambda e, thr=thr: e.tensor_scalar(
                t["junk"][:], t["pT"][:], thr.bitcast(F32), 0.0, ALU.is_ge, ALU.add, accum_out=t["cnt"][:]), s)
            s = dve.do(lambda e: e.tensor_scalar(t["ind"][:], t["cnt"][:], self.CAP - 0.5, None, ALU.is_ge), s)
            yield
            yield
            bank = ring.next()
            m = pe.do(lambda e, bank=bank: e.matmul(bank.ap[:, 0:1], self.same_b[:], t["ind"][:],
                                                    start=True, stop=True), s, bank.take())
            yield
            s = dve.do(lambda e, bank=bank, a=float(1 << shift): e.tensor_scalar(
                t["bits"][:], bank.ap[:, 0:1], a, -a, ALU.mult, ALU.add), m, s)
            bank.used_by(s)
            s = dve.do(lambda e, p=prefix: e.tensor_tensor(t["prefix"][:], p[:], t["bits"][:], ALU.bitwise_or), s)
            prefix = t["prefix"]
            if n + 1 < len(self.SHIFTS):
                s = dve.do(lambda e, n=n: e.tensor_tensor(t["thr"][:], prefix[:], self.digit[:, n + 1:n + 2],
                                                          ALU.bitwise_or), s)
                thr = t["thr"][:, 0:1]
        s = dve.do(lambda e: e.tensor_copy(t["Tfull"][:], prefix[:].bitcast(F32).to_broadcast([P, P])), s)
        yield
        bank = ring.next()
        m = pe.do(lambda e, bank=bank: e.transpose(bank.ap[:, 0:P], t["Tfull"][:], self.ident[:]), s, bank.take())
        yield
        s = dve.do(lambda e, bank=bank: e.tensor_copy(
            t["Tb"][:], bank.ap[:, 0:P].rearrange("p (b e j) -> p b e j", b=2, e=E)[:, :, :, 0]), m)
        bank.used_by(s)
        cmp = []
        for i in range(2):
            Tb = spread(t["Tb"][:, i], 1, NBLK)
            cmp.append(dve.do(lambda e, i=i, Tb=Tb: e.tensor_tensor(t["ge"][:, 0, i], pr[:, i], Tb, ALU.is_gt), s))
            cmp.append(dve.do(lambda e, i=i, Tb=Tb: e.tensor_tensor(t["ge"][:, 1, i], pr[:, i], Tb, ALU.is_equal)))
        yield
        cb, tb_ = ring.next(), ring.next()
        NV = 4 * NBLK * E
        cu = cb.ap[:, 0:NV].rearrange("p (g n e) -> p g n e", g=4, e=E)
        ge = t["ge"][:].rearrange("p g b n e -> p (g b) n e")
        tot = tb_.ap[:, 0:2 * E].rearrange("p (b e) -> p b e", e=E)
        pe.wait(cb.take(), tb_.take(), cmp)
        pe.do(lambda e: e.matmul(cb.ap[:, 0:NV], self.upto_b[:], t["ge"][:].rearrange("p g b n e -> p (g b n e)"),
                                 start=True, stop=False, skip_group_check=True))
        for n in range(NBLK - 1):
            pe.do(lambda e, n=n: e.matmul(
                cu[:, :, n + 1:, :], self.ones_b[:], spread(ge[:, :, n, :], 2, NBLK - 1 - n),
                start=False, stop=(n == NBLK - 2), skip_group_check=True))
        for n in range(NBLK):
            m = pe.do(lambda e, n=n: e.matmul(tot, self.ones_b[:], t["ge"][:, 0, :, n, :],
                                              start=(n == 0), stop=(n == NBLK - 1)))
        yield
        cg = cb.ap[:, 0:NV].rearrange("p (g b n e) -> p g b n e", g=2, b=2, e=E)
        s = dve.do(lambda e: e.tensor_scalar(t["need"][:], tot, -1.0, float(self.CAP), ALU.mult, ALU.add), m)
        tb_.used_by(s)
        need = spread(t["need"][:], 2, NBLK)
        s = dve.do(lambda e: e.tensor_tensor(t["m1"][:], cg[:, 1], need, ALU.is_le), s)
        s2 = dve.do(lambda e: e.tensor_tensor(t["pos"][:], cg[:, 1], need, ALU.min), s)
        s = dve.do(lambda e: e.tensor_tensor(t["sel"][:], t["m1"][:], t["ge"][:, 1], ALU.mult), s)
        s2 = dve.do(lambda e: e.tensor_tensor(t["pos"][:], cg[:, 0], t["pos"][:], ALU.add), s2)
        cb.used_by(s2)
        s = dve.do(lambda e: e.tensor_tensor(t["sel"][:], t["sel"][:], t["ge"][:, 0], ALU.add), s)
        s = dve.do(lambda e: e.tensor_tensor(t["pos"][:], t["pos"][:], t["sel"][:], ALU.mult), s, s2)
        s = dve.do(lambda e: e.tensor_scalar(t["key"][:], t["pos"][:], -1.0, None, ALU.add), s)
        s1 = dve.do(lambda e: e.tensor_scalar(t["hi4"][:], t["key"][:], 4, None, ALU.arith_shift_right), s)
        s = dve.do(lambda e: e.tensor_scalar(t["lo4"][:], t["key"][:], 15, None, ALU.bitwise_and))
        digits = [s1, s]
        yield
        i16 = spread(spread(self.iota16[:], 1, E), 1, NBLK)
        A, C = t["A"], t["C"]
        for i, b in enumerate(pair):
            C_users = C.take()
            dve.wait(A.take(), C_users)
            sa = dve.do(lambda e, i=i: e.tensor_tensor(A.ap[:], spread(t["hi4"][:, i], 3, 16), i16, ALU.is_equal),
                        digits)
            onehot = (t["pT"][:].rearrange("p (n e k) -> p n e k", n=NBLK, k=16) if i == 0 else
                      t["wide"][:].rearrange("p n b e j -> p (n b e j)").rearrange(
                          "p (n e k) -> p n e k", n=NBLK, k=16))
            s = dve.do(lambda e, i=i, onehot=onehot: e.tensor_tensor(onehot, spread(t["lo4"][:, i], 3, 16), i16,
                                                                     ALU.is_equal))
            s2 = pool.do(lambda e, i=i, onehot=onehot: e.tensor_tensor(
                C.ap[:, :, :, :, 1], onehot, spread(pr[:, i], 3, 16), ALU.mult), s, C_users)
            self.onehot_user = s2
            yield
            s = dve.do(lambda e, onehot=onehot: e.tensor_tensor(
                C.ap[:, :, :, :, 0], onehot, spread(spread(self.tokid[:], 2, E), 3, 16), ALU.mult), s)
            yield
            yield
            bank = ring.next()
            pe.wait(bank.take(), s, sa, s2)
            for n in range(NBLK):
                m = pe.do(lambda e, n=n, bank=bank: e.matmul(
                    bank.ap[:, 0:E * 32], A.ap[:, n].rearrange("p e a -> p (e a)"),
                    C.ap[:, n].rearrange("p e c t -> p (e c t)"), start=(n == 0), stop=(n == NBLK - 1)))
            A.used_by(m)
            C.used_by(m)
            yield
            R = t["R"][i]
            s = dve.do(lambda e, bank=bank: e.tensor_tensor(
                t["Rw"][:], bank.ap[:, 0:E * 32].rearrange("p (e k) -> p e k", e=E),
                spread(self.same_f[:], 2, 32), ALU.mult), m, self.rw_user)
            bank.used_by(s)
            s = self.rw_user = dve.do(lambda e, R=R: e.tensor_reduce(
                R.ap[:], t["Rw"][:].rearrange("p e k -> p k e"), AX.X, ALU.add), s, R.take())
            s = sp.dma(lambda e, R=R, b=b: e.dma_start(tabs[b].rearrange("e (a k) -> (e a) k", a=16), R.ap[:]),
                       sems["tab"][i], s)
            R.used_by(s)
            tab = t["tab"][b]
            s = sp.dma(lambda e, tab=tab, b=b: e.dma_start(
                tab[:].rearrange("p e h t -> p e (h t)"), tabs[b].rearrange("e (q k) -> q e k", k=4)),
                sems["tab"][i], s)
            yield
            dve.do(lambda e, tab=tab, b=b: e.tensor_copy(t["idx"][b][:], tab[:, :, :, 0]), s)
            s = dve.do(lambda e, tab=tab, b=b: e.tensor_scalar(t["row"][b][:], tab[:, :, :, 0], float(b * L), None,
                                                               ALU.add))
            self.idx_ready[b] = s
        yield

    def load_expert(self, e_, t, w1, w2, sems):
        pe, act, dve, pool, sp = self.queues
        D, Fh, DT, FT = self.D, self.F, self.DT, self.FT
        n = self.loaded
        self.loaded += 1
        stg = t["wst"]
        users = stg.take()
        a = sp.dma(lambda e: e.dma_start(stg.ap[:, 0].rearrange("p (k f) -> p k f", k=DT),
                                         w1[e_].rearrange("(k p) f -> p k f", p=P)), sems["w1"], users)
        c = sp.dma(lambda e: e.dma_start(stg.ap[:, 1].rearrange("p (k d) -> p k d", k=FT),
                                         w2[e_].rearrange("(k p) d -> p k d", p=P)), sems["w2"], users)
        yield
        hi, lo = t["whi"][n % 2], t["wlo"][n % 2]
        act.wait(hi.take())
        users = lo.take()
        pool.wait(users)
        dve.wait(users)
        steps = []
        for i, ready in ((0, a), (1, c)):
            for h in range(2):
                k = slice(h * DT * Fh // 2, (h + 1) * DT * Fh // 2)
                s = act.do(lambda e, i=i, k=k: e.copy(hi.ap[:, i, k], stg.ap[:, i, k]), ready)
                s = (pool if h else dve).do(lambda e, i=i, k=k: e.tensor_tensor(lo.ap[:, i, k], stg.ap[:, i, k],
                                                                hi.ap[:, i, k].bitcast(F32), ALU.subtract), s)
                stg.used_by(s)
                steps.append(s)
                yield
        self.weights[n] = (hi, lo, steps)

    def experts(self, pairs, routed, t, w1, w2, ysc, res_dram, sems):
        pe, act, dve, pool, sp = self.queues
        D, DT, FT, E = self.D, self.DT, self.FT, self.E
        x0, x1 = self.banks[0], self.banks[1]
        up = Ring(self.banks[2:4])
        down = self.banks[4:6]

        def gather(pair, e_):
            routed(pair)
            tiles = []
            for b in pair:
                for h in range(2):
                    g = t["xg"].next()
                    s = pool.dma(lambda e, g=g, b=b, h=h: e.indirect_dma_start(
                        out=g.ap[:], out_offset=None, in_=ysc[b],
                        in_offset=bass.IndirectOffsetOnAxis(ap=t["idx"][b][:, e_, h:h + 1], axis=0)),
                        sems["xg"][(t["xg"].n - 1) % 8], g.take(), self.idx_ready[b], self.y_written[b])
                    tiles.append((g, s))
            return tiles

        def xin(tiles):
            buf = t["xin"]
            hi, lo = buf.ap
            pe.wait(x0.take(), x1.take())
            for k, (g, s) in enumerate(tiles):
                pe.wait(s)
                for dt, bank in enumerate((x0, x1)):
                    m = pe.do(lambda e, k=k, g=g, dt=dt, bank=bank: e.transpose(
                        bank.ap[:, k * P:(k + 1) * P], g.ap[:, dt * P:(dt + 1) * P], self.ident[:]))
                g.used_by(m)
            out = []
            users = buf.take()
            act.wait(users)
            dve.wait(users)
            for dt, bank in enumerate((x0, x1)):
                a = act.do(lambda e, dt=dt, bank=bank: e.copy(hi[:, dt, :], bank.ap), m)
                c = dve.do(lambda e, dt=dt, bank=bank: e.tensor_tensor(lo[:, dt, :], bank.ap,
                                                                       hi[:, dt, :].bitcast(F32), ALU.subtract), a)
                bank.used_by(c)
                out.append(c)
            return buf, hi, lo, out

        work = [(pair, e_) for pair in pairs for e_ in range(E)]
        first = gather(*work[0])
        while 0 not in self.weights:
            next(self.weights_ahead)
        buf, xhi, xlo, xready = xin(first)
        yield
        for n, (pair, e_) in enumerate(work):
            tiles = gather(*work[n + 1]) if n + 1 < len(work) else None
            while self.used not in self.weights:
                next(self.weights_ahead)
            whi, wlo, wready = self.weights[self.used]
            self.used += 1
            pe.wait(xready, wready)
            w1h = whi.ap[:, 0].rearrange("p (k f) -> p k f", k=DT)
            w1l = wlo.ap[:, 0].rearrange("p (k f) -> p k f", k=DT)
            w2h = whi.ap[:, 1].rearrange("p (k d) -> p k d", k=FT)
            w2l = wlo.ap[:, 1].rearrange("p (k d) -> p k d", k=FT)
            hready = []
            for f in range(FT):
                bank = up.next()
                pe.wait(bank.take())
                fs = slice(f * P, (f + 1) * P)
                terms = [(w, x, dt) for dt in range(DT) for w, x in ((w1h, xhi), (w1h, xlo), (w1l, xhi))]
                for k, (w, x, dt) in enumerate(terms):
                    m = pe.do(lambda e, w=w, x=x, dt=dt, fs=fs, bank=bank, k=k: e.matmul(
                        bank.ap, w[:, dt, fs], x[:, dt, :], start=(k == 0), stop=(k == len(terms) - 1)))
                hb, parts = t["h"].next(), t["hs"][f]
                hhi, hlo = parts.ap
                a = act.do(lambda e, hb=hb, bank=bank: e.activation(hb.ap[:], bank.ap, ACT.Gelu), m, hb.take())
                bank.used_by(a)
                c = dve.do(lambda e, hb=hb, hhi=hhi: e.tensor_copy(hhi[:], hb.ap[:]), a, parts.take())
                c = dve.do(lambda e, hb=hb, hhi=hhi, hlo=hlo: e.tensor_tensor(
                    hlo[:], hb.ap[:], hhi[:].bitcast(F32), ALU.subtract), c)
                hb.used_by(c)
                hready.append(c)
                yield
            buf.used_by(m)
            if tiles:
                buf, xhi, xlo, xready = xin(tiles)
            for bank in down:
                pe.wait(bank.take())
            for f in range(FT):
                pe.wait(hready[f])
                hhi, hlo = t["hs"][f].ap
                for k in range(4):
                    bank = down[k // 2]
                    ks = slice(k * P, (k + 1) * P)
                    out = bank.ap[:, (k % 2) * D:(k % 2 + 1) * D]
                    for j, (h, w) in enumerate(((hhi, w2h), (hhi, w2l), (hlo, w2h))):
                        m = pe.do(lambda e, h=h, w=w, ks=ks, out=out, f=f, j=j, k=k: e.matmul(
                            out, h[:, ks], w[:, f, :], start=(f == 0 and j == 0 and k % 2 == 0),
                            stop=(f == FT - 1 and j == 2), skip_group_check=True))
                t["hs"][f].used_by(m)
                if f % 2:
                    yield
            whi.used_by(m)
            wlo.used_by(m)
            self.through += 1
            for k in range(4):
                b, h = pair[k // 2], k % 2
                bank = down[k // 2]
                yo = t["yo"].next()
                s = act.do(lambda e, yo=yo, bank=bank, h=h, b=b, e_=e_: e.mul(
                    yo.ap[:], bank.ap[:, h * D:(h + 1) * D], t["tab"][b][:, e_, h, 1:2]), m, yo.take())
                bank.used_by(s)
                s = pool.dma(lambda e, yo=yo, b=b, h=h, e_=e_: e.indirect_dma_start(
                    out=res_dram[:, :], out_offset=bass.IndirectOffsetOnAxis(ap=t["row"][b][:, e_, h:h + 1], axis=0),
                    in_=yo.ap[:], in_offset=None, compute_op=ALU.add),
                    sems["add"][b][h], s, self.added[b])
                yo.used_by(s)
                self.adding[b].append(s)
                if h == 1:
                    self.added[b], self.adding[b] = self.adding[b], []
            yield

    def stage_f(self, res_dram, gate_w, w1, w2, ysc, tabs, sems, before=None):
        pe, act, dve, pool, sp = self.queues
        with ExitStack() as st:
            t = self.route_tiles(st)
            self.route_banks = Ring(self.banks[6:8])
            self.y_written, self.idx_ready, self.stored = {}, {}, {}
            self.added = {b: [] for b in range(self.B)}
            self.adding = {b: [] for b in range(self.B)}
            self.rstd_user, self.rw_user, self.onehot_user = {}, None, None
            self.loaded = self.used = self.through = 0
            self.weights = {}
            s = sp.dma(lambda e: e.dma_start(t["gate"][:], gate_w), sems["gate"])
            bank = self.route_banks.next()
            pe.wait(bank.take(), s)
            for dt in range(self.DT):
                m = pe.do(lambda e, dt=dt: e.transpose(
                    bank.ap[:, dt * self.E:(dt + 1) * self.E], t["gate"][:, dt * P:(dt + 1) * P],
                    self.ident[0:self.E, 0:self.E]))
            s = dve.do(lambda e: e.tensor_copy(t["gateT"][:], bank.ap[:, 0:self.DT * self.E].rearrange(
                "p (k e) -> p k e", e=self.E)), m)
            bank.used_by(s)
            pe.wait(s)
            pairs = [(2 * k, 2 * k + 1) for k in range(self.B // 2)]
            route = lambda pair: self.route(pair, t, res_dram, ysc, tabs, sems)
            first = route(pairs[0])
            order = [e_ for _ in pairs for e_ in range(self.E)]

            def load_ahead():
                for k, e_ in enumerate(order):
                    while self.through < k - 1:
                        yield
                    yield from self.load_expert(e_, t, w1, w2, sems)
            if before is not None:
                self.rows_free = t["xy"]
                self.weights_ahead = load_ahead()
                for n, _ in enumerate(before):
                    self.pump(first)
                    if n % 3 == 0:
                        self.pump(first)
                    if n == 8:
                        self.pump(self.weights_ahead)
            self.expert_tiles(st, t)
            if before is None:
                self.weights_ahead = load_ahead()
            for n, _ in enumerate(first):
                if n % 3 == 0 and 0 not in self.weights:
                    self.pump(self.weights_ahead)
            later = route(pairs[1])

            def routed(pair):
                if pair == pairs[1]:
                    for _ in later:
                        pass
            for _ in self.experts(pairs, routed, t, w1, w2, ysc, res_dram, sems):
                self.pump(self.weights_ahead)
                self.pump(later)
            self.barrier()

    @staticmethod
    def pump(gen):
        try:
            next(gen)
        except StopIteration:
            pass

    def transpose_weights(self, st, spare, weights, scratch, sems):
        pe, act, dve, pool, sp = self.queues
        NT = self.H * self.DH // P
        natural = self.rows_free or Ring([Buffer(self.sbuf(st, "w_nat", [P, NT, self.D])) for _ in range(2)])
        parts = Ring([Buffer(a.bitcast(F32R).rearrange("p n (t c j) -> p n t c j", t=2, c=self.DT)) for a in spare])
        ring = Ring(self.banks[6:8])

        def load(i):
            nat = natural.next()
            return nat, sp.dma(lambda e: e.dma_start(nat.ap[:], weights[i].rearrange("h d c -> (h d) c").rearrange(
                "(n p) c -> p n c", p=P)), sems["nat"][i], nat.take())
        loads = [load(0), load(1)]
        for i, (w, out) in enumerate(zip(weights, scratch)):
            yield
            prt = parts.next()
            nat, s = loads[i]
            act.wait(prt.take())
            for ct in range(self.DT):
                for c in range(NT // 4):
                    bank = ring.next()
                    pe.wait(bank.take(), s)
                    for n in range(4 * c, 4 * c + 4):
                        m = pe.do(lambda e, n=n, ct=ct, bank=bank, nat=nat: e.transpose(
                            bank.ap[:, (n % 4) * P:(n % 4 + 1) * P], nat.ap[:, n, ct * P:(ct + 1) * P], self.ident[:]))
                    v = bank.ap.rearrange("p (n j) -> p n j", j=P)
                    ns = slice(4 * c, 4 * c + 4)
                    a = act.do(lambda e, v=v, ns=ns, ct=ct, prt=prt: e.copy(prt.ap[:, ns, 0, ct, :], v), m)
                    d = dve.do(lambda e, v=v, ns=ns, ct=ct, prt=prt: e.tensor_tensor(
                        prt.ap[:, ns, 1, ct, :], v, prt.ap[:, ns, 0, ct, :].bitcast(F32), ALU.subtract), a)
                    bank.used_by(d)
                yield
            nat.used_by(m)
            if i + 2 < len(weights):
                loads.append(load(i + 2))
            s = sp.dma(lambda e, prt=prt, out=out: e.dma_start(
                out.rearrange("n p k -> p n k"), prt.ap.rearrange("p n t c j -> p n (t c j)").bitcast(F32)),
                sems["wT"][i], d)
            prt.used_by(s)
        self.weights_moved = [u for b in parts.buffers for u in b.users]

    def stage_t(self, x_dram, out_dram, w_o, scratch, sems):
        pe, act, dve, pool, sp = self.queues
        B, L, D, NBLK, DT, DH = self.B, self.L, self.D, self.NBLK, self.DT, self.DH
        NHP = self.H // 2
        NC = L // BANK
        KPC = BANK // P
        QROWS = DH + NBLK
        scale = 1.0 / float(np.sqrt(DH))
        with ExitStack() as st:
            sb = lambda n, s, d=F32: self.sbuf(st, n, s, d)
            xy = Buffer(sb("t_xy", [P, NBLK, D]))
            xres_r = Ring([Buffer(sb("t_xres", [P, KPC, D])) for _ in range(2)])
            xT = Buffer((sb("t_xThi", [P, DT, L], F32R), sb("t_xTlo", [P, DT, L], F32R)))
            stats, mv, rstd = sb("t_stats", [P, NBLK, 6]), sb("t_mv", [P, NBLK, 2]), sb("t_rstd", [P, 2 * NBLK])
            wo = sb("t_wo", [P, NHP, D])
            wq_r = Ring([Buffer(sb("t_wq", [P, 2, DT, P], F32R)) for _ in range(2)])
            wk_r = Ring([Buffer(sb("t_wk", [P, 2, DT, P], F32R)) for _ in range(2)])
            wv_r = Ring([Buffer(sb("t_wv", [P, 2, 2, DT, P], F32R)) for _ in range(2)])
            qk_weights = {}
            v_r = Ring([Buffer(sb("t_v", [P, NBLK, 4 * DH])) for _ in range(2)])
            heads = [[Buffer({k: sb("t_" + k, [P, L], F32R) for k in ("qa", "qb", "ka", "kb")}) for _ in range(2)]
                     for _ in range(2)]
            p_r = Ring([Buffer(sb("t_p", [P, 2, BANK])) for _ in range(3)])
            acc_r = Ring([Buffer(sb("t_acc", [P, 2, BANK])) for _ in range(2)])
            yT = [Buffer(sb("t_yT", [P, NHP, BANK])) for _ in range(NC)]
            pvs_r = Ring([Buffer(sb("t_pvs", [P, BANK])) for _ in range(2)])
            den_b = Buffer(sb("t_den", [P, BANK]))
            rden_r = Ring([Buffer(sb("t_rden", [P, BANK // 32])) for _ in range(2)])
            mask = sb("t_mask", [P, BANK])
            pick = sb("t_pick", [NBLK, NBLK, P])
            junk_r = Ring([Buffer(sb("t_junk", [P, BANK], BF16)) for _ in range(2)])
            mcol_r = Ring([Buffer(sb("t_mcol", [P, 2, NBLK])) for _ in range(2)])
            work = Ring([self.banks[0], self.banks[1], self.banks[7]])
            psum2 = lambda k: Buffer(self.psum_all[:, k * BANK:(k + 2) * BANK].rearrange("p (i q) -> p i q", i=2))
            st_banks = Ring([psum2(2), psum2(4)])
            pv_bank = self.banks[6]

            s = pool.do(lambda e: e.memset(mask[:], 0.0))
            s2 = pool.do(lambda e: e.memset(pick[:], 0.0))
            pool.do(lambda e: e.affine_select(out=mask[:], in_=mask[:], compare_op=ALU.is_ge, fill=NEG,
                                              base=BANK - P, pattern=[[-1, BANK]], channel_multiplier=1), s, s2)
            consts = pool.do(lambda e: e.affine_select(out=pick[:], in_=pick[:], compare_op=ALU.not_equal, fill=-1.0,
                                                       base=0, pattern=[[-1, NBLK], [0, P]], channel_multiplier=1))
            for pair in heads:
                for hd in pair:
                    consts = dve.do(lambda e, hd=hd: e.tensor_copy(
                        hd.ap["kb"][DH:QROWS, :].rearrange("p (a b) -> p a b", b=P),
                        spread(self.ones[DH:QROWS, :], 1, NBLK)), consts)
            wo_ready = sp.dma(lambda e: e.dma_start(wo[:], w_o.rearrange("(n p) d -> p n d", p=P)), sems["w1"])
            pe.wait(consts)

            state = dict(tick=0, rstd_user=None)
            normed, xT_ready = {}, {}
            due = []
            v_of, qk_ready, late_ready, max_ready = {}, {}, {}, {}
            extra = []

            def at(delay, function):
                due.append((state["tick"] + delay, function))

            def tick():
                now = [f for t, f in due if t <= state["tick"]]
                due[:] = [(t, f) for t, f in due if t > state["tick"]]
                for f in now:
                    f()
                state["tick"] += 1

            def normalize(b):
                rows = slice(b * L, (b + 1) * L)
                s = sp.dma(lambda e: e.dma_start(xy.ap[:], x_dram[rows, :].rearrange("(n p) d -> p n d", p=P)),
                           sems["x"], xy.take())
                norm = []
                yield from self.layer_norm_pieces(xy.ap, xy.ap, stats, mv, rstd, NBLK, norm, s, state["rstd_user"])
                state["rstd_user"] = norm[-2:]
                normed[b] = norm

            def prepare(b):
                for _ in normalizing[b]:
                    pass
                hi, lo = xT.ap
                users = xT.take()
                act.wait(users)
                dve.wait(users)
                ready = []
                for c in range(NC):
                    for dt in range(DT):
                        bank = work.next()
                        pe.wait(bank.take())
                        for n in range(4 * c, 4 * c + 4):
                            m = pe.do(lambda e, n=n, dt=dt, bank=bank: e.transpose(
                                bank.ap[:, (n % 4) * P:(n % 4 + 1) * P], xy.ap[:, n, dt * P:(dt + 1) * P],
                                self.ident[:]), normed[b][n])
                        cs = slice(c * BANK, (c + 1) * BANK)
                        a = act.do(lambda e, dt=dt, cs=cs, bank=bank: e.copy(hi[:, dt, cs], bank.ap), m)
                        d = dve.do(lambda e, dt=dt, cs=cs, bank=bank: e.tensor_tensor(
                            lo[:, dt, cs], bank.ap, hi[:, dt, cs].bitcast(F32), ALU.subtract), a)
                        bank.used_by(d)
                        yield
                    ready.append(d)
                xy.used_by(m)
                xT_ready[b] = ready

            def project_values(b):
                xhi, xlo = xT.ap
                coming_v = load_v(0)
                for g in range(NHP // 2):
                    v = v_r.next()
                    v_of[b, g] = v
                    wv, s = coming_v
                    if g + 1 < NHP // 2:
                        coming_v = load_v(g + 1)
                    act.wait(v.take())
                    pe.wait(s)
                    for n in range(0, NBLK, 2):
                        bank = work.next()
                        pe.wait(bank.take())
                        for i in range(2):
                            ns = slice((n + i) * P, (n + i + 1) * P)
                            for k, (pw, px, ct) in enumerate(((0, xhi, 0), (1, xhi, 0), (0, xlo, 0),
                                                              (0, xhi, 1), (1, xhi, 1), (0, xlo, 1))):
                                m = pe.do(lambda e, pw=pw, px=px, ct=ct, k=k, ns=ns, i=i, bank=bank, wv=wv: e.matmul(
                                    bank.ap[:, i * 4 * DH:(i + 1) * 4 * DH], px[:, ct, ns], wv.ap[:, :, pw, ct, :],
                                    start=(k == 0), stop=(k == 5)))
                        a = act.do(lambda e, n=n, bank=bank, v=v: e.copy(
                            v.ap[:, n:n + 2, :], bank.ap.rearrange("p (i d) -> p i d", i=2)), m)
                        bank.used_by(a)
                        if n == NBLK - 2:
                            wv.used_by(m)
                        yield a

            def load_qk(b, hp):
                wk, wq = wk_r.next(), wq_r.next()
                qk_weights[b, hp] = [wk, wq] + [sp.dma(lambda e, w=w, d=d: e.dma_start(
                    w.ap[:].rearrange("p t c j -> p (t c j)").bitcast(F32), d[hp]),
                    sems["wqk"][hp % 2][i], w.take()) for i, (w, d) in enumerate(((wk, scratch[1]), (wq, scratch[0])))]

            def load_v(g):
                wv = wv_r.next()
                return wv, sp.dma(lambda e: e.dma_start(
                    wv.ap[:].rearrange("p n t c j -> p n (t c j)").bitcast(F32),
                    scratch[2][2 * g:2 * g + 2].rearrange("n p k -> p n k")), sems["wv"][g % 2], wv.take())

            def value_pieces(hp):
                return 4 if hp == 0 else 2 if hp < NHP - 1 else 0

            def project(b, hp):
                nonlocal values
                if hp == 0:
                    yield from prepare(b)
                    values = project_values(b)
                if hp == NHP - 2 and b + 1 < B:
                    normalizing[b + 1] = normalize(b + 1)
                    extra.append(normalizing[b + 1])
                xhi, xlo = xT.ap
                half = hp % 2
                pair = heads[half]
                if (b, hp) == units[0]:
                    load_qk(b, hp)
                if (b, hp) != units[-1]:
                    load_qk(*units[units.index((b, hp)) + 1])
                wk, wq, *loads = qk_weights[b, hp]
                for hd in pair:
                    users = hd.take()
                    act.wait(users)
                    dve.wait(users)
                    sp.wait(users)
                terms = [(0, xhi, 0), (1, xhi, 0), (0, xlo, 0), (0, xhi, 1), (1, xhi, 1), (0, xlo, 1)]
                out, late = [], []
                finish = None
                for is_q, w in enumerate((wk, wq)):
                    pe.wait(loads[is_q])
                    copies = []
                    for c in range(NC):
                        cs = slice(c * BANK, (c + 1) * BANK)
                        bank = work.next()
                        pe.wait(bank.take(), xT_ready[b][c])
                        for k, (pw, px, ct) in enumerate(terms):
                            m = pe.do(lambda e, w=w, pw=pw, px=px, ct=ct, k=k, cs=cs, bank=bank: e.matmul(
                                bank.ap, w.ap[:, pw, ct, :], px[:, ct, cs],
                                start=(k == 0), stop=(k == len(terms) - 1)))
                        hs = []
                        for i, hd in enumerate(pair):
                            src = bank.ap[i * DH:(i + 1) * DH, :]
                            hi = hd.ap["qa" if is_q else "ka"]
                            hs.append(act.do(lambda e, hi=hi, cs=cs, src=src: e.copy(hi[0:DH, cs], src), m))
                        copies.append(hs)
                        if finish:
                            finish()

                        def finish(is_q=is_q, cs=cs, bank=bank, hs=hs):
                            for i, hd in enumerate(pair):
                                src = bank.ap[i * DH:(i + 1) * DH, :]
                                hi = hd.ap["qa" if is_q else "ka"]
                                lo = hd.ap["qa"][DH:2 * DH, cs] if is_q else hd.ap["kb"][0:DH, cs]
                                d = dve.do(lambda e, lo=lo, hi=hi, cs=cs, src=src: e.tensor_tensor(
                                    lo, src, hi[0:DH, cs].bitcast(F32), ALU.subtract), hs[i])
                                out.append(d)
                            bank.used_by(d)
                        yield
                    w.used_by(m)
                    for i, hd in enumerate(pair):
                        src = hd.ap["qa" if is_q else "ka"][0:DH, :]
                        dup = hd.ap["qb"][0:DH, :] if is_q else hd.ap["ka"][DH:2 * DH, :]
                        (late if is_q else out).append(sp.dma(lambda e, dup=dup, src=src: e.dma_start(dup.bitcast(F32), src.bitcast(F32)),
                                          sems["dup"][half][i][is_q], [h[i] for h in copies]))
                for k in range(value_pieces(hp)):
                    late.append(next(values))
                    if finish:
                        finish()
                        finish = None
                    yield
                if finish:
                    finish()
                if hp == NHP - 1:
                    xT.used_by(pe.last)
                    values.close()
                qk_ready[b, hp], late_ready[b, hp] = out, late

            def maxima(b, hp):
                pe.wait(qk_ready[b, hp])
                out = []
                spread_rows = None
                for i, hd in enumerate(heads[hp % 2]):
                    t = hd.ap
                    mc = mcol_r.next()
                    dve.wait(mc.take())
                    for n in range(NBLK):
                        for c in range(n // KPC + 1):
                            w = min(BANK, (n + 1) * P - c * BANK)
                            bank = work.next()
                            m = pe.do(lambda e, t=t, n=n, c=c, w=w, bank=bank: e.matmul(
                                bank.ap[:, 0:w], t["qa"][:, n * P:(n + 1) * P], t["ka"][:, c * BANK:c * BANK + w],
                                start=True, stop=True), bank.take())
                            if c == n // KPC:
                                junk = junk_r.next()
                                d = dve.do(lambda e, n=n, c=c, w=w, bank=bank, mc=mc, junk=junk:
                                           e.tensor_tensor_reduce(
                                               junk.ap[:, 0:w], bank.ap[:, 0:w], mask[:, BANK - w:BANK], 1.0, NEG,
                                               ALU.add, ALU.max, mc.ap[:, c, n:n + 1]), m, junk.take())
                                junk.used_by(d)
                            else:
                                d = dve.do(lambda e, n=n, c=c, bank=bank, mc=mc: e.tensor_reduce(
                                    mc.ap[:, c, n:n + 1], bank.ap, AX.X, ALU.max), m)
                            bank.used_by(d)
                        if spread_rows and n == 3:
                            spread_rows()
                            spread_rows = None
                        if n != 0 and n != 2:
                            yield
                    d = dve.do(lambda e, mc=mc: e.tensor_tensor(
                        mc.ap[:, 0, KPC:], mc.ap[:, 0, KPC:], mc.ap[:, 1, KPC:], ALU.max), d)

                    def spread_rows(t=t, mc=mc, d=d):
                        bank = work.next()
                        m = pe.do(lambda e: e.transpose(bank.ap[0:NBLK, 0:P], mc.ap[:, 0, :], self.ident[:]),
                                  bank.take(), d)
                        mc.used_by(m)
                        d2 = dve.do(lambda e: e.tensor_tensor(
                            t["qb"][DH:QROWS, :].rearrange("p (a b) -> p a b", b=P),
                            spread(bank.ap[0:NBLK, 0:P], 1, NBLK), pick[:], ALU.mult), m)
                        bank.used_by(d2)
                        out.append(d2)
                yield
                spread_rows()
                max_ready[b, hp] = out + late_ready[b, hp]

            def attend(b, hp):
                pair = heads[hp % 2]
                v = v_of[b, hp // 2]
                vcol = (hp % 2) * 2 * DH
                for c in range(NC):
                    last = KPC * (c + 1) - 1
                    acc = acc_r.next()
                    chunk = dict(sum=None)

                    def weigh(kt, q0, p, s, c=c, last=last, acc=acc, chunk=chunk):
                        if kt == 0:
                            d = s
                            pe.wait(pv_bank.take())
                        else:
                            adder = pool if kt < KPC else dve
                            d = adder.do(lambda e: e.tensor_tensor(acc.ap[:, :, q0:], acc.ap[:, :, q0:],
                                                                   p.ap[:, :, q0:], ALU.add),
                                         s, chunk["sum"], chunk["first_used"])
                        chunk["sum"] = d
                        pe.wait(s)
                        for i in range(2):
                            m = pe.do(lambda e, i=i: e.matmul(
                                pv_bank.ap[i * DH:(i + 1) * DH, q0:BANK],
                                v.ap[:, kt, vcol + i * DH:vcol + (i + 1) * DH], p.ap[:, i, q0:BANK],
                                start=(kt == 0), stop=(kt == last), skip_group_check=True))
                        if kt == 0:
                            chunk["first_used"] = m
                        else:
                            p.used_by(d, m)
                        if kt == last:
                            pvs = pvs_r.next()
                            a = act.do(lambda e: e.copy(pvs.ap[:], pv_bank.ap), m, pvs.take())
                            pv_bank.used_by(a)
                            v.used_by(m)
                            at(1, lambda: divide(c, acc, d, pvs, a))

                    def divide(c, acc, d, pvs, a):
                        bank = work.next()
                        pe.wait(bank.take(), d)
                        for i in range(2):
                            m = pe.do(lambda e, i=i: e.matmul(
                                bank.ap[i * DH:(i + 1) * DH, :], self.ones[:, 0:DH], acc.ap[:, i, :],
                                start=True, stop=True, skip_group_check=True))
                        acc.used_by(m)
                        den, rden = den_b.ap, rden_r.next()
                        d = dve.do(lambda e: e.transpose(den[:], bank.ap), m, den_b.take())
                        bank.used_by(d)
                        d = dve.do(lambda e: e.reciprocal(
                            rden.ap[:, :], den[:].rearrange("p (n j) -> p n j", j=32)[:, :, 0]), d, rden.take())

                        def scale_rows():
                            d1 = dve.do(lambda e: e.transpose(den[:], spread(rden.ap[:], 2, 32)), d)
                            if hp == 0:
                                pool.wait(yT[c].take())
                            rden.used_by(d1)
                            d2 = pool.do(lambda e: e.tensor_tensor(yT[c].ap[:, hp, :], pvs.ap[:], den[:], ALU.mult),
                                         d1, a)
                            den_b.used_by(d2)
                            pvs.used_by(d2)
                            if hp == NHP - 1:
                                extra.append(output(b, c, d2))
                        at(1, scale_rows)

                    for kt in range(last + 1):
                        q0 = max(0, kt * P - c * BANK)
                        bank = st_banks.next()
                        qs = slice(c * BANK + q0, (c + 1) * BANK)
                        ks = slice(kt * P, (kt + 1) * P)
                        pe.wait(bank.take())
                        for i in range(2):
                            t = pair[i].ap
                            pe.do(lambda e, t=t, ks=ks, qs=qs, q0=q0, i=i, bank=bank: e.matmul(
                                bank.ap[:, i, q0:], t["ka"][:, ks], t["qa"][:, qs], start=True, stop=False))
                        if c == 0 and kt == 0:
                            pe.wait(max_ready[b, hp])
                        for i in range(2):
                            t = pair[i].ap
                            m = pe.do(lambda e, t=t, ks=ks, qs=qs, q0=q0, i=i, bank=bank: e.matmul(
                                bank.ap[:, i, q0:], t["kb"][0:QROWS, ks], t["qb"][0:QROWS, qs],
                                start=False, stop=True))
                        p = p_r.next() if kt else acc
                        s = act.do(lambda e, p=p, q0=q0, bank=bank: e.activation(
                            p.ap[:, :, q0:], bank.ap[:, :, q0:], ACT.Exp, scale=scale), m, p.take())
                        bank.used_by(s)
                        if kt >= KPC * c:
                            s = pool.do(lambda e, p=p, q0=q0: e.affine_select(
                                out=p.ap[:, :, q0:q0 + P], in_=p.ap[:, :, q0:q0 + P], compare_op=ALU.is_ge, fill=0.0,
                                base=0, pattern=[[0, 2], [1, P]], channel_multiplier=-1), s)
                        yield
                        tick()
                        at(0, lambda kt=kt, q0=q0, p=p, s=s, weigh=weigh: weigh(kt, q0, p, s))
                        yield
                for hd in pair:
                    hd.used_by(m)

            def output(b, c, y_ready):
                rows = slice(b * L + c * BANK, b * L + (c + 1) * BANK)
                k_ = xres_r.n % 2
                xres = xres_r.next()
                s = sp.dma(lambda e: e.dma_start(xres.ap[:], x_dram[rows, :].rearrange("(n p) d -> p n d", p=P)),
                           sems["xr"][k_], xres.take())
                pe.wait(y_ready, wo_ready)
                for n in range(KPC):
                    bank = work.next()
                    pe.wait(bank.take())
                    for k in range(NHP):
                        m = pe.do(lambda e, n=n, k=k, bank=bank: e.matmul(
                            bank.ap[:, 0:D], yT[c].ap[:, k, n * P:(n + 1) * P], wo[:, k, :],
                            start=(k == 0), stop=(k == NHP - 1)))
                    d = dve.do(lambda e, n=n, bank=bank, xres=xres: e.tensor_tensor(
                        xres.ap[:, n, :], bank.ap[:, 0:D], xres.ap[:, n, :], ALU.add), m, s)
                    bank.used_by(d)
                    if n == KPC - 1:
                        yT[c].used_by(m)
                        s = sp.dma(lambda e: e.dma_start(
                            out_dram[rows, :].rearrange("(n p) d -> p n d", p=P), xres.ap[:]), sems["xo"][k_], d)
                        xres.used_by(s)
                    yield

            units = [(b, hp) for b in range(B) for hp in range(NHP)]
            values = None
            normalizing = {0: normalize(0)}

            def ahead(b, hp):
                yield from project(b, hp)
                yield from maxima(b, hp)
            for _ in ahead(*units[0]):
                pass
            for n, unit in enumerate(units):
                coming = ahead(*units[n + 1]) if n + 1 < len(units) else iter(())
                hp = (unit[1] + 1) % NHP
                pieces = 2 * NC + value_pieces(hp) + 14 + 4 * (hp == 0)
                owed, halves = 0.0, 0
                for _ in attend(*unit):
                    owed += pieces / 20
                    while owed >= 1:
                        self.pump(coming)
                        owed -= 1
                    halves += 1
                    if extra and halves % 2:
                        try:
                            next(extra[0])
                        except StopIteration:
                            extra.pop(0)
                for _ in coming:
                    pass
            while due:
                tick()
            for stream in extra:
                for _ in stream:
                    pass
            self.barrier()


PHASES = "AFTF"


def hybrid_kernel(nc, x, w_q, w_k, w_v, w_o, gate_w, w1, w2, out):
    B, L, D = x.shape
    E, _, Fh = w1.shape
    H = w_q.shape[0]
    rows = B * L
    scratch = lambda name, shape, dtype=F32: nc.dram_tensor(name, shape, dtype, kind="Internal").ap()
    n_f = PHASES.count("F")
    with ExitStack() as ctx:
        pr = Program(nc, ctx, dict(x=x.shape, w1=w1.shape, w_q=w_q.shape))
        sems = {n: pr.dma_sem("loaded_" + n) for n in ("x", "w1", "w2", "gate")}
        sems["wv"] = [pr.dma_sem(f"loaded_wv{i}") for i in range(2)]
        sems["xr"] = [pr.dma_sem(f"loaded_xres{i}") for i in range(2)]
        sems["xo"] = [pr.dma_sem(f"stored_x{i}") for i in range(2)]
        sems["wqk"] = [[pr.dma_sem(f"loaded_w{n}{i}") for n in "kq"] for i in range(2)]
        sems["dup"] = [[[pr.dma_sem(f"doubled_{n}{i}_{h}") for n in "kq"] for h in range(2)] for i in range(2)]
        sems["tab"] = [pr.dma_sem(f"moved_tab{i}") for i in range(2)]
        sems["fx"] = [pr.dma_sem(f"loaded_fx{i}") for i in range(2)]
        sems["y"] = [pr.dma_sem(f"stored_y{b}") for b in range(B)]
        sems["xg"] = [pr.dma_sem(f"gathered{i}") for i in range(8)]
        sems["add"] = [[pr.dma_sem(f"added{b}_{h}") for h in range(2)] for b in range(B)]
        a_x = [pr.dma_sem(f"a_x{b}") for b in range(B)]
        a_out = [pr.dma_sem(f"a_out{i}") for i in range(2)]
        sems["nat"] = [pr.dma_sem(f"loaded_nat{i}") for i in range(3)]
        sems["wT"] = [pr.dma_sem(f"stored_wT{i}") for i in range(3)]
        pr.constants()
        pr.barrier()
        wT = [scratch(n, (H * pr.DH // P, P, 2 * pr.DT * P)) for n in ("wqT", "wkT", "wvT")]
        flat_x, flat_out = x.rearrange("b l d -> (b l) d"), out.rearrange("b l d -> (b l) d")
        res = scratch("res", (rows, D))
        f_round = 0
        if "T" in PHASES:
            with ExitStack() as st:
                pass
        for n, phase in enumerate(PHASES):
            if phase == "A":
                before = pr.stage_a(flat_x, res if "T" in PHASES else flat_out, a_x, a_out,
                                    lambda st, spare: pr.transpose_weights(st, spare, (w_q, w_k, w_v), wT, sems))
                if PHASES[n + 1:n + 2] != "F":
                    for _ in before:
                        pass
            elif phase == "F":
                ysc = [scratch(f"ysc{f_round}_{b}", (L, D)) for b in range(B)]
                tabs = [scratch(f"tab{f_round}_{b}", (E, 512)) for b in range(B)]
                f_round += 1
                pr.stage_f(flat_out if ("T" not in PHASES or "T" in PHASES[:n]) else res, gate_w, w1, w2,
                           ysc, tabs, sems, before if n == 1 else None)
            else:
                pr.stage_t(res, flat_out, w_o, wT, sems)
        for q in pr.queues:
            q.number()
        block = ctx.enter_context(nc.Block())
        block.tensor(lambda e: pr.pe.play(e))
        block.scalar(lambda e: pr.act.play(e))
        block.vector(lambda e: pr.dve.play(e))
        block.gpsimd(lambda e: pr.pool.play(e))
        block.sync(lambda e: pr.sp.play(e))


NAMES = ["L0_attn_a_x", "L0_attn_b_w_q", "L0_attn_b_w_k", "L0_attn_b_w_v", "L0_attn_b_w_o",
         "L0_ffn_gate_w", "L0_ffn_w1", "L0_ffn_w2"]


def kernel(**inputs):
    import concourse.bacc as bacc
    from concourse.bass_utils import run_bass_kernel_spmd as run

    nc = bacc.Bacc("TRN2", target_bir_lowering=False, num_devices=1)
    arrays = {n: np.ascontiguousarray(inputs[n]) for n in NAMES}
    args = [nc.dram_tensor("in_" + n, a.shape, mybir.dt.from_np(a.dtype), kind="ExternalInput").ap()
            for n, a in arrays.items()]
    out = nc.dram_tensor("out", arrays[NAMES[0]].shape, F32, kind="ExternalOutput").ap()
    hybrid_kernel(nc, *args, out)
    r = run(nc, [{"in_" + n: a for n, a in arrays.items()}], core_ids=[0])
    return r.results[0]["out"]
```
